# Optimizing a Trainium2 kernel written in Bass

```python
import numpy as np
import jax
import jax.numpy as jnp

def _softmax(x, axis=-1):
    return jax.nn.softmax(x, axis=axis)

def _gelu(x):
    return jax.nn.gelu(x, approximate=True)

def _silu(x):
    return jax.nn.silu(x)

def _sigmoid(x):
    return jax.nn.sigmoid(x)

def _layernorm(x, axis=-1, eps=1e-05):
    m = jnp.mean(x, axis=axis, keepdims=True)
    v = jnp.var(x, axis=axis, keepdims=True)
    return (x - m) / jnp.sqrt(v + eps)

def _scatter_add(tgt, idx, src, axis=0):
    return tgt.at[idx].add(src)

def _segment_sum(src, seg, n):
    return jax.ops.segment_sum(src, seg, n)
kernel_name = 'mk_pixart_seq_d4_seqx_r4_44c096'

def setup_inputs(seed: int=0):
    np.random.seed(seed)
    _w = jnp.asarray

    def _rec_inputs():
        import jax
        import jax.numpy as jnp
        _rk = jax.random.key(seed)
        x = -0.0002928 + 1 * jax.random.normal(jax.random.fold_in(_rk, 1), (2, 1024, 256), jnp.float32)
        _lenS = 1024 - jax.random.randint(jax.random.fold_in(_rk, 7), (2,), 0, max(1, 1024 // 4) + 1, jnp.int32)
        _lenS2 = 154 - jax.random.randint(jax.random.fold_in(_rk, 8), (2,), 0, max(1, 154 // 4) + 1, jnp.int32)
        cond_1024 = 0.0061147 + 1.02565 * jax.random.normal(jax.random.fold_in(_rk, 11), (2, 256), jnp.float32)
        _ctx_1024P = jax.random.normal(jax.random.fold_in(_rk, 12), (2, 16, 256), jnp.float32)
        _ctx_1024c = jax.random.dirichlet(jax.random.fold_in(_rk, 512), 0.3 * jnp.ones((16,), jnp.float32), (2, 154))
        _ctx_1024t = jnp.einsum('bsk,bkd->bsd', _ctx_1024c, _ctx_1024P)
        _ctx_1024t = _ctx_1024t * jax.lax.rsqrt(jnp.mean(jnp.square(_ctx_1024t)) + 1e-12) * 0.953939
        ctx_1024 = -0.00265004 + 0.998804 * (_ctx_1024t + 0.3 * jax.random.normal(jax.random.fold_in(_rk, 612), (2, 154, 256), jnp.float32))
        _validS = jnp.arange(1024)[None, :] < _lenS[:, None]
        _validS2 = jnp.arange(154)[None, :] < _lenS2[:, None]
        _causal = jnp.tril(jnp.ones((1024, 1024), dtype=bool))
        mask_BxS2_bf0 = jnp.logical_not(jnp.ones((2, 154), dtype=bool))
        return (x, cond_1024, ctx_1024, mask_BxS2_bf0)
    x, cond_1024, ctx_1024, mask_BxS2_bf0 = _rec_inputs()

    def _L0_xcond_setup():
        import jax, jax.numpy as jnp
        import numpy as np
        D, H, B, N, S = (256, 16, 4, 256, 77)
        HD = D // H
        DF = 4 * D
        EPS = 1e-06
        SCALE = HD ** (-0.5)

        def _ln(x):
            m = jnp.mean(x, axis=-1, keepdims=True)
            v = jnp.mean((x - m) ** 2, axis=-1, keepdims=True)
            return (x - m) / jnp.sqrt(v + EPS)
        key = jax.random.key(seed)
        ks = jax.random.split(key, 24)
        s = 0.02
        inp = {'x': jax.random.normal(ks[0], (B, N, D), jnp.float32), 't_emb': jax.random.normal(ks[1], (B, D), jnp.float32), 'context': jax.random.normal(ks[2], (B, S, D), jnp.float32), 'context_mask': jnp.zeros((B, S), jnp.bool_), 'ada_w': jax.random.normal(ks[3], (D, 6 * D), jnp.float32) * s, 'ada_b': jnp.zeros((6 * D,), jnp.float32), 'qkv_w': jax.random.normal(ks[4], (D, 3 * D), jnp.float32) * s, 'qkv_b': jnp.zeros((3 * D,), jnp.float32), 'sa_proj_w': jax.random.normal(ks[5], (D, D), jnp.float32) * s, 'sa_proj_b': jnp.zeros((D,), jnp.float32), 'q_w': jax.random.normal(ks[6], (D, D), jnp.float32) * s, 'q_b': jnp.zeros((D,), jnp.float32), 'kv_w': jax.random.normal(ks[7], (D, 2 * D), jnp.float32) * s, 'kv_b': jnp.zeros((2 * D,), jnp.float32), 'ca_proj_w': jax.random.normal(ks[8], (D, D), jnp.float32) * s, 'ca_proj_b': jnp.zeros((D,), jnp.float32), 'fc1_w': jax.random.normal(ks[9], (D, DF), jnp.float32) * s, 'fc1_b': jnp.zeros((DF,), jnp.float32), 'fc2_w': jax.random.normal(ks[10], (DF, D), jnp.float32) * s, 'fc2_b': jnp.zeros((D,), jnp.float32)}
        return inp
    _L0_xcond_all = _L0_xcond_setup()
    _L0_xcond_in = {k: v for k, v in _L0_xcond_all.items() if k in ('ada_w', 'ada_b', 'qkv_w', 'qkv_b', 'sa_proj_w', 'sa_proj_b', 'q_w', 'q_b', 'kv_w', 'kv_b', 'ca_proj_w', 'ca_proj_b', 'fc1_w', 'fc1_b', 'fc2_w', 'fc2_b')}
    del _L0_xcond_all

    def _L1_xcond_setup():
        import jax, jax.numpy as jnp
        import numpy as np
        C = 256
        H = 16
        D = C // H
        WIN = 128
        SHIFT = 64
        TOPK = 16
        HID = 1024
        EPS = 1e-06

        def _ln(x):
            x32 = x.astype(jnp.float32)
            m = x32.mean(-1, keepdims=True)
            v = jnp.mean((x32 - m) ** 2, axis=-1, keepdims=True)
            return ((x32 - m) * jax.lax.rsqrt(v + EPS)).astype(x.dtype)

        def _self_attn(h, w_qkv, b_qkv, w_so, b_so):
            B, L, _ = h.shape
            qkv = h @ w_qkv + b_qkv
            qkv = jnp.roll(qkv, -SHIFT, axis=1)
            nw = L // WIN
            qkv = qkv.reshape(B, nw, WIN, 3, H, D)
            q, k, v = (qkv[:, :, :, 0], qkv[:, :, :, 1], qkv[:, :, :, 2])
            scores = jnp.einsum('bnqhd,bnkhd->bnhqk', q, k) / jnp.sqrt(jnp.float32(D)).astype(h.dtype)
            attn = jax.nn.softmax(scores, axis=-1)
            o = jnp.einsum('bnhqk,bnkhd->bnqhd', attn, v).reshape(B, L, C)
            o = jnp.roll(o, SHIFT, axis=1)
            return o @ w_so + b_so

        def _topk_cross_attn(h, ctx, w_q, b_q, w_kv, b_kv, w_co, b_co):
            B, L, _ = h.shape
            Lc = ctx.shape[1]
            q = (h @ w_q + b_q).reshape(B, L, H, D)
            kv = (ctx @ w_kv + b_kv).reshape(B, Lc, 2, H, D)
            k, v = (kv[:, :, 0], kv[:, :, 1])
            scores = jnp.einsum('bqhd,bkhd->bhqk', q, k) / jnp.sqrt(jnp.float32(D)).astype(h.dtype)
            top_s, top_i = jax.lax.top_k(scores, TOPK)
            attn = jax.nn.softmax(top_s, axis=-1)
            v_bh = jnp.transpose(v, (0, 2, 1, 3))
            vg = jnp.take_along_axis(v_bh[:, :, None, :, :], top_i[..., None], axis=3)
            o = jnp.einsum('bhqk,bhqkd->bqhd', attn, vg).reshape(B, L, C)
            return o @ w_co + b_co

        def _swiglu(h, w_m1, b_m1, w_m2, b_m2):
            u = h @ w_m1 + b_m1
            a, b = (u[..., :HID], u[..., HID:])
            return jax.nn.silu(a) * b @ w_m2 + b_m2
        key = jax.random.key(seed)
        ks = jax.random.split(key, 24)
        s = 0.02
        inp = {'x': jax.random.normal(ks[0], (2, 1024, C), jnp.float32), 'mod': jax.random.normal(ks[1], (2, C), jnp.float32), 'context': jax.random.normal(ks[2], (2, 256, C), jnp.float32), 'w_ada': jax.random.normal(ks[3], (C, 9 * C), jnp.float32) * s, 'b_ada': jnp.zeros((9 * C,), jnp.float32), 'w_qkv': jax.random.normal(ks[4], (C, 3 * C), jnp.float32) * s, 'b_qkv': jnp.zeros((3 * C,), jnp.float32), 'w_so': jax.random.normal(ks[5], (C, C), jnp.float32) * s, 'b_so': jnp.zeros((C,), jnp.float32), 'w_q': jax.random.normal(ks[6], (C, C), jnp.float32) * s, 'b_q': jnp.zeros((C,), jnp.float32), 'w_kv': jax.random.normal(ks[7], (C, 2 * C), jnp.float32) * s, 'b_kv': jnp.zeros((2 * C,), jnp.float32), 'w_co': jax.random.normal(ks[8], (C, C), jnp.float32) * s, 'b_co': jnp.zeros((C,), jnp.float32), 'w_m1': jax.random.normal(ks[9], (C, 2 * HID), jnp.float32) * s, 'b_m1': jnp.zeros((2 * HID,), jnp.float32), 'w_m2': jax.random.normal(ks[10], (HID, C), jnp.float32) * s, 'b_m2': jnp.zeros((C,), jnp.float32)}
        return inp
    _L1_xcond_all = _L1_xcond_setup()
    _L1_xcond_in = {k: v for k, v in _L1_xcond_all.items() if k in ('w_ada', 'b_ada', 'w_qkv', 'b_qkv', 'w_so', 'b_so', 'w_q', 'b_q', 'w_kv', 'b_kv', 'w_co', 'b_co', 'w_m1', 'b_m1', 'w_m2', 'b_m2')}
    del _L1_xcond_all

    def _L2_xcond_setup():
        import jax, jax.numpy as jnp
        import numpy as np
        EPS = 1e-05

        def _ada_ln(x, c, W_ss, b_ss):
            mu = jnp.mean(x, axis=-1, keepdims=True)
            var = jnp.mean((x - mu) ** 2, axis=-1, keepdims=True)
            h = (x - mu) / jnp.sqrt(var + EPS)
            ss = jax.nn.silu(c) @ W_ss + b_ss
            scale, bias = jnp.split(ss, 2, axis=-1)
            return (1.0 + scale)[:, None, :] * h + bias[:, None, :]
        key = jax.random.key(seed)
        ks = jax.random.split(key, 12)
        B, Lq, Lkv, H = (8, 512, 128, 256)
        s = 0.02
        return {'x_q': jax.random.normal(ks[0], (B, Lq, H), jnp.float32), 'x_kv': jax.random.normal(ks[1], (B, Lkv, H), jnp.float32), 't_vec': jax.random.normal(ks[2], (B, H), jnp.float32), 'Wq': jax.random.normal(ks[3], (H, H), jnp.float32) * s, 'bq': jnp.zeros((H,), jnp.float32), 'Wkv': jax.random.normal(ks[4], (H, 2 * H), jnp.float32) * s, 'bkv': jnp.zeros((2 * H,), jnp.float32), 'Wp': jax.random.normal(ks[5], (H, H), jnp.float32) * s, 'bp': jnp.zeros((H,), jnp.float32), 'Wss_q': jax.random.normal(ks[6], (H, 2 * H), jnp.float32) * s, 'bss_q': jnp.zeros((2 * H,), jnp.float32), 'Wss_kv': jax.random.normal(ks[7], (H, 2 * H), jnp.float32) * s, 'bss_kv': jnp.zeros((2 * H,), jnp.float32)}
    _L2_xcond_all = _L2_xcond_setup()
    _L2_xcond_in = {k: v for k, v in _L2_xcond_all.items() if k in ('Wq', 'bq', 'Wkv', 'bkv', 'Wp', 'bp', 'Wss_q', 'bss_q', 'Wss_kv', 'bss_kv')}
    del _L2_xcond_all

    def _L3_xcond_setup():
        import jax, jax.numpy as jnp
        import numpy as np
        LN_EPS = 1e-06

        def _ln(x):
            mu = jnp.mean(x, axis=-1, keepdims=True)
            var = jnp.var(x, axis=-1, keepdims=True)
            return (x - mu) * jax.lax.rsqrt(var + LN_EPS)
        key = jax.random.key(seed)
        H, NH = (256, 16)
        B, N, S = (4, 256, 77)
        MLP = int(H * 4.0)
        ks = jax.random.split(key, 20)
        s = 1.0 / np.sqrt(H)
        return {'x': jax.random.normal(ks[0], (B, N, H), jnp.float32), 'c': jax.random.normal(ks[1], (B, H), jnp.float32), 'context': jax.random.normal(ks[2], (B, S, H), jnp.float32), 'W_mod': jax.random.normal(ks[3], (H, 6 * H), jnp.float32) * s, 'b_mod': jnp.zeros((6 * H,), jnp.float32), 'W_qkv': jax.random.normal(ks[4], (H, 3 * H), jnp.float32) * s, 'b_qkv': jnp.zeros((3 * H,), jnp.float32), 'W_proj': jax.random.normal(ks[5], (H, H), jnp.float32) * s, 'b_proj': jnp.zeros((H,), jnp.float32), 'W_qc': jax.random.normal(ks[6], (H, H), jnp.float32) * s, 'b_qc': jnp.zeros((H,), jnp.float32), 'W_kvc': jax.random.normal(ks[7], (H, 2 * H), jnp.float32) * s, 'b_kvc': jnp.zeros((2 * H,), jnp.float32), 'W_cproj': jax.random.normal(ks[8], (H, H), jnp.float32) * s, 'b_cproj': jnp.zeros((H,), jnp.float32), 'W_mlp1': jax.random.normal(ks[9], (H, MLP), jnp.float32) * s, 'b_mlp1': jnp.zeros((MLP,), jnp.float32), 'W_mlp2': jax.random.normal(ks[10], (MLP, H), jnp.float32) * (1.0 / np.sqrt(MLP)), 'b_mlp2': jnp.zeros((H,), jnp.float32)}
    _L3_xcond_all = _L3_xcond_setup()
    _L3_xcond_in = {k: v for k, v in _L3_xcond_all.items() if k in ('W_mod', 'b_mod', 'W_qkv', 'b_qkv', 'W_proj', 'b_proj', 'W_qc', 'b_qc', 'W_kvc', 'b_kvc', 'W_cproj', 'b_cproj', 'W_mlp1', 'b_mlp1', 'W_mlp2', 'b_mlp2')}
    del _L3_xcond_all
    return {'x': x, 'cond_1024': cond_1024, 'ctx_1024': ctx_1024, 'mask_BxS2_bf0': mask_BxS2_bf0, 'L0_xcond_ada_w': _L0_xcond_in['ada_w'], 'L0_xcond_ada_b': _L0_xcond_in['ada_b'], 'L0_xcond_qkv_w': _L0_xcond_in['qkv_w'], 'L0_xcond_qkv_b': _L0_xcond_in['qkv_b'], 'L0_xcond_sa_proj_w': _L0_xcond_in['sa_proj_w'], 'L0_xcond_sa_proj_b': _L0_xcond_in['sa_proj_b'], 'L0_xcond_q_w': _L0_xcond_in['q_w'], 'L0_xcond_q_b': _L0_xcond_in['q_b'], 'L0_xcond_kv_w': _L0_xcond_in['kv_w'], 'L0_xcond_kv_b': _L0_xcond_in['kv_b'], 'L0_xcond_ca_proj_w': _L0_xcond_in['ca_proj_w'], 'L0_xcond_ca_proj_b': _L0_xcond_in['ca_proj_b'], 'L0_xcond_fc1_w': _L0_xcond_in['fc1_w'], 'L0_xcond_fc1_b': _L0_xcond_in['fc1_b'], 'L0_xcond_fc2_w': _L0_xcond_in['fc2_w'], 'L0_xcond_fc2_b': _L0_xcond_in['fc2_b'], 'L1_xcond_w_ada': _L1_xcond_in['w_ada'], 'L1_xcond_b_ada': _L1_xcond_in['b_ada'], 'L1_xcond_w_qkv': _L1_xcond_in['w_qkv'], 'L1_xcond_b_qkv': _L1_xcond_in['b_qkv'], 'L1_xcond_w_so': _L1_xcond_in['w_so'], 'L1_xcond_b_so': _L1_xcond_in['b_so'], 'L1_xcond_w_q': _L1_xcond_in['w_q'], 'L1_xcond_b_q': _L1_xcond_in['b_q'], 'L1_xcond_w_kv': _L1_xcond_in['w_kv'], 'L1_xcond_b_kv': _L1_xcond_in['b_kv'], 'L1_xcond_w_co': _L1_xcond_in['w_co'], 'L1_xcond_b_co': _L1_xcond_in['b_co'], 'L1_xcond_w_m1': _L1_xcond_in['w_m1'], 'L1_xcond_b_m1': _L1_xcond_in['b_m1'], 'L1_xcond_w_m2': _L1_xcond_in['w_m2'], 'L1_xcond_b_m2': _L1_xcond_in['b_m2'], 'L2_xcond_Wq': _L2_xcond_in['Wq'], 'L2_xcond_bq': _L2_xcond_in['bq'], 'L2_xcond_Wkv': _L2_xcond_in['Wkv'], 'L2_xcond_bkv': _L2_xcond_in['bkv'], 'L2_xcond_Wp': _L2_xcond_in['Wp'], 'L2_xcond_bp': _L2_xcond_in['bp'], 'L2_xcond_Wss_q': _L2_xcond_in['Wss_q'], 'L2_xcond_bss_q': _L2_xcond_in['bss_q'], 'L2_xcond_Wss_kv': _L2_xcond_in['Wss_kv'], 'L2_xcond_bss_kv': _L2_xcond_in['bss_kv'], 'L3_xcond_W_mod': _L3_xcond_in['W_mod'], 'L3_xcond_b_mod': _L3_xcond_in['b_mod'], 'L3_xcond_W_qkv': _L3_xcond_in['W_qkv'], 'L3_xcond_b_qkv': _L3_xcond_in['b_qkv'], 'L3_xcond_W_proj': _L3_xcond_in['W_proj'], 'L3_xcond_b_proj': _L3_xcond_in['b_proj'], 'L3_xcond_W_qc': _L3_xcond_in['W_qc'], 'L3_xcond_b_qc': _L3_xcond_in['b_qc'], 'L3_xcond_W_kvc': _L3_xcond_in['W_kvc'], 'L3_xcond_b_kvc': _L3_xcond_in['b_kvc'], 'L3_xcond_W_cproj': _L3_xcond_in['W_cproj'], 'L3_xcond_b_cproj': _L3_xcond_in['b_cproj'], 'L3_xcond_W_mlp1': _L3_xcond_in['W_mlp1'], 'L3_xcond_b_mlp1': _L3_xcond_in['b_mlp1'], 'L3_xcond_W_mlp2': _L3_xcond_in['W_mlp2'], 'L3_xcond_b_mlp2': _L3_xcond_in['b_mlp2']}

def reference(x, cond_1024, ctx_1024, mask_BxS2_bf0, L0_xcond_ada_w, L0_xcond_ada_b, L0_xcond_qkv_w, L0_xcond_qkv_b, L0_xcond_sa_proj_w, L0_xcond_sa_proj_b, L0_xcond_q_w, L0_xcond_q_b, L0_xcond_kv_w, L0_xcond_kv_b, L0_xcond_ca_proj_w, L0_xcond_ca_proj_b, L0_xcond_fc1_w, L0_xcond_fc1_b, L0_xcond_fc2_w, L0_xcond_fc2_b, L1_xcond_w_ada, L1_xcond_b_ada, L1_xcond_w_qkv, L1_xcond_b_qkv, L1_xcond_w_so, L1_xcond_b_so, L1_xcond_w_q, L1_xcond_b_q, L1_xcond_w_kv, L1_xcond_b_kv, L1_xcond_w_co, L1_xcond_b_co, L1_xcond_w_m1, L1_xcond_b_m1, L1_xcond_w_m2, L1_xcond_b_m2, L2_xcond_Wq, L2_xcond_bq, L2_xcond_Wkv, L2_xcond_bkv, L2_xcond_Wp, L2_xcond_bp, L2_xcond_Wss_q, L2_xcond_bss_q, L2_xcond_Wss_kv, L2_xcond_bss_kv, L3_xcond_W_mod, L3_xcond_b_mod, L3_xcond_W_qkv, L3_xcond_b_qkv, L3_xcond_W_proj, L3_xcond_b_proj, L3_xcond_W_qc, L3_xcond_b_qc, L3_xcond_W_kvc, L3_xcond_b_kvc, L3_xcond_W_cproj, L3_xcond_b_cproj, L3_xcond_W_mlp1, L3_xcond_b_mlp1, L3_xcond_W_mlp2, L3_xcond_b_mlp2):
    import jax
    import jax.numpy as jnp

    def _L0_xcond_ref(x, t_emb, context, context_mask, ada_w, ada_b, qkv_w, qkv_b, sa_proj_w, sa_proj_b, q_w, q_b, kv_w, kv_b, ca_proj_w, ca_proj_b, fc1_w, fc1_b, fc2_w, fc2_b):
        import jax, jax.numpy as jnp
        import numpy as np
        D, H, B, N, S = (256, 16, 4, 256, 77)
        HD = D // H
        DF = 4 * D
        EPS = 1e-06
        SCALE = HD ** (-0.5)

        def _ln(x):
            m = jnp.mean(x, axis=-1, keepdims=True)
            v = jnp.mean((x - m) ** 2, axis=-1, keepdims=True)
            return (x - m) / jnp.sqrt(v + EPS)
        Bx, Nx, C = x.shape
        Sx = context.shape[1]
        mod = jax.nn.silu(t_emb) @ ada_w + ada_b
        shift_sa, scale_sa, gate_sa, shift_ff, scale_ff, gate_ff = [m[:, None, :] for m in jnp.split(mod, 6, axis=-1)]
        xm1 = _ln(x) * (1 + scale_sa) + shift_sa
        qkv = (xm1 @ qkv_w + qkv_b).reshape(Bx, Nx, 3, H, HD)
        q, k, v = (qkv[:, :, 0], qkv[:, :, 1], qkv[:, :, 2])
        attn = jnp.einsum('bnhd,bmhd->bhnm', q, k) * SCALE
        attn = jax.nn.softmax(attn, axis=-1)
        sa = jnp.einsum('bhnm,bmhd->bnhd', attn, v).reshape(Bx, Nx, C)
        sa = sa @ sa_proj_w + sa_proj_b
        x = x + gate_sa * sa
        xn2 = _ln(x)
        qc = (xn2 @ q_w + q_b).reshape(Bx, Nx, H, HD)
        kvc = (context @ kv_w + kv_b).reshape(Bx, Sx, 2, H, HD)
        kc, vc = (kvc[:, :, 0], kvc[:, :, 1])
        attn_c = jnp.einsum('bnhd,bshd->bhns', qc, kc) * SCALE
        attn_c = jnp.where(context_mask[:, None, None, :], -jnp.inf, attn_c)
        attn_c = jax.nn.softmax(attn_c, axis=-1)
        ca = jnp.einsum('bhns,bshd->bnhd', attn_c, vc).reshape(Bx, Nx, C)
        ca = ca @ ca_proj_w + ca_proj_b
        x = x + ca
        xm3 = _ln(x) * (1 + scale_ff) + shift_ff
        h = jax.nn.gelu(xm3 @ fc1_w + fc1_b, approximate=False)
        ff = h @ fc2_w + fc2_b
        x = x + gate_ff * ff
        return x

    def _L1_xcond_ref(x, mod, context, w_ada, b_ada, w_qkv, b_qkv, w_so, b_so, w_q, b_q, w_kv, b_kv, w_co, b_co, w_m1, b_m1, w_m2, b_m2):
        import jax, jax.numpy as jnp
        import numpy as np
        C = 256
        H = 16
        D = C // H
        WIN = 128
        SHIFT = 64
        TOPK = 16
        HID = 1024
        EPS = 1e-06

        def _ln(x):
            x32 = x.astype(jnp.float32)
            m = x32.mean(-1, keepdims=True)
            v = jnp.mean((x32 - m) ** 2, axis=-1, keepdims=True)
            return ((x32 - m) * jax.lax.rsqrt(v + EPS)).astype(x.dtype)

        def _self_attn(h, w_qkv, b_qkv, w_so, b_so):
            B, L, _ = h.shape
            qkv = h @ w_qkv + b_qkv
            qkv = jnp.roll(qkv, -SHIFT, axis=1)
            nw = L // WIN
            qkv = qkv.reshape(B, nw, WIN, 3, H, D)
            q, k, v = (qkv[:, :, :, 0], qkv[:, :, :, 1], qkv[:, :, :, 2])
            scores = jnp.einsum('bnqhd,bnkhd->bnhqk', q, k) / jnp.sqrt(jnp.float32(D)).astype(h.dtype)
            attn = jax.nn.softmax(scores, axis=-1)
            o = jnp.einsum('bnhqk,bnkhd->bnqhd', attn, v).reshape(B, L, C)
            o = jnp.roll(o, SHIFT, axis=1)
            return o @ w_so + b_so

        def _topk_cross_attn(h, ctx, w_q, b_q, w_kv, b_kv, w_co, b_co):
            B, L, _ = h.shape
            Lc = ctx.shape[1]
            q = (h @ w_q + b_q).reshape(B, L, H, D)
            kv = (ctx @ w_kv + b_kv).reshape(B, Lc, 2, H, D)
            k, v = (kv[:, :, 0], kv[:, :, 1])
            scores = jnp.einsum('bqhd,bkhd->bhqk', q, k) / jnp.sqrt(jnp.float32(D)).astype(h.dtype)
            top_s, top_i = jax.lax.top_k(scores, TOPK)
            attn = jax.nn.softmax(top_s, axis=-1)
            v_bh = jnp.transpose(v, (0, 2, 1, 3))
            vg = jnp.take_along_axis(v_bh[:, :, None, :, :], top_i[..., None], axis=3)
            o = jnp.einsum('bhqk,bhqkd->bqhd', attn, vg).reshape(B, L, C)
            return o @ w_co + b_co

        def _swiglu(h, w_m1, b_m1, w_m2, b_m2):
            u = h @ w_m1 + b_m1
            a, b = (u[..., :HID], u[..., HID:])
            return jax.nn.silu(a) * b @ w_m2 + b_m2
        m = jax.nn.silu(mod) @ w_ada + b_ada
        sh_msa, sc_msa, g_msa, sh_mca, sc_mca, g_mca, sh_mlp, sc_mlp, g_mlp = [m[:, i * C:(i + 1) * C][:, None, :] for i in range(9)]
        h = _ln(x) * (1 + sc_msa) + sh_msa
        h = _self_attn(h, w_qkv, b_qkv, w_so, b_so)
        x = x + h * g_msa
        h = _ln(x) * (1 + sc_mca) + sh_mca
        h = _topk_cross_attn(h, context, w_q, b_q, w_kv, b_kv, w_co, b_co)
        x = x + h * g_mca
        h = _ln(x) * (1 + sc_mlp) + sh_mlp
        h = _swiglu(h, w_m1, b_m1, w_m2, b_m2)
        x = x + h * g_mlp
        return x

    def _L2_xcond_ref(x_q, x_kv, t_vec, Wq, bq, Wkv, bkv, Wp, bp, Wss_q, bss_q, Wss_kv, bss_kv):
        import jax, jax.numpy as jnp
        import numpy as np
        EPS = 1e-05

        def _ada_ln(x, c, W_ss, b_ss):
            mu = jnp.mean(x, axis=-1, keepdims=True)
            var = jnp.mean((x - mu) ** 2, axis=-1, keepdims=True)
            h = (x - mu) / jnp.sqrt(var + EPS)
            ss = jax.nn.silu(c) @ W_ss + b_ss
            scale, bias = jnp.split(ss, 2, axis=-1)
            return (1.0 + scale)[:, None, :] * h + bias[:, None, :]
        B, Lq, H = x_q.shape
        Lkv = x_kv.shape[1]
        nh = 16
        dh = H // nh
        xq = _ada_ln(x_q, t_vec, Wss_q, bss_q)
        xkv = _ada_ln(x_kv, t_vec, Wss_kv, bss_kv)
        q = (xq @ Wq + bq).reshape(B, Lq, nh, dh)
        kv = (xkv @ Wkv + bkv).reshape(B, Lkv, 2, nh, dh)
        k = kv[:, :, 0]
        v = kv[:, :, 1]
        scores = jnp.einsum('bqhd,bkhd->bhqk', q, k) / jnp.sqrt(jnp.float32(dh))
        attn = jax.nn.softmax(scores, axis=-1)
        out = jnp.einsum('bhqk,bkhd->bqhd', attn, v).reshape(B, Lq, H)
        return x_q + (out @ Wp + bp)

    def _L3_xcond_ref(x, c, context, W_mod, b_mod, W_qkv, b_qkv, W_proj, b_proj, W_qc, b_qc, W_kvc, b_kvc, W_cproj, b_cproj, W_mlp1, b_mlp1, W_mlp2, b_mlp2):
        import jax, jax.numpy as jnp
        import numpy as np
        LN_EPS = 1e-06

        def _ln(x):
            mu = jnp.mean(x, axis=-1, keepdims=True)
            var = jnp.var(x, axis=-1, keepdims=True)
            return (x - mu) * jax.lax.rsqrt(var + LN_EPS)
        B, N, H = x.shape
        NH = 16
        hd = H // NH
        scale = hd ** (-0.5)
        c_proj = jax.nn.silu(c) @ W_mod + b_mod
        shift_a, scale_a, gate_a, shift_m, scale_m, gate_m = jnp.split(c_proj, 6, axis=-1)

        def modulate(t, shift, sc):
            return t * (1 + sc[:, None]) + shift[:, None]
        x_norm = modulate(_ln(x), shift_a, scale_a)
        qkv = x_norm @ W_qkv + b_qkv
        q, k, v = jnp.split(qkv, 3, axis=-1)
        q = q.reshape(B, N, NH, hd).transpose(0, 2, 1, 3)
        k = k.reshape(B, N, NH, hd).transpose(0, 2, 1, 3)
        v = v.reshape(B, N, NH, hd).transpose(0, 2, 1, 3)
        attn_w = jax.nn.softmax(jnp.einsum('bhqd,bhkd->bhqk', q, k) * scale, axis=-1)
        attn_out = jnp.einsum('bhqk,bhkd->bhqd', attn_w, v)
        attn_out = attn_out.transpose(0, 2, 1, 3).reshape(B, N, H)
        attn_out = attn_out @ W_proj + b_proj
        x = x + gate_a[:, None] * attn_out
        S = context.shape[1]
        q_c = _ln(x) @ W_qc + b_qc
        kv_c = _ln(context) @ W_kvc + b_kvc
        k_c, v_c = jnp.split(kv_c, 2, axis=-1)
        q_c = q_c.reshape(B, N, NH, hd).transpose(0, 2, 1, 3)
        k_c = k_c.reshape(B, S, NH, hd).transpose(0, 2, 1, 3)
        v_c = v_c.reshape(B, S, NH, hd).transpose(0, 2, 1, 3)
        c_attn_w = jax.nn.softmax(jnp.einsum('bhqd,bhsd->bhqs', q_c, k_c) * scale, axis=-1)
        c_attn_out = jnp.einsum('bhqs,bhsd->bhqd', c_attn_w, v_c)
        c_attn_out = c_attn_out.transpose(0, 2, 1, 3).reshape(B, N, H)
        c_attn_out = c_attn_out @ W_cproj + b_cproj
        x = x + c_attn_out
        x_norm2 = modulate(_ln(x), shift_m, scale_m)
        h = jax.nn.gelu(x_norm2 @ W_mlp1 + b_mlp1)
        h = h @ W_mlp2 + b_mlp2
        x = x + gate_m[:, None] * h
        return x
    x = _L0_xcond_ref(x, cond_1024, ctx_1024, mask_BxS2_bf0, L0_xcond_ada_w, L0_xcond_ada_b, L0_xcond_qkv_w, L0_xcond_qkv_b, L0_xcond_sa_proj_w, L0_xcond_sa_proj_b, L0_xcond_q_w, L0_xcond_q_b, L0_xcond_kv_w, L0_xcond_kv_b, L0_xcond_ca_proj_w, L0_xcond_ca_proj_b, L0_xcond_fc1_w, L0_xcond_fc1_b, L0_xcond_fc2_w, L0_xcond_fc2_b)
    x = _L1_xcond_ref(x, cond_1024, ctx_1024, L1_xcond_w_ada, L1_xcond_b_ada, L1_xcond_w_qkv, L1_xcond_b_qkv, L1_xcond_w_so, L1_xcond_b_so, L1_xcond_w_q, L1_xcond_b_q, L1_xcond_w_kv, L1_xcond_b_kv, L1_xcond_w_co, L1_xcond_b_co, L1_xcond_w_m1, L1_xcond_b_m1, L1_xcond_w_m2, L1_xcond_b_m2)
    x = _L2_xcond_ref(x, ctx_1024, cond_1024, L2_xcond_Wq, L2_xcond_bq, L2_xcond_Wkv, L2_xcond_bkv, L2_xcond_Wp, L2_xcond_bp, L2_xcond_Wss_q, L2_xcond_bss_q, L2_xcond_Wss_kv, L2_xcond_bss_kv)
    x = _L3_xcond_ref(x, cond_1024, ctx_1024, L3_xcond_W_mod, L3_xcond_b_mod, L3_xcond_W_qkv, L3_xcond_b_qkv, L3_xcond_W_proj, L3_xcond_b_proj, L3_xcond_W_qc, L3_xcond_b_qc, L3_xcond_W_kvc, L3_xcond_b_kvc, L3_xcond_W_cproj, L3_xcond_b_cproj, L3_xcond_W_mlp1, L3_xcond_b_mlp1, L3_xcond_W_mlp2, L3_xcond_b_mlp2)
    return x

_drawn_inputs = setup_inputs


def setup_inputs(seed=0):
    import zlib

    import numpy as np

    out = dict(_drawn_inputs(seed))
    spreads = {'L0_xcond_ada_b': (0.0, 0.41),
     'L0_xcond_qkv_b': (0.0, 0.8),
     'L0_xcond_sa_proj_b': (0.0, 0.308),
     'L0_xcond_q_b': (0.0, 2.0),
     'L0_xcond_kv_b': (0.0, 0.348),
     'L0_xcond_ca_proj_b': (0.0, 0.1),
     'L0_xcond_fc1_b': (0.0, 0.8),
     'L0_xcond_fc2_b': (0.0, 0.352),
     'L1_xcond_b_ada': (0.0, 0.448),
     'L1_xcond_b_qkv': (0.0, 0.8),
     'L1_xcond_b_so': (0.0, 0.361),
     'L1_xcond_b_q': (0.0, 0.8),
     'L1_xcond_b_kv': (0.0, 0.8),
     'L1_xcond_b_co': (0.0, 0.327),
     'L1_xcond_b_m1': (0.0, 0.8),
     'L1_xcond_b_m2': (0.0, 2.0),
     'L2_xcond_bq': (0.0, 2.0),
     'L2_xcond_bkv': (0.0, 2.0),
     'L2_xcond_bp': (0.0, 2.0),
     'L2_xcond_bss_q': (0.0, 2.0),
     'L2_xcond_bss_kv': (0.0, 2.0),
     'L3_xcond_b_mod': (0.0, 0.707),
     'L3_xcond_b_qkv': (0.0, 0.8),
     'L3_xcond_b_proj': (0.0, 0.8),
     'L3_xcond_b_qc': (0.0, 2.0),
     'L3_xcond_b_kvc': (0.0, 2.0),
     'L3_xcond_b_cproj': (0.0, 0.8),
     'L3_xcond_b_mlp1': (0.0, 2.0),
     'L3_xcond_b_mlp2': (0.0, 0.8)}
    factors = {'L0_xcond_qkv_w': 8.0,
     'L0_xcond_sa_proj_w': 6.103,
     'L0_xcond_q_w': 31.745,
     'L0_xcond_fc1_w': 2.785,
     'L1_xcond_w_qkv': 8.0,
     'L1_xcond_w_so': 5.6,
     'L1_xcond_w_q': 6.63,
     'L1_xcond_w_kv': 3.42,
     'L1_xcond_w_co': 2.926,
     'L1_xcond_w_m1': 7.504,
     'L1_xcond_w_m2': 7.497,
     'L2_xcond_Wq': 64.0,
     'L2_xcond_Wss_q': 64.0,
     'L2_xcond_Wkv': 7.995,
     'L2_xcond_Wp': 6.627,
     'L2_xcond_Wss_kv': 8.0,
     'L3_xcond_W_qc': 5.064}
    for name, (base, spread) in spreads.items():
        noise = np.random.default_rng([zlib.crc32(name.encode()), seed]).standard_normal(out[name].shape)
        drawn = base * np.exp(spread * noise) if base else spread * noise
        out[name] = jnp.asarray(drawn.astype(out[name].dtype))
    for name, factor in factors.items():
        out[name] = (out[name] * factor).astype(out[name].dtype)
    return out
```

```python
from contextlib import ExitStack

import numpy as np

import concourse.bass as bass
from concourse import mybir

F32 = mybir.dt.float32
BF16 = mybir.dt.bfloat16
U8 = mybir.dt.uint8
ACT = mybir.ActivationFunctionType
ALU = mybir.AluOpType
AX = mybir.AxisListType

P = 128
B, N, D, H, HD = 2, 1024, 256, 16, 16
S, SP = 154, 160
SR = S - P
SHIFT = 64
KT = D // P
TOK = B * N
CW = 512
CH = TOK // CW
DF = 1024
FT = DF // P
SCALE = HD ** -0.5
BIG = -3.0e38
HG = 4
PARTS = 3
PAIRS = 6
QPART = (0, 0, 0, 1, 1, 2)
KPART = (0, 1, 2, 0, 1, 0)
Q_RUNS = ((0, 0, 3), (3, 1, 2), (5, 2, 1))
K_RUNS = ((0, 3), (3, 2), (5, 1))
ONE_BF16_TWICE = float(np.array([0x3F803F80], np.uint32).view(np.float32)[0])
R_MASK = PAIRS * HD
R_MAX = R_MASK + 1
R_ALL = R_MAX + 2

BIASES = [("L0_xcond_ada_b", 12), ("L1_xcond_b_ada", 18), ("L2_xcond_bss_q", 4), ("L2_xcond_bss_kv", 4),
          ("L3_xcond_b_mod", 12),
          ("L0_xcond_qkv_b", 6), ("L0_xcond_sa_proj_b", 2), ("L0_xcond_q_b", 2), ("L0_xcond_kv_b", 4),
          ("L0_xcond_ca_proj_b", 2), ("L0_xcond_fc1_b", 8), ("L0_xcond_fc2_b", 2),
          ("L1_xcond_b_qkv", 6), ("L1_xcond_b_so", 2), ("L1_xcond_b_q", 2), ("L1_xcond_b_kv", 4),
          ("L1_xcond_b_co", 2), ("L1_xcond_b_m1", 16), ("L1_xcond_b_m2", 2),
          ("L2_xcond_bq", 2), ("L2_xcond_bkv", 4), ("L2_xcond_bp", 2),
          ("L3_xcond_b_qkv", 6), ("L3_xcond_b_proj", 2), ("L3_xcond_b_qc", 2), ("L3_xcond_b_kvc", 4),
          ("L3_xcond_b_cproj", 2), ("L3_xcond_b_mlp1", 8), ("L3_xcond_b_mlp2", 2)]
ADA = [("L0_xcond_ada_w", 12), ("L1_xcond_w_ada", 18), ("L2_xcond_Wss_q", 4), ("L2_xcond_Wss_kv", 4),
       ("L3_xcond_W_mod", 12)]
MT = sum(n for _, n in ADA)
MOD0 = {"L0": 0, "L1": 12, "L2q": 30, "L2kv": 34, "L3": 38}
SCALE_TILES = [("L0", 2), ("L0", 8), ("L1", 2), ("L1", 8), ("L1", 14), ("L2q", 0), ("L2kv", 0), ("L3", 2), ("L3", 8)]
KV = [("L0_xcond_kv_w", "L0_xcond_kv_b"), ("L1_xcond_w_kv", "L1_xcond_b_kv"), ("L2_xcond_Wkv", "L2_xcond_bkv"),
      ("L3_xcond_W_kvc", "L3_xcond_b_kvc")]
KV_CTX = (0, 0, 1, 2)
V_BIAS = [("L0_xcond_qkv_b", 512), ("L0_xcond_kv_b", 256), ("L1_xcond_b_qkv", 512), ("L1_xcond_b_kv", 256),
          ("L2_xcond_bkv", 256), ("L3_xcond_b_qkv", 512), ("L3_xcond_b_kvc", 256)]


def bias_column(name, tile=0):
    at = 0
    for n, tiles in BIASES:
        if n == name:
            return at + tile
        at += tiles
    raise KeyError(name)


TOKEN_STAGES = [
    dict(proj=None, ln=(1e-6, ("L0", 2), ("L0", 0)), mlp=None, ln2=None, out=("qkv", "L0_xcond_qkv_w", "L0_xcond_qkv_b")),
    dict(proj=("L0_xcond_sa_proj_w", "L0_xcond_sa_proj_b", ("L0", 4)), ln=(1e-6, None, None), mlp=None, ln2=None,
         out=("q", "L0_xcond_q_w", "L0_xcond_q_b")),
    dict(proj=("L0_xcond_ca_proj_w", "L0_xcond_ca_proj_b", None), ln=(1e-6, ("L0", 8), ("L0", 6)),
         mlp=("L0_xcond_fc1_w", "L0_xcond_fc1_b", "gelu", "L0_xcond_fc2_w", "L0_xcond_fc2_b", ("L0", 10)),
         ln2=(1e-6, ("L1", 2), ("L1", 0)), out=("qkv", "L1_xcond_w_qkv", "L1_xcond_b_qkv")),
    dict(proj=("L1_xcond_w_so", "L1_xcond_b_so", ("L1", 4)), ln=(1e-6, ("L1", 8), ("L1", 6)), mlp=None, ln2=None,
         out=("q", "L1_xcond_w_q", "L1_xcond_b_q")),
    dict(proj=("L1_xcond_w_co", "L1_xcond_b_co", ("L1", 10)), ln=(1e-6, ("L1", 14), ("L1", 12)),
         mlp=("L1_xcond_w_m1", "L1_xcond_b_m1", "swiglu", "L1_xcond_w_m2", "L1_xcond_b_m2", ("L1", 16)),
         ln2=(1e-5, ("L2q", 0), ("L2q", 2)), out=("q", "L2_xcond_Wq", "L2_xcond_bq")),
    dict(proj=("L2_xcond_Wp", "L2_xcond_bp", None), ln=(1e-6, ("L3", 2), ("L3", 0)), mlp=None, ln2=None,
         out=("qkv", "L3_xcond_W_qkv", "L3_xcond_b_qkv")),
    dict(proj=("L3_xcond_W_proj", "L3_xcond_b_proj", ("L3", 4)), ln=(1e-6, None, None), mlp=None, ln2=None,
         out=("q", "L3_xcond_W_qc", "L3_xcond_b_qc")),
    dict(proj=("L3_xcond_W_cproj", "L3_xcond_b_cproj", None), ln=(1e-6, ("L3", 8), ("L3", 6)),
         mlp=("L3_xcond_W_mlp1", "L3_xcond_b_mlp1", "gelu_tanh", "L3_xcond_W_mlp2", "L3_xcond_b_mlp2", ("L3", 10)),
         ln2=None, out=None),
]
ATTENTION = [("self", None, 0), ("cross", 0, 1), ("window", None, 2), ("topk", 1, 3), ("cross", 2, 4),
             ("self", None, 5), ("cross", 3, 6)]
HALVES = 16
MAX_TILES = {"self": 32, "cross": 8, "window": 4}
EXP_STEPS = {"self": 16, "cross": 3, "window": 2}


def head_last(w):
    return w.rearrange("p (g j d) -> p g d j", j=HG, d=HD)


class TokenOrder:

    def __init__(self, stages):
        n = dict(lin=0, pair=0, lnt=0, y=0, xt=0, h=0, split=0, ab=0, ln=0, res=0, store=0)
        self.stages = []
        self.xt_last_product = []
        self.h_last_product = []
        for st in stages:
            phases = []
            if st["proj"]:
                phases += [("proj", *st["proj"]), ("residual", st["ln"])]
            else:
                phases += [("norm", st["ln"])]
            phases.append(("spread", st["ln"]))
            if st["mlp"]:
                up_w, up_b, kind, dn_w, dn_b, gate = st["mlp"]
                phases += [("up", up_w, up_b, kind), ("down", dn_w, dn_b, gate), ("residual", st["ln2"])]
                if st["ln2"]:
                    phases.append(("spread", st["ln2"]))
            if st["out"]:
                phases.append(st["out"])
            items = []
            xt = [None] * CH
            hb = [None] * CH
            yb = [None] * CH
            for t in range(len(phases) + CH - 1):
                for c in range(CH):
                    if not 0 <= t - c < len(phases):
                        continue
                    ph = phases[t - c]
                    it = dict(kind=ph[0], spec=ph, c=c, first=(t - c, c))
                    if ph[0] in ("proj", "down"):
                        it["lin"] = n["lin"]
                        n["lin"] += KT
                        it["y"] = yb[c] = n["y"]
                        n["y"] += 1
                        if ph[0] == "down":
                            it["h"] = hb[c]
                            self.h_last_product.append(n["lin"])
                    if ph[0] in ("residual", "norm"):
                        if ph[0] == "residual":
                            it["pair"] = n["pair"]
                            n["pair"] += 1
                            it["y"] = yb[c]
                            it["res"] = n["res"]
                            n["res"] += 1
                        if ph[1]:
                            it["ln"] = n["ln"]
                            n["ln"] += 1
                        else:
                            it["store"] = n["store"]
                            n["store"] += 1
                    if ph[0] == "spread":
                        it["lnt"] = n["lnt"]
                        n["lnt"] += 1
                        it["xt"] = xt[c] = n["xt"]
                        n["xt"] += 1
                    if ph[0] == "up":
                        it["lin"] = n["lin"]
                        n["lin"] += FT * (2 if ph[3] == "swiglu" else 1)
                        it["xt"] = xt[c]
                        self.xt_last_product.append(("lin", n["lin"]))
                        it["h"] = hb[c] = n["h"]
                        n["h"] += 1
                        if ph[3] == "swiglu":
                            it["ab"] = n["ab"]
                            n["ab"] += FT
                    if ph[0] in ("qkv", "q"):
                        it["lin"] = n["lin"]
                        it["split"] = n["split"]
                        tiles = KT * (2 if ph[0] == "qkv" else 1)
                        n["lin"] += tiles
                        n["split"] += tiles
                        it["xt"] = xt[c]
                        if ph[0] == "qkv":
                            it["pair"] = n["pair"]
                            n["pair"] += 1
                            it["v"] = n["pair"]
                            self.xt_last_product.append(("pair", n["pair"]))
                        else:
                            self.xt_last_product.append(("lin", n["lin"]))
                    items.append(it)
            self.stages.append(items)
        self.n = n


def build_program(nc, ins, out, stages):
    order = TokenOrder(TOKEN_STAGES[:stages])
    ctx = ExitStack()
    with ctx:
        def sb(name, shape, dt=F32):
            return ctx.enter_context(nc.sbuf_tensor(name, shape, dt))

        def sem(name):
            return ctx.enter_context(nc.semaphore(name))

        def sems(name, n):
            return [sem(f"{name}{i}") for i in range(n)]

        q_parts = nc.dram_tensor("q_parts", (2 * B, 2, PARTS, P, CW), BF16, kind="Internal").ap()
        k_parts = nc.dram_tensor("k_parts", (2 * B, PARTS, P, N), BF16, kind="Internal").ap()
        kc_parts = nc.dram_tensor("kc_parts", (len(KV) * 2 * B, PARTS, P, SP), BF16, kind="Internal").ap()

        x = sb("x", [P, TOK // P, D])
        v_all = sb("v_all", [P, 2 * B, N // P, P])
        o_t = sb("o_t", [P, 2 * B, N])
        ident = sb("ident", [P, P])
        ident_bf = sb("ident_bf", [P, P], BF16)
        bias_cols = sb("bias_cols", [P, 2 * P])
        bias_cols_hl = sb("bias_cols_hl", [P, 2 * P])
        mod = sb("mod", [P, MT, B])
        v_bias = sb("v_bias", [P, len(V_BIAS), 2 * B, 2])
        v_ctx = sb("v_ctx", [P, len(KV), B, D])
        v_ctx_rest = sb("v_ctx_rest", [P, len(KV), B, D])
        reorder = sb("reorder", [P, 2 * D])
        v_topk_rest = sb("v_topk_rest", [32, B, D])
        mask_row = sb("mask_row", [1, B, SP], BF16)
        minus_half = sb("minus_half", [P, 4])

        WBYTES = (28 * 1024, 24 * 1024)
        weights = [sb(f"weights{i}", [P, WBYTES[i] // 4]) for i in range(2)]
        WORK = 80 * 1024
        work = sb("work", [P, WORK // 4])

        class Carve:
            def __init__(self):
                self.at = 0

            def take(self, words, dt=F32):
                ap = work[:, self.at:self.at + words]
                self.at += words
                assert self.at * 4 <= WORK, self.at * 4
                return ap if dt is F32 else ap.bitcast(dt)

        cw = Carve()
        ada_w = cw.take(KT * MT * P).rearrange("p (k n) -> p k n", k=KT)
        bias_rows = cw.take(2 * P).rearrange("p (r n) -> p r n", r=2)
        bias_rows_hl = cw.take(2 * P).rearrange("p (r n) -> p r n", r=2)
        cond_t = cw.take(KT * B).rearrange("p (k b) -> p k b", k=KT)
        cond_silu = cw.take(KT * B).rearrange("p (k b) -> p k b", k=KT)
        ctx_tok = cw.take(2 * B * D).rearrange("p (t d) -> p t d", t=2 * B)
        ctx_norm = weights[0][:, 4096:4096 + 2 * 2 * B * D].rearrange("p (e t d) -> p e t d", e=2, t=2 * B)
        ctx_t = cw.take(3 * KT * B * SP).rearrange("p (e k s) -> p e k s", e=3, k=KT)
        ctx_stats = cw.take(6 * 2 * B).rearrange("p (t s) -> p t s", s=6)
        ctx_mv = cw.take(2 * 2 * B).rearrange("p (t s) -> p t s", s=2)
        ctx_eps = cw.take(2 * 2 * B).rearrange("p (e t) -> p e t", e=2)
        ctx_rstd = cw.take(2 * 2 * B).rearrange("p (e t) -> p e t", e=2)
        kc32 = [cw.take(B * SP) for _ in range(2)]
        kc_rest = [cw.take(B * SP) for _ in range(2)]
        kc_split = [cw.take(PARTS * B * SP // 2, BF16).rearrange("p (a s) -> p a s", a=PARTS) for _ in range(4)]
        v_rest = weights[1][0:32, 4096:4096 + len(KV) * B * D].rearrange("p (l b d) -> p l b d", l=len(KV), b=B)
        mask_u8 = cw.take(B * SP, U8)[0:1, 0:B * SP].rearrange("p (b s) -> p b s", b=B)
        mask_f = cw.take(B * SP)[0:1, :].rearrange("p (b s) -> p b s", b=B)

        ct = Carve()
        h = [ct.take(FT * CW).rearrange("p (m t) -> p m t", m=FT) for _ in range(2)]
        xt = [ct.take(KT * CW).rearrange("p (k t) -> p k t", k=KT) for _ in range(2)]
        xn = [ct.take(4 * D).rearrange("p (t d) -> p t d", t=4) for _ in range(2)]
        y = [ct.take(KT * CW).rearrange("p (k t) -> p k t", k=KT) for _ in range(2)]
        gate_half = [ct.take(CW) for _ in range(2)]
        x32 = [ct.take(CW) for _ in range(2)]
        xrest = [ct.take(CW) for _ in range(2)]
        split = [ct.take(PARTS * CW // 2, BF16).rearrange("p (a t) -> p a t", a=PARTS) for _ in range(3)]
        stats = [ct.take(4 * 6).rearrange("p (t s) -> p t s", s=6) for _ in range(2)]
        mv = [ct.take(4 * 2).rearrange("p (t s) -> p t s", s=2) for _ in range(2)]
        var_eps = [ct.take(4) for _ in range(2)]
        rstd = [ct.take(4) for _ in range(2)]

        ca = Carve()
        q_stack = [ca.take(HG * N // 2, BF16).rearrange("p (a j t) -> p a j t", a=2, j=HG) for _ in range(2)]
        k_stack = [ca.take(HG * N // 2, BF16).rearrange("p (j t) -> p j t", j=HG) for _ in range(2)]
        v_ones = [ca.take(N // P * HG * 2 * HD).rearrange("p (t j e) -> p t j e", t=N // P, j=HG) for _ in range(2)]
        v_ones_rest = [ca.take(HG * 2 * HD).rearrange("p (j e) -> p j e", j=HG) for _ in range(2)]
        NPR = 4
        probs = [ca.take(2 * CW) for _ in range(NPR)]
        o_raw = ca.take(CW)
        o_norm = ca.take(4 * HG * HD).rearrange("p (t d) -> p t d", t=4)
        o_rsum = ca.take(4 * HG)
        row_max = ca.take(HG * 4 * 2)
        neg_max = ca.take(HG * 4)
        max_parts = ca.take(HG * 4, BF16)
        max_rows = ca.take(P // 2, BF16)[0:2 * HG * 4, :]
        top1 = [ca.take(2 * 8).rearrange("p (a e) -> p a e", a=2) for _ in range(2)]
        top2 = [ca.take(2 * 8).rearrange("p (a e) -> p a e", a=2) for _ in range(2)]
        neg_top = [ca.take(2) for _ in range(2)]

        ps = ctx.enter_context(nc.psum_tensor("ps", [P, 8, 512], F32))
        LIN = (0, 1, 2, 3)
        PS_SPREAD, PS_PAIR = 4, 6
        PS_EXP, PS_MAX, PS_OUT, PS_MISC = 0, 4, 6, 7

        stage_end = {e: sem(f"{e}_stage_end") for e in ("pe", "act", "dve", "pool", "sp")}
        const_ready = sem("const_ready")
        bias_loaded, ada_loaded, cond_loaded, ctx_loaded, mask_loaded, x_loaded = (
            sem(n) for n in ("bias_loaded", "ada_loaded", "cond_loaded", "ctx_loaded", "mask_loaded", "x_loaded"))
        w_loaded, kv_loaded = sem("w_loaded"), sem("kv_loaded")
        kc_stored = sems("kc_stored", 4)
        act_link, dve_link, pool_link = sem("act_link"), sem("dve_link"), sem("pool_link")
        pre_pe, pre_act, pre_dve, pre_pool, pre_dma = (sem(f"pre_{n}") for n in ("pe", "act", "dve", "pool", "dma"))
        lin_full = sem("lin_full")
        lin_free = sems("lin_free", len(LIN))
        pair_full, pair_free = sem("pair_full"), sem("pair_free")
        spread_full = sem("spread_full")
        y_ready, xn_ready, xt_ready, h_ready, h_done = (sem(n) for n in ("y_ready", "xn_ready", "xt_ready", "h_ready", "h_done"))
        a_ready, var_ready, rstd_ready = sem("a_ready"), sem("var_ready"), sem("rstd_ready")
        hi_ready, mid_ready, lo_ready = sem("hi_ready"), sem("mid_ready"), sem("lo_ready")
        parts_stored = sems("parts_stored", 3)
        x_final, out_stored = sem("x_final"), sem("out_stored")
        reordered, bias_reordered, kv_reordered = sem("reordered"), sem("bias_reordered"), sem("kv_reordered")
        unit_loaded = sems("unit_loaded", 2)
        v_ready = sem("v_ready")
        init_done, q_ones_ready = sem("init_done"), sem("q_ones_ready")
        max_full, max_done, max_parts_ready = sem("max_full"), sem("max_done"), sem("max_parts_ready")
        rows_full, rows_ready, rows_loaded = sem("rows_full"), sem("rows_ready"), sem("rows_loaded")
        exp_full, exp_done, pv_done = sem("exp_full"), sem("exp_done"), sem("pv_done")
        raw_ready, raw_t_full, norm_ready, norm_t_full, o_ready = (
            sem(n) for n in ("raw_ready", "raw_t_full", "norm_ready", "norm_t_full", "o_ready"))
        rsum_ready = sem("rsum_ready")
        top_ready, weight_ready, prob_ready, turn_full, turned = (
            sem(n) for n in ("top_ready", "weight_ready", "prob_ready", "turn_full", "turned"))
        turned_rest = sem("turned_rest")
        neg_top_ready = sem("neg_top_ready")
        masked_ready = sem("masked_ready")
        topk_link, topk_hold = sem("topk_link"), sem("topk_hold")

        NSTAGE = 1 + stages + min(stages, len(ATTENTION))
        ENGINES = ("pe", "act", "dve", "pool", "sp")

        def leave_stage(eng, name):
            eng.drain().then_inc(stage_end[name], 1)

        def enter_stage(eng, name, number):
            for other in ENGINES:
                if other != name:
                    eng.wait_ge(stage_end[other], number)

        def stage_sequence():
            number = 1
            for s in range(stages):
                yield "token", s, number
                number += 1
                if s + 1 < stages:
                    yield "attention", s, number
                    number += 1

        def weight_list(s):
            st = TOKEN_STAGES[s]
            names = []
            if st["proj"]:
                names.append(st["proj"][0])
            if st["mlp"]:
                names += [st["mlp"][0], st["mlp"][3]]
            if st["out"]:
                names.append(st["out"][1])
            return names

        weight_at, weight_count = {}, [0]
        for s in range(stages):
            at, buf = 0, weights[s % 2]
            for name in weight_list(s):
                rows, cols = ins[name].shape
                words = rows // P * cols
                weight_at[name] = buf[:, at:at + words].rearrange("p (k n) -> p k n", k=rows // P)
                at += words
            assert at * 4 <= WBYTES[s % 2], (s, at * 4)
            weight_count.append(weight_count[-1] + len(weight_list(s)))

        def load_weights(sp, s):
            for name in weight_list(s):
                sp.dma_start(weight_at[name], ins[name].rearrange("(k p) n -> p k n", p=P)).then_inc(w_loaded, 16)

        def x_rows(dram, b):
            half = P - SHIFT
            yield dram[b, SHIFT:SHIFT + (N // P - 1) * P, :].rearrange("(t p) d -> p t d", p=P), slice(0, P), slice(0, N // P - 1)
            yield dram[b, N - half:N, :], slice(0, half), slice(N // P - 1, N // P)
            yield dram[b, 0:SHIFT, :], slice(half, P), slice(N // P - 1, N // P)

        def mod_col(which, k, b):
            layer, tile = which
            return mod[:, MOD0[layer] + tile + k, b:b + 1]

        def bias_col(name, tile):
            c = bias_column(name, tile)
            return bias_cols[:, c:c + 1]

        def bias_col_head_last(name, tile):
            c = bias_column(name, tile)
            return bias_cols_hl[:, c:c + 1]


        def sp_token(sp, s):
            for it in order.stages[s]:
                c = it["c"]
                if it["kind"] in ("q", "qkv"):
                    tiles = KT * (2 if it["kind"] == "qkv" else 1)
                    for m in range(tiles):
                        n = it["split"] + m
                        turn = c // 2 * 2 + m % KT
                        if m < KT:
                            dst = q_parts[turn, c % 2, :, :, :]
                        else:
                            dst = k_parts[turn, :, :, c % 2 * CW:(c % 2 + 1) * CW]
                        sp.wait_ge(lo_ready, n + 1)
                        sp.dma_start(dst.rearrange("a p t -> p a t"), split[n % 3]).then_inc(parts_stored[n % 3], 16)
                if "store" in it:
                    sp.wait_ge(x_final, it["store"] + 1)
                    store_chunk(sp, c)
            for r in range(3):
                uses = sum(1 for n in range(split_uses(s)) if n % 3 == r)
                if uses:
                    sp.wait_ge(parts_stored[r], 16 * uses)
            if s + 1 == len(TOKEN_STAGES):
                sp.wait_ge(out_stored, 16 * stored[0])

        stored = [0]

        def store_chunk(sp, c):
            b, first = c // 2, c % 2 * 4
            if first == 0:
                sp.dma_start(out[b, SHIFT:SHIFT + CW, :].rearrange("(t p) d -> p t d", p=P), x[:, c * 4:c * 4 + 4, :]).then_inc(out_stored, 16)
                stored[0] += 1
            else:
                half = P - SHIFT
                sp.dma_start(out[b, SHIFT + CW:SHIFT + CW + 3 * P, :].rearrange("(t p) d -> p t d", p=P),
                             x[:, c * 4:c * 4 + 3, :]).then_inc(out_stored, 16)
                sp.dma_start(out[b, N - half:N, :], x[0:half, c * 4 + 3, :]).then_inc(out_stored, 16)
                sp.dma_start(out[b, 0:SHIFT, :], x[half:P, c * 4 + 3, :]).then_inc(out_stored, 16)
                stored[0] += 3

        def split_uses(s):
            n = 0
            for st in order.stages[:s + 1]:
                for it in st:
                    if it["kind"] in ("q", "qkv"):
                        n = max(n, it["split"] + KT * (2 if it["kind"] == "qkv" else 1))
            return n

        def before(s, per_kind):
            return sum(per_kind(ATTENTION[a]) for a in range(s))

        def usual(count):
            return lambda a: HALVES * (count[a[0]] if a[0] in count else 0)

        def base(s, what):
            if what == "max":
                return before(s, usual({**MAX_TILES, "topk": 8}))
            if what == "exp":
                return before(s, usual(EXP_STEPS))
            if what == "pv":
                return before(s, usual({**EXP_STEPS, "topk": 4}))
            if what == "half":
                return before(s, usual({k: 1 for k in ("self", "cross", "window", "topk")}))
            if what == "maxrow":
                return before(s, usual({k: 1 for k in ("self", "cross", "window")}))
            if what == "unit":
                return before(s, lambda a: HALVES // 2)
            if what == "load":
                return before(s, lambda a: HALVES // 4 * 16 * loads(a))
            if what == "topk":
                return before(s, usual({"topk": 1}))
            raise KeyError(what)

        def has_mask(a):
            return a[0] == "cross" and a[1] == 0

        def loads(a):
            return 2 * len(Q_RUNS) + len(K_RUNS) + has_mask(a)

        def k_view(kind, par):
            if kind in ("self", "window"):
                return k_stack[par]
            return k_stack[par].rearrange("p j t -> p (j t)")[:, 0:HG * SP].rearrange("p (j s) -> p j s", j=HG)

        def on_halves(eng, body):
            turns = HALVES // 4
            body(0, True, False)
            with eng.Fori(1, turns - 1) as i:
                body(i, False, False)
            body(turns - 1, False, True)

        def sp_attention(sp, s):
            kind, layer, _ = ATTENTION[s]
            lb, rb = base(s, "load"), base(s, "maxrow")
            def load_unit(i, par, first):
                u = i * 2 + par
                if not first:
                    if kind == "topk":
                        sp.wait_ge(max_full, base(s, "max") + (u - 1) * 16)
                    else:
                        sp.wait_ge(exp_full, base(s, "exp") + (u - 1) * 2 * EXP_STEPS[kind])
                rows = slice(par * 64, par * 64 + 64)
                for a in range(2):
                    for at, part, n in Q_RUNS:
                        src = q_parts[i, a, part:part + 1, rows, :].rearrange("x (d j) t -> x d (j t)", j=HG)
                        sp.dma_start(q_stack[par][at * HD:(at + n) * HD, a, :, :], src.to_broadcast([n, HD, HG * CW]))\
                            .then_inc(unit_loaded[par], 16)
                    if a == 0:
                        for at, n in K_RUNS:
                            src = k_parts[i, 0:n, rows, :] if kind in ("self", "window") else kc_parts[i + layer * 4, 0:n, rows, :]
                            sp.dma_start(k_view(kind, par)[at * HD:(at + n) * HD, :, :], src.rearrange("x (d j) t -> x d (j t)", j=HG))\
                                .then_inc(unit_loaded[par], 16)
                if has_mask(ATTENTION[s]):
                    if isinstance(i, int) and i == 0:
                        sp.wait_ge(init_done, s + 1)
                    at = slice(i, i + 1) if isinstance(i, int) else bass.ds(i, 1)
                    sp.dma_start(k_view(kind, par)[R_MASK:R_MASK + 1, :, :], mask_by_turn[:, at, :].to_broadcast([1, HG, SP]))\
                        .then_inc(unit_loaded[par], 16)

            def max_row(i, q):
                p = i * 4 + q
                par, hq = q // 2, q % 2
                sp.wait_ge(rows_ready, rb + p + 1)
                sp.dma_start(q_stack[par][R_MAX:R_MAX + 2, hq, :, :].rearrange("p j t -> p (j t)"), max_rows[:, :]).then_inc(rows_loaded, 16)

            def body(i, first, last):
                for q in range(4):
                    if kind != "topk":
                        max_row(i, q)
                    if q == 0:
                        load_unit(i, 1, first)
                    if q == 2 and not last:
                        load_unit(i + 1, 0, False)

            load_unit(0, 0, True)
            on_halves(sp, body)
            for par in range(2):
                sp.wait_ge(unit_loaded[par], base(s + 1, "load"))
            if kind != "topk":
                sp.wait_ge(rows_loaded, 16 * (rb + HALVES))

        mask_by_turn = sb("mask_by_turn", [1, 2 * B, SP], BF16)

        MIDS0 = KT * len(KV)

        def columns_head_last(pool, w):
            n = w.shape[1]
            tmp = reorder[:, 0:n]
            nc.gpsimd.tensor_copy(tmp.rearrange("p (g d j) -> p g d j", j=HG, d=HD), head_last(w)).then_inc(reordered, 1)
            reorders[0] += 1
            pool.wait_ge(reordered, reorders[0])
            nc.gpsimd.tensor_copy(w, tmp).then_inc(reordered, 1)
            reorders[0] += 1
            pool.wait_ge(reordered, reorders[0])

        reorders = [0]

        def reorder_weights(pool, s):
            st = TOKEN_STAGES[s]
            if st["out"]:
                pool.wait_ge(w_loaded, 16 * weight_count[s + 1])
                w = weight_at[st["out"][1]]
                for k in range(KT):
                    columns_head_last(pool, w[:, k, 0:D * (2 if st["out"][0] == "qkv" else 1)])

        def pool_token(pool, s):
            for it in order.stages[s]:
                if "ln" in it:
                    n = it["ln"]
                    pool.wait_ge(var_ready, n + 1)
                    nc.gpsimd.tensor_tensor(rstd[n % 2], var_eps[n % 2], minus_half[:, :], ALU.pow).then_inc(rstd_ready, 1)
                if it["kind"] in ("q", "qkv"):
                    for m in range(KT * (2 if it["kind"] == "qkv" else 1)):
                        n = it["split"] + m
                        pool.wait_ge(mid_ready, MIDS0 + n + 1)
                        nc.gpsimd.tensor_tensor(split[n % 3][:, 2, :], xrest[n % 2], split[n % 3][:, 1, :], ALU.subtract)\
                            .then_inc(lo_ready, 1)

        def pool_attention(pool, s):
            kind, layer, _ = ATTENTION[s]
            links = [pool_links(s)]

            def link(ins_):
                links[0] += 1
                ins_.then_inc(pool_link, 1)
                pool.wait_ge(pool_link, links[0])

            if kind != "topk":
                for par in range(2):
                    kv = k_view(kind, par).bitcast(F32)
                    link(nc.gpsimd.memset(kv[R_MASK:R_ALL, :, :], ONE_BF16_TWICE))
                    link(nc.gpsimd.memset(kv[R_MASK:R_MASK + 1, :, :], 0.0))
            pool.drain().then_inc(init_done, 1)

            def value_ones(par):
                tiles = N // P if kind in ("self", "window") else 1
                link(nc.gpsimd.memset(v_ones[par][:, 0:tiles, :, HD:2 * HD], 1.0))
                if kind == "cross":
                    link(nc.gpsimd.memset(v_ones_rest[par], 0.0))
                    for j in range(HG):
                        link(nc.gpsimd.memset(v_ones_rest[par][32 * j:32 * j + SR, j, HD:2 * HD], 1.0))
                if kind == "topk":
                    link(nc.gpsimd.memset(v_ones_rest[par], 1.0))

            def copy_values(i, par, first):
                u = i * 2 + par
                if not first:
                    steps = 4 if kind == "topk" else EXP_STEPS[kind]
                    pool.wait_ge(pv_done, base(s, "pv") + (u - 1) * 2 * steps)
                if kind in ("self", "window"):
                    src = v_all[:, bass.ds(i, 1), :, par * 64:par * 64 + 64] if not isinstance(i, int) else v_all[:, i:i + 1, :, par * 64:par * 64 + 64]
                    nc.gpsimd.tensor_copy(v_ones[par][:, :, :, 0:HD], src.rearrange("p a t (j e) -> p (a t) j e", j=HG)).then_inc(v_ready, 1)
                    return
                flat = v_ctx[:, layer, :, :].rearrange("p b (k f) -> p (b k) f", k=KT)
                flat_rest = v_ctx_rest[:, layer, :, :].rearrange("p b (k f) -> p (b k) f", k=KT)
                at = bass.ds(i, 1) if not isinstance(i, int) else slice(i, i + 1)
                src = flat[:, at, par * 64:par * 64 + 64].rearrange("p a (j e) -> p (a j) e", j=HG)
                nc.gpsimd.tensor_copy(v_ones[par][:, 0, :, 0:HD], src).then_inc(v_ready, 1)
                pool.wait_ge(v_ready, v_base(s) + u * v_copies(kind) + 1)
                if kind == "cross":
                    src = flat_rest[:, at, par * 64:par * 64 + 64].rearrange("p a (j e) -> p (a j) e", j=HG)
                    nc.gpsimd.tensor_copy(v_ones_rest[par][:, :, 0:HD], src).then_inc(v_ready, 1)
                else:
                    plain = v_topk_rest[:, :, :].rearrange("p b (k f) -> p (b k) f", k=KT)
                    src = plain[:, at, par * 64:par * 64 + 64].rearrange("p a (j e) -> p (a j) e", j=HG)
                    nc.gpsimd.tensor_copy(v_ones_rest[par][0:32, :, 0:HD], src).then_inc(v_ready, 1)

            def subtract(i, q, k):
                n = (i * 4 + q) * 8 + k
                a = k % 2
                if not (isinstance(n, int) and n < 2):
                    pool.wait_ge(turn_full, base(s, "topk") * 8 + n - 1)
                pool.wait_ge(weight_ready, base(s, "topk") * 8 + n + 1)
                nc.gpsimd.tensor_tensor(tk_prob(a), tk_exp(a), tk_rest_exp(a), ALU.subtract).then_inc(prob_ready, 1)

            def body(i, first, last):
                for q in range(4):
                    if q == 0:
                        copy_values(i, 1, first)
                    if q == 2 and not last:
                        copy_values(i + 1, 0, False)
                    if kind == "topk":
                        for k in range(8):
                            subtract(i, q, k)

            value_ones(0)
            copy_values(0, 0, True)
            value_ones(1)
            assert links[0] == pool_links(s + 1)
            on_halves(pool, body)
            if s + 1 < stages:
                reorder_weights(pool, s + 1)

        def pool_links(s):
            return 4 + sum(2 * {"cross": 4 + HG, "topk": 2}.get(ATTENTION[a][0], 3) for a in range(s))

        def v_copies(kind):
            return {"self": 1, "window": 1, "cross": 2, "topk": 2}[kind]

        def v_base(s):
            return before(s, lambda a: HALVES // 2 * v_copies(a[0]))

        def tk(a, n):
            at = probs[a][:, :]
            return at[:, n * 2 * S:(n + 1) * 2 * S].rearrange("p (h s) -> p h s", h=2)

        def tk_left(a):
            return tk(a, 0)

        def tk_exp(a):
            return tk(a, 1)

        def tk_prob(a):
            return tk(a, 2)

        tk_rest_store = [v_ones[a][:, 1:8, :, :].rearrange("p t j e -> p (t j e)") for a in range(2)]

        def tk_rest_exp(a):
            return tk_rest_store[a][:, 0:2 * S].rearrange("p (h s) -> p h s", h=2)

        def turned_main(a):
            return probs[2 + a][:, 0:512].rearrange("p (j t) -> p j t", j=HG)

        def turned_last(a):
            return probs[2 + a][0:SR, 512:1024].rearrange("p (j t) -> p j t", j=HG)

        bias_rows_total = sum(n for _, n in BIASES)
        bias_dmas = len(BIASES) + sum(1 for i in range(1, 2) for j in range(1) if any(
            bias_column(n) < P < bias_column(n) + t for n, t in BIASES)) 

        def lin_wait(pe, n):
            if n >= len(LIN):
                pe.wait_ge(lin_free[n % len(LIN)], n // len(LIN))

        def pe_token(pe, s):
            st = TOKEN_STAGES[s]
            pe.wait_ge(w_loaded, 16 * weight_count[s + 1])
            for it in order.stages[s]:
                c, kind = it["c"], it["kind"]
                if kind in ("proj", "down"):
                    w = weight_at[it["spec"][1]]
                    if kind == "down":
                        pe.wait_ge(h_ready, FT * (it["h"] + 1))
                    for m in range(KT):
                        n = it["lin"] + m
                        lin_wait(pe, n)
                        ks = KT if kind == "proj" else FT
                        for k in range(ks):
                            if kind == "proj":
                                src = o_t[:, c // 2 * 2 + k, c % 2 * CW:(c % 2 + 1) * CW]
                            else:
                                src = h[it["h"] % 2][:, k, :]
                            last = nc.tensor.matmul(ps[:, n % 4, :], w[:, k, m * P:(m + 1) * P], src,
                                                    start=(k == 0), stop=(k == ks - 1))
                        last.then_inc(lin_full, 1)
                if kind == "residual":
                    pe.wait_ge(y_ready, KT * (it["y"] + 1))
                    if it["pair"]:
                        pe.wait_ge(pair_free, it["pair"])
                    for t in range(4):
                        for k in range(KT):
                            last = nc.tensor.transpose(ps[:, PS_PAIR + t // 2, (t % 2 * KT + k) * P:(t % 2 * KT + k + 1) * P],
                                                       y[it["y"] % 2][:, k, t * P:(t + 1) * P], ident[:, :])
                    last.then_inc(pair_full, 1)
                if kind == "spread":
                    n = it["lnt"]
                    pe.wait_ge(xn_ready, n + 1)
                    if n:
                        pe.wait_ge(xt_ready, KT * n)
                    for k in range(KT):
                        for t in range(4):
                            last = nc.tensor.transpose(ps[:, PS_SPREAD + k, t * P:(t + 1) * P],
                                                       xn[n % 2][:, t, k * P:(k + 1) * P], ident[:, :])
                    last.then_inc(spread_full, 1)
                if kind in ("up", "q", "qkv"):
                    w = weight_at[it["spec"][1]]
                    tiles = {"q": KT, "qkv": 2 * KT}.get(kind) or (FT * (2 if it["spec"][3] == "swiglu" else 1))
                    swiglu = kind == "up" and it["spec"][3] == "swiglu"
                    pe.wait_ge(xt_ready, KT * (it["xt"] + 1))
                    for m in range(tiles):
                        n = it["lin"] + m
                        lin_wait(pe, n)
                        mm = m // 2 + m % 2 * FT if swiglu else m
                        for k in range(KT):
                            last = nc.tensor.matmul(ps[:, n % 4, :], w[:, k, mm * P:(mm + 1) * P], xt[it["xt"] % 2][:, k, :],
                                                    start=(k == 0), stop=(k == KT - 1))
                        last.then_inc(lin_full, 1)
                    if kind == "qkv":
                        if it["pair"]:
                            pe.wait_ge(pair_free, it["pair"])
                        for t in range(4):
                            for k in range(KT):
                                last = nc.tensor.matmul(ps[:, PS_PAIR + t // 2, t % 2 * D:(t % 2 + 1) * D],
                                                        xt[it["xt"] % 2][:, k, t * P:(t + 1) * P], w[:, k, 2 * D:3 * D],
                                                        start=(k == 0), stop=(k == KT - 1))
                        last.then_inc(pair_full, 1)

        def pe_attention(pe, s):
            kind, layer, _ = ATTENTION[s]
            if kind == "topk":
                return pe_topk(pe, s)
            M, E = MAX_TILES[kind], EXP_STEPS[kind]
            mb, eb, pb, hb, rb, ub = (base(s, n) for n in ("max", "exp", "pv", "half", "maxrow", "unit"))
            out_bank = ps[:, PS_OUT, :]
            misc = ps[:, PS_MISC, :]
            misc_bf = misc.bitcast(BF16)

            def wait_last_rows():
                pe.wait_ge(init_done, s + 1)
                pe.wait_ge(q_ones_ready, 2 * before(s + 1, lambda a: a[0] != "topk"))

            def max_tile(i, q, k):
                p = i * 4 + q
                par = q // 2
                if k == 0 and q % 2 == 0:
                    pe.wait_ge(unit_loaded[par], base(s, "load") + (i + 1) * 16 * loads(ATTENTION[s]))
                n = p * M + k
                pe_wait_reuse(pe, max_done, mb, n, 2, i, q, k)
                dst = ps[:, PS_MAX + k % 2, :]
                if kind == "self":
                    t, j, kh = k // (2 * HG), k // 2 % HG, k % 2
                    qs = q_stack[par][0:R_MASK, q % 2, j, t * P:(t + 1) * P]
                    last = nc.tensor.matmul(dst, qs, k_view(kind, par)[0:R_MASK, j, kh * CW:(kh + 1) * CW], start=True, stop=True)
                elif kind == "cross":
                    t, jp = k // 2, k % 2
                    for a in range(2):
                        j = jp * 2 + a
                        qs = q_stack[par][0:R_MAX, q % 2, j, t * P:(t + 1) * P]
                        last = nc.tensor.matmul(dst[:, a * S:(a + 1) * S], qs, k_view(kind, par)[0:R_MAX, j, 0:S], start=True, stop=True)
                else:
                    at = q % 2 * CW + k * P
                    for j in range(HG):
                        last = nc.tensor.matmul(dst[:, j * P:(j + 1) * P], q_stack[par][0:R_MASK, q % 2, j, k * P:(k + 1) * P],
                                                k_view(kind, par)[0:R_MASK, j, at:at + P], start=True, stop=True)
                last.then_inc(max_full, 1)

            def turn_max(i, q):
                p = i * 4 + q
                pe.wait_ge(max_parts_ready, rb + p + 1)
                if not (isinstance(i, int) and i == 0 and q < 2):
                    pe.wait_ge(o_ready, hb + p - 1)
                nc.tensor.transpose(misc_bf[0:32, 0:P], max_parts[:, 0:32], ident_bf[:, :]).then_inc(rows_full, 1)

            def exp_step(i, q, e):
                p = i * 4 + q
                par = q // 2
                n = p * E + e
                slot = (q * E + e) % 2
                if e == 0:
                    pe.wait_ge(rows_loaded, 16 * (rb + p + 1))
                pe_wait_reuse(pe, exp_done, eb, n, 2, i, q, e, E)
                for a in range(2):
                    dst = ps[:, PS_EXP + slot * 2 + a, :]
                    if kind == "self":
                        kt, j = e // 2, e % 2 * 2 + a
                        last = nc.tensor.matmul(dst, k_view(kind, par)[0:R_ALL, j, kt * P:(kt + 1) * P],
                                                q_stack[par][0:R_ALL, q % 2, j, :], start=True, stop=True)
                    elif kind == "window":
                        at = q % 2 * CW + (e * 2 + a) * P
                        for j in range(HG):
                            last = nc.tensor.matmul(dst[:, j * P:(j + 1) * P], k_view(kind, par)[0:R_ALL, j, at:at + P],
                                                    q_stack[par][0:R_ALL, q % 2, j, at - q % 2 * CW:at - q % 2 * CW + P], start=True, stop=True)
                    elif e < 2:
                        j = e * 2 + a
                        last = nc.tensor.matmul(dst, k_view(kind, par)[0:R_ALL, j, 0:P],
                                                q_stack[par][0:R_ALL, q % 2, j, :], start=True, stop=True)
                    elif a == 0:
                        for j in range(HG):
                            last = nc.tensor.matmul(dst[32 * j:32 * j + 32, :], k_view(kind, par)[0:R_ALL, j, P:SP],
                                                    q_stack[par][0:R_ALL, q % 2, j, :], start=True, stop=True)
                last.then_inc(exp_full, 1)

            def pv_wait(i, q, e):
                p = i * 4 + q
                pe.wait_ge(exp_done, eb + p * E + e + 1)

            def pv_first(i, q):
                p = i * 4 + q
                if not (isinstance(i, int) and i == 0 and q == 0):
                    pe.wait_ge(raw_ready, hb + p)
                if q % 2 == 0:
                    pe.wait_ge(v_ready, v_base(s) + (i * 2 + q // 2 + 1) * v_copies(kind))

            def pv_step(i, q, e):
                par = q // 2
                if kind == "self":
                    if e % 2 == 0:
                        return
                    kt = e // 2
                    pv_wait(i, q, e)
                    if kt == 0:
                        pv_first(i, q)
                    for j in range(HG):
                        pr = probs[(q * E + e - 1 + j // 2) % NPR]
                        last = nc.tensor.matmul(out_bank[32 * j:32 * j + 32, :], v_ones[par][:, kt, j, :],
                                                pr[:, j % 2 * CW:(j % 2 + 1) * CW], start=(kt == 0), stop=(kt == N // P - 1))
                    last.then_inc(pv_done, 2)
                elif kind == "window":
                    pv_wait(i, q, e)
                    if e == 0:
                        pv_first(i, q)
                    pr = probs[(q * E + e) % NPR]
                    for a in range(2):
                        w = e * 2 + a
                        for j in range(HG):
                            last = nc.tensor.matmul(out_bank[32 * j:32 * j + 32, w * P:(w + 1) * P],
                                                    v_ones[par][:, q % 2 * 4 + w, j, :], pr[:, a * CW + j * P:a * CW + (j + 1) * P],
                                                    start=True, stop=True)
                    last.then_inc(pv_done, 1)
                else:
                    if e == 0:
                        return
                    pv_wait(i, q, e)
                    if e == 1:
                        pv_first(i, q)
                    for j in range(HG):
                        if e == 1:
                            pr = probs[(q * E + j // 2) % NPR][:, j % 2 * CW:(j % 2 + 1) * CW]
                            w = v_ones[par][:, 0, j, :]
                        else:
                            pr = probs[(q * E + 2) % NPR][:, 0:CW]
                            w = v_ones_rest[par][:, j, :]
                        last = nc.tensor.matmul(out_bank[32 * j:32 * j + 32, :], w, pr, start=(e == 1), stop=(e == 2))
                    last.then_inc(pv_done, 2 if e == 1 else 1)

            def before_half(i, q):
                return (i, q - 1) if q else (i - 1, 3)

            def after_half(i, q):
                return (i, q + 1) if q < 3 else (i + 1, 0)

            lead = {"self": 6, "cross": 2, "window": 1}[kind]
            lag = {"self": 3, "cross": 1, "window": 1}[kind]
            at_raw, at_norm = {"self": (2, 5), "cross": (0, 1), "window": (0, 1)}[kind]

            def half(i, q, first, last):
                first_half = first and q == 0
                last_half = last and q == 3
                k = 0
                if not last_half:
                    while k < lead:
                        max_tile(*after_half(i, q), k)
                        k += 1
                turn_max(i, q)
                for e in range(E + lag):
                    if not last_half:
                        until = lead + ((M - lead) * (e + 1)) // E
                        while k < min(until, M):
                            max_tile(*after_half(i, q), k)
                            k += 1
                    if e < E:
                        exp_step(i, q, e)
                    if e == at_raw and not first_half:
                        turn_raw(pe, s, *before_half(i, q), False)
                    if e == at_norm and not first_half:
                        turn_norm(pe, s, *before_half(i, q))
                    if e >= lag:
                        pv_step(i, q, e - lag)

            def body(i, first, last):
                for q in range(4):
                    half(i, q, first, last)

            if kind == "cross":
                wait_last_rows()
            for k in range(M):
                max_tile(0, 0, k)
            if kind != "cross":
                wait_last_rows()
            on_halves(pe, body)
            turn_raw(pe, s, HALVES // 4 - 1, 3, True)
            turn_norm(pe, s, HALVES // 4 - 1, 3)

        def pe_wait_reuse(pe, done, base_count, n, ring, i, q, k, per=None):
            if isinstance(n, int) and n < ring:
                return
            pe.wait_ge(done, base_count + n - ring + 1)

        def turn_raw(pe, s, i, q, last):
            hb, rb = base(s, "half"), base(s, "maxrow")
            p = i * 4 + q
            pe.wait_ge(raw_ready, hb + p + 1)
            if not last and ATTENTION[s][0] != "topk":
                pe.wait_ge(rows_ready, rb + p + 2)
            if not (isinstance(p, int) and p == 0):
                pe.wait_ge(o_ready, hb + p)
            for t in range(4):
                last_i = nc.tensor.transpose(ps[:, PS_MISC, t * P:(t + 1) * P], o_raw[:, t * P:(t + 1) * P], ident[:, :])
            last_i.then_inc(raw_t_full, 1)

        def turn_norm(pe, s, i, q):
            hb = base(s, "half")
            p = i * 4 + q
            pe.wait_ge(norm_ready, hb + p + 1)
            for a in range(2):
                last_i = nc.tensor.transpose(ps[:, PS_MISC, a * P:(a + 1) * P], o_norm[:, 2 * a:2 * a + 2, :], ident[:, :])
            last_i.then_inc(norm_t_full, 1)

        def pe_topk(pe, s):
            mb, hb, tb, pb = base(s, "max"), base(s, "half"), base(s, "topk"), base(s, "pv")

            def scores(i, q, k):
                p = i * 4 + q
                par = q // 2
                n = p * 8 + k
                if k == 0 and q % 2 == 0:
                    pe.wait_ge(unit_loaded[par], base(s, "load") + (i + 1) * 16 * loads(ATTENTION[s]))
                if not (isinstance(n, int) and n < 2):
                    pe.wait_ge(max_done, mb + n - 1)
                    pe.wait_ge(weight_ready, tb * 8 + n - 1)
                t, jp = k // 2, k % 2
                for a in range(2):
                    j = jp * 2 + a
                    qs = q_stack[par][0:R_MASK, q % 2, j, t * P:(t + 1) * P]
                    last = nc.tensor.matmul(ps[:, PS_MAX + k % 2, a * S:(a + 1) * S], qs, k_view("topk", par)[0:R_MASK, j, 0:S],
                                            start=True, stop=True)
                last.then_inc(max_full, 1)

            def turn(i, q, k):
                p = i * 4 + q
                n = p * 8 + k
                t, jp = k // 2, k % 2
                pe.wait_ge(prob_ready, tb * 8 + n + 1)
                if jp == 0:
                    m = p * 4 + t
                    if not (isinstance(m, int) and m < 2):
                        pe.wait_ge(turned, tb * 4 + m - 1)
                        pe.wait_ge(turned_rest, tb * 4 + m - 1)
                for a in range(2):
                    j = jp * 2 + a
                    pr = tk_prob(k % 2)[:, a, :]
                    nc.tensor.transpose(ps[:, PS_EXP + t % 2, j * P:(j + 1) * P], pr[:, 0:P], ident[:, :])
                    last = nc.tensor.transpose(ps[0:SR, PS_EXP + 2 + t % 2, j * P:(j + 1) * P], pr[:, P:S], ident[:, :])
                last.then_inc(turn_full, 1)

            def pv(i, q, t):
                p = i * 4 + q
                par = q // 2
                m = p * 4 + t
                pe.wait_ge(turned, tb * 4 + m + 1)
                pe.wait_ge(turned_rest, tb * 4 + m + 1)
                if t == 0:
                    if not (isinstance(i, int) and i == 0 and q == 0):
                        pe.wait_ge(raw_ready, hb + p)
                    if q % 2 == 0:
                        pe.wait_ge(v_ready, v_base(s) + (i * 2 + q // 2 + 1) * v_copies("topk"))
                for j in range(HG):
                    dst = ps[32 * j:32 * j + 32, PS_OUT, t * P:(t + 1) * P]
                    nc.tensor.matmul(dst, v_ones[par][:, 0, j, :], turned_main(t % 2)[:, j, :], start=True, stop=False)
                    last = nc.tensor.matmul(dst, v_ones_rest[par][0:SR, j, :], turned_last(t % 2)[:, j, :], start=False, stop=True)
                last.then_inc(pv_done, 1)

            def before_half(i, q):
                return (i, q - 1) if q else (i - 1, 3)

            def after_half(i, q):
                return (i, q + 1) if q < 3 else (i + 1, 0)

            def body(i, first, last):
                for q in range(4):
                    for k in range(8):
                        if k + 2 < 8:
                            scores(i, q, k + 2)
                        elif not (last and q == 3):
                            scores(*after_half(i, q), k + 2 - 8)
                        turn(i, q, k)
                        if k % 2 == 0 and k >= 2:
                            pv(i, q, k // 2 - 1)
                        if k == 2 and not (first and q == 0):
                            turn_raw(pe, s, *before_half(i, q), False)
                        if k == 4 and not (first and q == 0):
                            turn_norm(pe, s, *before_half(i, q))
                    pv(i, q, 3)

            scores(0, 0, 0)
            scores(0, 0, 1)
            on_halves(pe, body)
            turn_raw(pe, s, HALVES // 4 - 1, 3, True)
            turn_norm(pe, s, HALVES // 4 - 1, 3)

        HIS0 = KT * len(KV)

        def act_token(act, s):
            for it in order.stages[s]:
                c, kind = it["c"], it["kind"]
                b = c // 2
                if kind == "spread":
                    n = it["xt"]
                    act.wait_ge(spread_full, it["lnt"] + 1)
                    if n >= 2:
                        what, count = order.xt_last_product[n - 2]
                        act.wait_ge(lin_full if what == "lin" else pair_full, count)
                    _, scale, shift = it["spec"][1]
                    for k in range(KT):
                        src = ps[:, PS_SPREAD + k, :]
                        if scale:
                            nc.scalar.activation(xt[n % 2][:, k, :], src, ACT.Identity, bias=mod_col(shift, k, b),
                                                 scale=mod_col(scale, k, b)).then_inc(xt_ready, 1)
                        else:
                            nc.scalar.activation(xt[n % 2][:, k, :], src, ACT.Copy).then_inc(xt_ready, 1)
                if kind == "up":
                    _, _, bname, how = it["spec"]
                    hn = it["h"]
                    if hn >= 2 and how != "swiglu":
                        act.wait_ge(lin_full, order.h_last_product[hn - 2])
                    for m in range(FT):
                        if how == "swiglu":
                            n = it["lin"] + 2 * m
                            ab = it["ab"] + m
                            act.wait_ge(lin_full, n + 1)
                            if ab >= 2:
                                act.wait_ge(h_done, ab - 1)
                            nc.scalar.activation(gate_half[ab % 2], ps[:, n % 4, :], ACT.Silu, bias=bias_col(bname, m))\
                                .then_inc(lin_free[n % 4], 1)
                        else:
                            n = it["lin"] + m
                            act.wait_ge(lin_full, n + 1)
                            func = ACT.Gelu if how == "gelu" else ACT.Gelu_apprx_tanh
                            last = nc.scalar.activation(h[hn % 2][:, m, :], ps[:, n % 4, :], func, bias=bias_col(bname, m))
                            last.then_inc(lin_free[n % 4], 1)
                    if how != "swiglu":
                        act.drain().then_inc(h_ready, FT)
                if kind in ("q", "qkv"):
                    bname = it["spec"][2]
                    for m in range(KT * (2 if kind == "qkv" else 1)):
                        n, sn = it["lin"] + m, it["split"] + m
                        act.wait_ge(lin_full, n + 1)
                        if sn >= 2:
                            act.wait_ge(mid_ready, MIDS0 + sn - 1)
                        if sn >= 3:
                            act.wait_ge(parts_stored[sn % 3], 16 * (sn // 3))
                        nc.scalar.activation(x32[sn % 2], ps[:, n % 4, :], ACT.Identity, bias=bias_col_head_last(bname, m)).then_inc(hi_ready, 1)
                        nc.scalar.activation(split[sn % 3][:, 0, :], ps[:, n % 4, :], ACT.Identity, bias=bias_col_head_last(bname, m))\
                            .then_inc(lin_free[n % 4], 1)
                    if kind == "qkv":
                        act.wait_ge(pair_full, it["v"])
                        for k in range(KT):
                            src = ps[:, PS_PAIR:PS_PAIR + 2, :].rearrange("p a (t d) -> p (a t) d", t=2)[:, :, k * P:(k + 1) * P]
                            last = nc.scalar.activation(v_all[:, b * 2 + k, c % 2 * 4:c % 2 * 4 + 4, :], src, ACT.Copy)
                        last.then_inc(pair_free, 1)

        def act_o_copies(act, s):
            hb = base(s, "half")
            pv_per = {**EXP_STEPS, "topk": 4}[ATTENTION[s][0]]
            vb = ATTENTION[s][2]

            def raw(i, q):
                p = i * 4 + q
                act.wait_ge(pv_done, base(s, "pv") + (p + 1) * pv_per)
                if not (isinstance(p, int) and p == 0):
                    act.wait_ge(raw_t_full, hb + p)
                nc.scalar.activation(o_raw, ps[:, PS_OUT, :], ACT.Copy).then_inc(raw_ready, 1)

            def final(i, q):
                p = i * 4 + q
                par = q // 2
                act.wait_ge(norm_t_full, hb + p + 1)
                dyn = not isinstance(i, int)
                at = bass.ds(i, 1) if dyn else slice(i, i + 1)
                for r in range(2):
                    rows = slice(64 * r, 64 * r + 64)
                    bias = v_bias[rows, vb, at, par:par + 1].rearrange("p a c -> p (a c)")
                    dst = o_t[par * 64:par * 64 + 64, at, q % 2 * CW:(q % 2 + 1) * CW]
                    dst = dst.rearrange("p x (a r t) -> p (x a) r t", a=2, r=2)[:, :, r, :]
                    src = ps[rows, PS_MISC, 0:2 * P].rearrange("p (a t) -> p a t", a=2)
                    last = nc.scalar.activation(dst, src, ACT.Identity, bias=bias)
                last.then_inc(o_ready, 1)

            return raw, final

        def act_attention(act, s):
            kind = ATTENTION[s][0]
            raw, final = act_o_copies(act, s)
            if kind == "topk":
                return act_topk(act, s, raw, final)
            E = EXP_STEPS[kind]
            eb, pb, rb = base(s, "exp"), base(s, "pv"), base(s, "maxrow")
            at_raw, at_final = {"self": (0, 6), "cross": (0, 1), "window": (0, 1)}[kind]

            def rows(i, q):
                p = i * 4 + q
                act.wait_ge(rows_full, rb + p + 1)
                act.wait_ge(rows_loaded, 16 * (rb + p))
                nc.scalar.activation(max_rows[:, :], ps[:, PS_MISC, :].bitcast(BF16)[0:32, 0:P], ACT.Copy).then_inc(rows_ready, 1)

            def exp_step(i, q, e):
                n = (i * 4 + q) * E + e
                slot, ring = (q * E + e) % 2, (q * E + e) % NPR
                act.wait_ge(exp_full, eb + n + 1)
                if not (isinstance(n, int) and n < NPR):
                    act.wait_ge(pv_done, pb + n - NPR + 1)
                if kind == "cross" and e == 2:
                    dst, src = probs[ring][:, 0:CW], ps[:, PS_EXP + slot * 2, :]
                else:
                    dst = probs[ring].rearrange("p (a t) -> p a t", a=2)
                    src = ps[:, PS_EXP + slot * 2:PS_EXP + slot * 2 + 2, :]
                nc.scalar.activation(dst, src, ACT.Exp, scale=SCALE).then_inc(exp_done, 1)

            def body(i, first, last):
                for q in range(4):
                    rows(i, q)
                    before = (i, q - 1) if q else (i - 1, 3)
                    for e in range(E):
                        exp_step(i, q, e)
                        if e == at_raw and not (first and q == 0):
                            raw(*before)
                        if e == at_final and not (first and q == 0):
                            final(*before)

            on_halves(act, body)
            raw(HALVES // 4 - 1, 3)
            final(HALVES // 4 - 1, 3)

        def act_topk(act, s, raw, final):
            tb = base(s, "topk")

            def weights_of(i, q, k):
                n = (i * 4 + q) * 8 + k
                a = k % 2
                act.wait_ge(top_ready, tb * 16 + 2 * n + 1)
                nc.scalar.activation(neg_top[a], top1[a][:, :, 0], ACT.Copy, scale=-SCALE).then_inc(neg_top_ready, 1)
                act.wait_ge(neg_top_ready, tb * 8 + n + 1)
                if not (isinstance(n, int) and n < 2):
                    act.wait_ge(prob_ready, tb * 8 + n - 1)
                act.wait_ge(max_done, base(s, "max") + n + 1)
                for b in range(2):
                    nc.scalar.activation(tk_exp(a)[:, b, :], ps[:, PS_MAX + a, b * S:(b + 1) * S], ACT.Exp,
                                         bias=neg_top[a][:, b:b + 1], scale=SCALE)
                act.wait_ge(top_ready, tb * 16 + 2 * n + 2)
                for b in range(2):
                    last = nc.scalar.activation(tk_rest_exp(a)[:, b, :], tk_left(a)[:, b, :], ACT.Exp,
                                                bias=neg_top[a][:, b:b + 1], scale=SCALE)
                last.then_inc(weight_ready, 1)

            def turned_copy(i, q, t):
                p = i * 4 + q
                m = p * 4 + t
                act.wait_ge(turn_full, tb * 8 + 2 * (m + 1))
                if not (isinstance(m, int) and m < 2):
                    act.wait_ge(pv_done, base(s, "pv") + m - 1)
                nc.scalar.activation(turned_main(t % 2), ps[:, PS_EXP + t % 2, :].rearrange("p (j t) -> p j t", j=HG), ACT.Copy)\
                    .then_inc(turned, 1)

            def body(i, first, last):
                for q in range(4):
                    for k in range(8):
                        weights_of(i, q, k)
                        before = (i, q - 1) if q else (i - 1, 3)
                        if k == 2 and not (first and q == 0):
                            pass
                        if k % 2 == 0 and k >= 2:
                            turned_copy(i, q, k // 2 - 1)
                        if k == 0 and not (first and q == 0):
                            turned_copy(*before, 3)
                            raw(*before)
                        if k == 5 and not (first and q == 0):
                            final(*before)

            on_halves(act, body)
            last_half = (HALVES // 4 - 1, 3)
            turned_copy(*last_half, 3)
            raw(*last_half)
            final(*last_half)

        def dve_token(dve, s, link):
            if s == 0:
                dve.wait_ge(x_loaded, 16 * 3 * B)
            for it in order.stages[s]:
                c, kind = it["c"], it["kind"]
                b = c // 2
                if kind in ("proj", "down"):
                    _, _, bname, gate = it["spec"]
                    yn = it["y"]
                    if yn >= 2:
                        dve.wait_ge(pair_full, y_turned[yn - 2])
                    for m in range(KT):
                        n = it["lin"] + m
                        dve.wait_ge(lin_full, n + 1)
                        if gate:
                            ins_ = nc.vector.tensor_scalar(y[yn % 2][:, m, :], ps[:, n % 4, :], bias_col(bname, m),
                                                           mod_col(gate, m, b), ALU.add, ALU.mult)
                        else:
                            ins_ = nc.vector.tensor_scalar(y[yn % 2][:, m, :], ps[:, n % 4, :], bias_col(bname, m), None, ALU.add)
                        ins_.then_inc(lin_free[n % 4], 1)
                    dve.drain().then_inc(y_ready, KT)
                if kind == "up" and it["spec"][3] == "swiglu":
                    bname = it["spec"][2]
                    hn = it["h"]
                    if hn >= 2:
                        dve.wait_ge(lin_full, order.h_last_product[hn - 2])
                    for m in range(FT):
                        n, ab = it["lin"] + 2 * m + 1, it["ab"] + m
                        dve.wait_ge(lin_full, n + 1)
                        dve.wait_ge(lin_free[(n - 1) % 4], (n - 1) // 4 + 1)
                        ins_ = nc.vector.scalar_tensor_tensor(out=h[hn % 2][:, m, :], in0=ps[:, n % 4, :], scalar=bias_col(bname, FT + m),
                                                              in1=gate_half[ab % 2], op0=ALU.add, op1=ALU.mult)
                        ins_.then_inc(lin_free[n % 4], 1)
                        dve.wait_ge(lin_free[n % 4], n // 4 + 1)
                        dve.sem_inc(h_done, 1)
                    dve.drain().then_inc(h_ready, FT)
                if kind in ("residual", "norm"):
                    rows = x[:, c * 4:c * 4 + 4, :]
                    if kind == "residual":
                        dve.wait_ge(pair_full, it["pair"] + 1)
                        ins_ = nc.vector.tensor_tensor(rows, rows, ps[:, PS_PAIR:PS_PAIR + 2, :].rearrange("p a (t d) -> p (a t) d", t=2), ALU.add)
                        ins_.then_inc(pair_free, 1)
                        dve.wait_ge(pair_free, it["pair"] + 1)
                    if "store" in it:
                        dve.drain().then_inc(x_final, 1)
                    else:
                        n = it["ln"]
                        eps = it["spec"][1][0]
                        for t in range(4):
                            last = nc.vector.bn_stats(stats[n % 2][:, t, :], rows[:, t, :])
                        link(last)
                        for t in range(4):
                            last = nc.vector.bn_aggr(mv[n % 2][:, t, :], stats[n % 2][:, t, :])
                        link(last)
                        nc.vector.tensor_scalar_add(var_eps[n % 2], mv[n % 2][:, :, 1], eps).then_inc(var_ready, 1)
                        dve.wait_ge(rstd_ready, n + 1)
                        if n >= 2:
                            dve.wait_ge(spread_full, n - 1)
                        for t in range(4):
                            last = nc.vector.tensor_scalar(xn[n % 2][:, t, :], rows[:, t, :], mv[n % 2][:, t, 0:1], rstd[n % 2][:, t:t + 1],
                                                           ALU.subtract, ALU.mult)
                        last.then_inc(xn_ready, 1)
                if kind in ("q", "qkv"):
                    for m in range(KT * (2 if kind == "qkv" else 1)):
                        n, sn = it["lin"] + m, it["split"] + m
                        dve.wait_ge(lin_free[n % 4], n // 4 + 1)
                        if sn >= 2:
                            dve.wait_ge(lo_ready, sn - 1)
                        link(nc.vector.tensor_tensor(xrest[sn % 2], x32[sn % 2], split[sn % 3][:, 0, :], ALU.subtract))
                        nc.vector.tensor_copy(split[sn % 3][:, 1, :], xrest[sn % 2]).then_inc(mid_ready, 1)

        y_turned = {}
        for st_items in order.stages:
            for it in st_items:
                if it["kind"] == "residual":
                    y_turned[it["y"]] = it["pair"] + 1

        def dve_normalise(dve, s):
            hb = base(s, "half")

            def normalise(i, q):
                p = i * 4 + q
                dve.wait_ge(raw_t_full, hb + p + 1)
                if not (isinstance(p, int) and p == 0):
                    dve.wait_ge(norm_t_full, hb + p)
                both = ps[:, PS_MISC, :].rearrange("p (c e) -> p c e", e=2 * HD)
                nc.vector.reciprocal(o_rsum, both[:, :, HD]).then_inc(rsum_ready, 1)
                dve.wait_ge(rsum_ready, hb + p + 1)
                nc.vector.tensor_tensor(o_norm.rearrange("p t (j e) -> p (t j) e", j=HG), both[:, :, 0:HD],
                                        o_rsum.unsqueeze(2).to_broadcast([P, 4 * HG, HD]), ALU.mult).then_inc(norm_ready, 1)

            return normalise

        def dve_attention(dve, s):
            kind = ATTENTION[s][0]
            normalise = dve_normalise(dve, s)
            if kind == "topk":
                return dve_topk(dve, s, normalise)
            M, E = MAX_TILES[kind], EXP_STEPS[kind]
            mb, rb = base(s, "max"), base(s, "maxrow")

            def reduce_tile(i, q, k):
                n = (i * 4 + q) * M + k
                if kind != "self" and k == 0 and not (isinstance(i, int) and i == 0 and q == 0):
                    dve.wait_ge(max_parts_ready, rb + i * 4 + q)
                dve.wait_ge(max_full, mb + n + 1)
                src = ps[:, PS_MAX + k % 2, :]
                if kind == "self":
                    t, j, kh = k // (2 * HG), k // 2 % HG, k % 2
                    dst = row_max.rearrange("p (j t h) -> p j t h", j=HG, t=4)[:, j, t, kh:kh + 1]
                    ins_ = nc.vector.tensor_reduce(dst, src, AX.X, ALU.max)
                elif kind == "cross":
                    t, jp = k // 2, k % 2
                    dst = neg_max.rearrange("p (j t) -> p j t", j=HG)[:, jp * 2:jp * 2 + 2, t]
                    ins_ = nc.vector.tensor_reduce(dst, src[:, 0:2 * S].rearrange("p (a s) -> p a s", a=2), AX.X, ALU.max, negate=True)
                else:
                    dst = neg_max.rearrange("p (j t) -> p j t", j=HG)[:, :, k]
                    ins_ = nc.vector.tensor_reduce(dst, src.rearrange("p (j s) -> p j s", j=HG), AX.X, ALU.max, negate=True)
                ins_.then_inc(max_done, 1)

            def parts(i, q):
                p = i * 4 + q
                ln_ = links_before(s) + p * links_per(kind)
                dve.wait_ge(max_done, mb + (p + 1) * M)
                step = 0
                if kind == "self":
                    nc.vector.tensor_reduce(neg_max, row_max.rearrange("p (c h) -> p c h", h=2), AX.X, ALU.max, negate=True)\
                        .then_inc(masked_ready, 1)
                    step += 1
                    dve.wait_ge(masked_ready, ln_ + step)
                if not (isinstance(p, int) and p == 0):
                    dve.wait_ge(rows_full, rb + p)
                nc.vector.tensor_copy(max_parts[:, 0:16], neg_max).then_inc(masked_ready, 1)
                step += 1
                dve.wait_ge(masked_ready, ln_ + step)
                nc.vector.tensor_tensor(max_parts[:, 16:32], neg_max, max_parts[:, 0:16], ALU.subtract).then_inc(max_parts_ready, 1)

            lead = {"self": 6, "cross": 2, "window": 1}[kind]
            at_raw = {"self": 2, "cross": 0, "window": 0}[kind]
            norm_at = min(M, lead + ((M - lead) * (at_raw + 1)) // E)

            def body(i, first, last):
                for q in range(4):
                    nxt = (i, q + 1) if q < 3 else (i + 1, 0)
                    before = (i, q - 1) if q else (i - 1, 3)
                    last_half = last and q == 3
                    for k in range(M + 1):
                        if k == norm_at and not (first and q == 0):
                            normalise(*before)
                        if k < M and not last_half:
                            reduce_tile(*nxt, k)
                    if not last_half:
                        parts(*nxt)

            for par in range(2):
                row = q_stack[par].rearrange("p a j t -> p (a j t)").bitcast(F32)[R_MASK:R_MASK + 1, :]
                nc.vector.memset(row, ONE_BF16_TWICE).then_inc(q_ones_ready, 1)
            for k in range(M):
                reduce_tile(0, 0, k)
            parts(0, 0)
            on_halves(dve, body)
            normalise(HALVES // 4 - 1, 3)

        def links_per(kind):
            return {"self": 2, "cross": 1, "window": 1, "topk": 0}[kind]

        def links_before(s):
            return before(s, lambda a: HALVES * links_per(a[0]))

        def dve_topk(dve, s, normalise):
            mb, tb = base(s, "max"), base(s, "topk")
            lk = 1000

            def strike(i, q, k):
                n = (i * 4 + q) * 8 + k
                a = k % 2
                first_use = isinstance(n, int) and n < 2
                at = tb * 48 + n * 6
                scores = [ps[:, PS_MAX + a, b * S:(b + 1) * S] for b in range(2)]
                left = [tk_left(a)[:, b, :] for b in range(2)]

                def hold(sem_, value):
                    dve.wait_ge(sem_, value)
                    dve.sem_inc(topk_hold, 1)

                if not first_use:
                    hold(weight_ready, tb * 8 + n - 1)
                hold(max_full, mb + n + 1)
                nc.vector.max(top1[a][:, 0, :], scores[0]).then_inc(topk_link, 1)
                nc.vector.max(top1[a][:, 1, :], scores[1]).then_inc(top_ready, 1)
                hold(topk_link, at + 1)
                nc.vector.match_replace(left[0], top1[a][:, 0, :], scores[0], BIG).then_inc(topk_link, 1)
                hold(top_ready, tb * 16 + 2 * n + 1)
                nc.vector.match_replace(left[1], top1[a][:, 1, :], scores[1], BIG).then_inc(max_done, 1)
                hold(topk_link, at + 2)
                nc.vector.max(top2[a][:, 0, :], left[0]).then_inc(topk_link, 1)
                hold(max_done, mb + n + 1)
                nc.vector.max(top2[a][:, 1, :], left[1]).then_inc(topk_link, 1)
                hold(topk_link, at + 3)
                nc.vector.match_replace(left[0], top2[a][:, 0, :], left[0], BIG).then_inc(topk_link, 1)
                hold(topk_link, at + 4)
                nc.vector.match_replace(left[1], top2[a][:, 1, :], left[1], BIG).then_inc(topk_link, 1)
                dve.wait_ge(topk_link, at + 6)
                dve.sem_inc(top_ready, 1)

            def rest_copy(i, q, t):
                m = (i * 4 + q) * 4 + t
                dve.wait_ge(turn_full, tb * 8 + 2 * (m + 1))
                if not (isinstance(m, int) and m < 2):
                    dve.wait_ge(pv_done, base(s, "pv") + m - 1)
                nc.vector.tensor_copy(turned_last(t % 2), ps[0:SR, PS_EXP + 2 + t % 2, :].rearrange("p (j t) -> p j t", j=HG))\
                    .then_inc(turned_rest, 1)

            def body(i, first, last):
                for q in range(4):
                    before = (i, q - 1) if q else (i - 1, 3)
                    for k in range(8):
                        strike(i, q, k)
                        if k % 2 == 1 and k >= 3:
                            rest_copy(i, q, k // 2 - 1)
                        if k == 1 and not (first and q == 0):
                            rest_copy(*before, 3)
                        if k == 4 and not (first and q == 0):
                            normalise(*before)

            on_halves(dve, body)
            rest_copy(HALVES // 4 - 1, 3, 3)
            normalise(HALVES // 4 - 1, 3)


        block = ctx.enter_context(nc.Block())

        @block.sync
        def _(sp):
            for b in range(B):
                for k in range(KT):
                    sp.dma_start(cond_t[:, k, b:b + 1], ins["cond_1024"][b, k * P:(k + 1) * P].rearrange("(p a) -> p a", a=1))\
                        .then_inc(cond_loaded, 16)
            row = 0
            for name, tiles in BIASES:
                src = ins[name].rearrange("(m p) -> m p", p=P)
                done = 0
                while done < tiles:
                    n = min(tiles - done, P - row % P)
                    sp.dma_start(bias_rows[row % P:row % P + n, row // P, :], src[done:done + n, :]).then_inc(bias_loaded, 16)
                    row += n
                    done += n
            at = 0
            for name, tiles in ADA:
                sp.dma_start(ada_w[:, :, at:at + tiles * P], ins[name].rearrange("(k p) n -> p k n", p=P)).then_inc(ada_loaded, 16)
                at += tiles * P
            for b in range(B):
                sp.dma_start(ctx_tok[:, 2 * b, :], ins["ctx_1024"][b, 0:P, :]).then_inc(ctx_loaded, 16)
                sp.dma_start(ctx_tok[0:SR, 2 * b + 1, :], ins["ctx_1024"][b, P:S, :]).then_inc(ctx_loaded, 16)
                sp.dma_start(ctx_tok[SR:32, 2 * b + 1, :], ins["ctx_1024"][b, S - (SP - S):S, :]).then_inc(ctx_loaded, 16)
                sp.dma_start(mask_u8[:, b, 0:S], ins["mask_BxS2_bf0"][b:b + 1, :]).then_inc(mask_loaded, 16)
                sp.dma_start(mask_u8[:, b, S:SP], ins["mask_BxS2_bf0"][b:b + 1, S - (SP - S):S]).then_inc(mask_loaded, 16)
            for l, (w, _) in enumerate(KV):
                sp.dma_start(weights[1][:, l * KT * 2 * D:(l + 1) * KT * 2 * D].rearrange("p (k n) -> p k n", k=KT),
                             ins[w].rearrange("(k p) n -> p k n", p=P)).then_inc(kv_loaded, 16)
            for b in range(B):
                for src, parts, tiles in x_rows(ins["x"], b):
                    dst = x[parts, b * (N // P) + tiles.start:b * (N // P) + tiles.stop, :]
                    sp.dma_start(dst, src if tiles.stop - tiles.start > 1 else src.unsqueeze(1)).then_inc(x_loaded, 16)
            load_weights(sp, 0)
            for l in range(len(KV)):
                for m in range(KT):
                    n = l * KT + m
                    sp.wait_ge(pre_pool, 3 + n + 1)
                    for b in range(B):
                        sp.dma_start(kc_parts[l * 4 + b * 2 + m, :, :, :].rearrange("a p s -> p a s"),
                                     kc_split[n % 4][:, :, b * SP:(b + 1) * SP]).then_inc(kc_stored[n % 4], 16)
            sp.wait_ge(pre_act, 2 * len(KV) * B)
            for j in range(HG):
                def heads(ap):
                    return ap.rearrange("p l b (g j e) -> p (l b g) j e", g=H // HG, j=HG)[:, :, j, :]
                sp.dma_start(heads(v_ctx_rest[32 * j:32 * j + SR, :, :, :]), heads(v_rest[0:SR, :, :, :])).then_inc(pre_dma, 16)
            sp.dma_start(v_topk_rest[:, :, :], v_rest[:, 1, :, :]).then_inc(pre_dma, 16)
            for r in range(4):
                sp.wait_ge(kc_stored[r], 16 * B * (KT * len(KV) // 4))
            sp.wait_ge(pre_dma, 16 * (HG + 1))
            leave_stage(sp, "sp")

            for kind, s, number in stage_sequence():
                enter_stage(sp, "sp", number)
                if kind == "token":
                    sp_token(sp, s)
                else:
                    if s + 1 < stages:
                        load_weights(sp, s + 1)
                    sp_attention(sp, s)
                leave_stage(sp, "sp")
            if stages < len(TOKEN_STAGES):
                enter_stage(sp, "sp", number + 1)
                for c in range(CH):
                    store_chunk(sp, c)
                sp.wait_ge(out_stored, 16 * stored[0])

        @block.gpsimd
        def _(pool):
            nc.gpsimd.memset(ident[:, :], 0.0).then_inc(pool_link, 1)
            nc.gpsimd.memset(minus_half[:, :], -0.5).then_inc(pool_link, 1)
            nc.gpsimd.memset(v_ctx_rest[:, :, :, :], 0.0).then_inc(pool_link, 1)
            pool.wait_ge(pool_link, 3)
            nc.gpsimd.affine_select(out=ident[:, :], in_=ident[:, :], compare_op=ALU.not_equal, fill=1.0, base=0,
                                    pattern=[[-1, P]], channel_multiplier=1).then_inc(pool_link, 1)
            pool.wait_ge(pool_link, 4)
            nc.gpsimd.tensor_copy(ident_bf[:, :], ident[:, :]).then_inc(pre_pool, 1)
            pool.wait_ge(pre_dve, 1)
            for e in range(2):
                nc.gpsimd.tensor_tensor(ctx_rstd[:, e, :], ctx_eps[:, e, :], minus_half[:, :], ALU.pow).then_inc(pre_pool, 1)
            pool.wait_ge(kv_loaded, 16 * len(KV))
            for l in range(len(KV)):
                for k in range(KT):
                    at = (l * KT + k) * 2 * D
                    columns_head_last(pool, weights[1][:, at:at + D])
            pool.sem_inc(kv_reordered, 1)
            for n in range(KT * len(KV)):
                pool.wait_ge(mid_ready, n + 1)
                if n >= 4:
                    pool.wait_ge(kc_stored[n % 4], 16 * B * (n // 4))
                nc.gpsimd.tensor_tensor(kc_split[n % 4][:, 2, :], kc_rest[n % 2], kc_split[n % 4][:, 1, :], ALU.subtract)\
                    .then_inc(pre_pool, 1)
            reorder_weights(pool, 0)
            leave_stage(pool, "pool")
            for kind, s, number in stage_sequence():
                enter_stage(pool, "pool", number)
                (pool_token if kind == "token" else pool_attention)(pool, s)
                leave_stage(pool, "pool")

        @block.tensor
        def _(pe):
            pe.wait_ge(pre_pool, 1)
            pe.wait_ge(bias_loaded, 16 * bias_dmas)
            pe.wait_ge(bias_reordered, 2)
            last = None
            for r in range(2):
                rows = P if r == 0 else bias_rows_total - P
                nc.tensor.transpose(ps[:, 0, r * P:r * P + rows], bias_rows[0:rows, r, :], ident[0:rows, 0:rows])
                last = nc.tensor.transpose(ps[:, 0, (2 + r) * P:(2 + r) * P + rows], bias_rows_hl[0:rows, r, :], ident[0:rows, 0:rows])
            last.then_inc(pre_pe, 1)
            pe.wait_ge(ada_loaded, 16 * len(ADA))
            pe.wait_ge(act_link, 1)
            for m in range(MT):
                for k in range(KT):
                    last = nc.tensor.matmul(ps[:, 1, m * B:(m + 1) * B], ada_w[:, k, m * P:(m + 1) * P], cond_silu[:, k, :],
                                            start=(k == 0), stop=(k == KT - 1))
            last.then_inc(pre_pe, 1)
            for e in range(3):
                if e == 0:
                    pe.wait_ge(ctx_loaded, 16 * 3 * B)
                else:
                    pe.wait_ge(pre_dve, 1 + e * 2 * B)
                for k in range(KT):
                    for t in range(2 * B):
                        n = P if t % 2 == 0 else 32
                        at = t // 2 * SP + t % 2 * P
                        src = ctx_tok[0:n, t, k * P:(k + 1) * P] if e == 0 else ctx_norm[0:n, e - 1, t, k * P:(k + 1) * P]
                        last = nc.tensor.transpose(ps[:, 2 + (e * KT + k) % 6, at:at + n], src, ident[0:n, 0:n])
                    last.then_inc(pre_pe, 1)
            pe.wait_ge(kv_loaded, 16 * len(KV))
            pe.wait_ge(kv_reordered, 1)
            for l in range(len(KV)):
                w = weights[1][:, l * KT * 2 * D:(l + 1) * KT * 2 * D].rearrange("p (k n) -> p k n", k=KT)
                for m in range(KT):
                    n = l * KT + m
                    if n == 0:
                        pe.wait_ge(act_link, 1 + 3 * KT)
                        pe.wait_ge(pre_dve, 1 + 4 * B + 2 + 1)
                    if n >= 2:
                        pe.wait_ge(hi_ready, n - 1)
                    for k in range(KT):
                        last = nc.tensor.matmul(ps[:, n % 2, 0:B * SP], w[:, k, m * P:(m + 1) * P], ctx_t[:, KV_CTX[l], k, :],
                                                start=(k == 0), stop=(k == KT - 1))
                    last.then_inc(pre_pe, 1)
                for b in range(B):
                    for t in range(2):
                        n = (l * B + b) * 2 + t
                        if n >= 2:
                            pe.wait_ge(pre_act, n - 1)
                        rows = P if t == 0 else 32
                        for k in range(KT):
                            last = nc.tensor.matmul(ps[0:rows, 2 + n % 2, 0:D], ctx_t[:, KV_CTX[l], k, b * SP + t * P:b * SP + t * P + rows],
                                                    w[:, k, D:2 * D], start=(k == 0), stop=(k == KT - 1))
                        last.then_inc(pre_pe, 1)
            leave_stage(pe, "pe")
            for kind, s, number in stage_sequence():
                enter_stage(pe, "pe", number)
                (pe_token if kind == "token" else pe_attention)(pe, s)
                leave_stage(pe, "pe")

        @block.scalar
        def _(act):
            act.wait_ge(cond_loaded, 16 * KT * B)
            nc.scalar.activation(cond_silu, cond_t, ACT.Silu).then_inc(act_link, 1)
            for e in range(3):
                for k in range(KT):
                    act.wait_ge(pre_pe, 2 + e * KT + k + 1)
                    if e == 1 and k == 0:
                        act.wait_ge(pre_dve, 1 + 4 * B + 2 + 1)
                    src = ps[:, 2 + (e * KT + k) % 6, 0:B * SP]
                    if e == 1:
                        for b in range(B):
                            last = nc.scalar.activation(ctx_t[:, e, k, b * SP:(b + 1) * SP], src[:, b * SP:(b + 1) * SP], ACT.Identity,
                                                        bias=mod_col(("L2kv", 2), k, b), scale=mod_col(("L2kv", 0), k, b))
                        last.then_inc(act_link, 1)
                    else:
                        nc.scalar.activation(ctx_t[:, e, k, :], src, ACT.Copy).then_inc(act_link, 1)
            for l, (_, bname) in enumerate(KV):
                for m in range(KT):
                    n = l * KT + m
                    act.wait_ge(pre_pe, 2 + 3 * KT + l * (KT + 2 * B) + m + 1)
                    if n >= 2:
                        act.wait_ge(mid_ready, n - 1)
                    if n >= 4:
                        act.wait_ge(kc_stored[n % 4], 16 * B * (n // 4))
                    src = ps[:, n % 2, 0:B * SP]
                    nc.scalar.activation(kc32[n % 2], src, ACT.Identity, bias=bias_col_head_last(bname, m))
                    nc.scalar.activation(kc_split[n % 4][:, 0, :], src, ACT.Identity, bias=bias_col_head_last(bname, m)).then_inc(hi_ready, 1)
                for b in range(B):
                    for t in range(2):
                        n = (l * B + b) * 2 + t
                        act.wait_ge(pre_pe, 2 + 3 * KT + l * (KT + 2 * B) + KT + b * 2 + t + 1)
                        if t == 0:
                            nc.scalar.activation(v_ctx[:, l, b, :], ps[:, 2 + n % 2, 0:D], ACT.Copy).then_inc(pre_act, 1)
                        else:
                            nc.scalar.activation(v_rest[:, l, b, :], ps[0:32, 2 + n % 2, 0:D], ACT.Copy).then_inc(pre_act, 1)
            leave_stage(act, "act")
            for kind, s, number in stage_sequence():
                enter_stage(act, "act", number)
                (act_token if kind == "token" else act_attention)(act, s)
                leave_stage(act, "act")

        @block.vector
        def _(dve):
            links = [0]

            def link(ins_):
                links[0] += 1
                ins_.then_inc(dve_link, 1)
                dve.wait_ge(dve_link, links[0])

            dve.wait_ge(bias_loaded, 16 * bias_dmas)
            for r in range(2):
                rows = P if r == 0 else bias_rows_total - P
                dst = bias_rows_hl[0:rows, r, :].rearrange("p (g d j) -> p g d j", j=HG, d=HD)
                nc.vector.tensor_copy(dst, head_last(bias_rows[0:rows, r, :])).then_inc(bias_reordered, 1)
            link(nc.vector.memset(ctx_mv, 1.0))
            dve.wait_ge(ctx_loaded, 16 * 3 * B)
            for t in range(2 * B):
                n = P if t % 2 == 0 else 32
                last = nc.vector.bn_stats(ctx_stats[0:n, t, :], ctx_tok[0:n, t, :])
            link(last)
            for t in range(2 * B):
                n = P if t % 2 == 0 else 32
                last = nc.vector.bn_aggr(ctx_mv[0:n, t, :], ctx_stats[0:n, t, :])
            link(last)
            for e, eps in enumerate((1e-5, 1e-6)):
                last = nc.vector.tensor_scalar_add(ctx_eps[:, e, :], ctx_mv[:, :, 1], eps)
            last.then_inc(pre_dve, 1)
            dve.wait_ge(pre_pool, 3)
            for e in range(2):
                for t in range(2 * B):
                    n = P if t % 2 == 0 else 32
                    nc.vector.tensor_scalar(ctx_norm[0:n, e, t, :], ctx_tok[0:n, t, :], ctx_mv[0:n, t, 0:1], ctx_rstd[0:n, e, t:t + 1],
                                            ALU.subtract, ALU.mult).then_inc(pre_dve, 1)
            dve.wait_ge(pre_pe, 1)
            nc.vector.tensor_copy(bias_cols_hl[:, 0:bias_rows_total], ps[:, 0, 2 * P:2 * P + bias_rows_total])
            link(nc.vector.tensor_copy(bias_cols[:, 0:bias_rows_total], ps[:, 0, 0:bias_rows_total]))
            for n, (name, at) in enumerate(V_BIAS):
                c = bias_column(name, at // P)
                for r in range(2):
                    for g in range(2):
                        nc.vector.tensor_copy(v_bias[64 * r:64 * r + 64, n, :, g].rearrange("p (b k) -> p b k", b=B),
                                              bias_cols[64 * g:64 * g + 64, c:c + KT].unsqueeze(1).to_broadcast([64, B, KT]))
            dve.wait_ge(pre_pe, 2)
            for b in range(B):
                last = nc.vector.tensor_tensor(mod[:, :, b], ps[:, 1, 0:MT * B].rearrange("p (m b) -> p m b", b=B)[:, :, b],
                                               bias_cols[:, 0:MT], ALU.add)
                last.then_inc(pre_dve, 1)
                links[0] += 0
            dve.wait_ge(pre_dve, 1 + 4 * B + 2)
            for which, tile in SCALE_TILES:
                at = MOD0[which] + tile
                last = nc.vector.tensor_scalar_add(mod[:, at:at + KT, :], mod[:, at:at + KT, :], 1.0)
            last.then_inc(pre_dve, 1)
            dve.wait_ge(mask_loaded, 16 * 2 * B)
            link(nc.vector.tensor_copy(mask_f, mask_u8))
            link(nc.vector.tensor_scalar(mask_f, mask_f, 0.0, None, ALU.not_equal))
            link(nc.vector.tensor_scalar(mask_row[:, :, :], mask_f, BIG, 10.0, ALU.mult, ALU.mult))
            for i in range(2 * B):
                last = nc.vector.tensor_copy(mask_by_turn[:, i, :], mask_row[:, i // 2, :])
            link(last)
            for n in range(KT * len(KV)):
                dve.wait_ge(hi_ready, n + 1)
                if n >= 2:
                    dve.wait_ge(pre_pool, 3 + n - 1)
                link(nc.vector.tensor_tensor(kc_rest[n % 2], kc32[n % 2], kc_split[n % 4][:, 0, :], ALU.subtract))
                nc.vector.tensor_copy(kc_split[n % 4][:, 1, :], kc_rest[n % 2]).then_inc(mid_ready, 1)
            leave_stage(dve, "dve")
            for kind, s, number in stage_sequence():
                enter_stage(dve, "dve", number)
                if kind == "token":
                    dve_token(dve, s, link)
                else:
                    dve_attention(dve, s)
                leave_stage(dve, "dve")


INPUTS = (["x", "cond_1024", "ctx_1024", "mask_BxS2_bf0"] + [n for n, _ in BIASES] + [n for n, _ in ADA] + [w for w, _ in KV]
          + [n for st in TOKEN_STAGES for n in ([st["proj"][0]] if st["proj"] else [])
             + ([st["mlp"][0], st["mlp"][3]] if st["mlp"] else []) + ([st["out"][1]] if st["out"] else [])])


def kernel(**inputs):
    import concourse.bacc as bacc
    from concourse.bass_utils import run_bass_kernel_spmd

    nc = bacc.Bacc("TRN2", target_bir_lowering=False, num_devices=1)
    arrays, ins = {}, {}
    for name in INPUTS:
        a = np.ascontiguousarray(inputs[name])
        arrays["in_" + name] = a
        ins[name] = nc.dram_tensor("in_" + name, a.shape, mybir.dt.from_np(a.dtype), kind="ExternalInput").ap()
    out = nc.dram_tensor("out", (B, N, D), F32, kind="ExternalOutput").ap()
    build_program(nc, ins, out, len(TOKEN_STAGES))
    return run_bass_kernel_spmd(nc, [arrays], core_ids=[0]).results[0]["out"]
```

```python
from contextlib import ExitStack

import numpy as np

import concourse.bass as bass
from concourse import mybir

F32 = mybir.dt.float32
BF16 = mybir.dt.bfloat16
U8 = mybir.dt.uint8
ACT = mybir.ActivationFunctionType
ALU = mybir.AluOpType
AX = mybir.AxisListType

P = 128
B, N, D, H, HD = 2, 1024, 256, 16, 16
S, SP = 154, 160
SR = S - P
SHIFT = 64
KT = D // P
TOK = B * N
CW = 512
CH = TOK // CW
DF = 1024
FT = DF // P
SCALE = HD ** -0.5
BIG = -3.0e38
HG = 4
PARTS = 3
PAIRS = 6
QPART = (0, 0, 0, 1, 1, 2)
KPART = (0, 1, 2, 0, 1, 0)
Q_RUNS = ((0, 0, 3), (3, 1, 2), (5, 2, 1))
K_RUNS = ((0, 3), (3, 2), (5, 1))
ONE_BF16_TWICE = float(np.array([0x3F803F80], np.uint32).view(np.float32)[0])
R_MASK = PAIRS * HD
R_MAX = R_MASK + 1
R_ALL = R_MAX + 2

BIASES = [("L0_xcond_ada_b", 12), ("L1_xcond_b_ada", 18), ("L2_xcond_bss_q", 4), ("L2_xcond_bss_kv", 4),
          ("L3_xcond_b_mod", 12),
          ("L0_xcond_qkv_b", 6), ("L0_xcond_sa_proj_b", 2), ("L0_xcond_q_b", 2), ("L0_xcond_kv_b", 4),
          ("L0_xcond_ca_proj_b", 2), ("L0_xcond_fc1_b", 8), ("L0_xcond_fc2_b", 2),
          ("L1_xcond_b_qkv", 6), ("L1_xcond_b_so", 2), ("L1_xcond_b_q", 2), ("L1_xcond_b_kv", 4),
          ("L1_xcond_b_co", 2), ("L1_xcond_b_m1", 16), ("L1_xcond_b_m2", 2),
          ("L2_xcond_bq", 2), ("L2_xcond_bkv", 4), ("L2_xcond_bp", 2),
          ("L3_xcond_b_qkv", 6), ("L3_xcond_b_proj", 2), ("L3_xcond_b_qc", 2), ("L3_xcond_b_kvc", 4),
          ("L3_xcond_b_cproj", 2), ("L3_xcond_b_mlp1", 8), ("L3_xcond_b_mlp2", 2)]
ADA = [("L0_xcond_ada_w", 12), ("L1_xcond_w_ada", 18), ("L2_xcond_Wss_q", 4), ("L2_xcond_Wss_kv", 4),
       ("L3_xcond_W_mod", 12)]
MT = sum(n for _, n in ADA)
MOD0 = {"L0": 0, "L1": 12, "L2q": 30, "L2kv": 34, "L3": 38}
SCALE_TILES = [("L0", 2), ("L0", 8), ("L1", 2), ("L1", 8), ("L1", 14), ("L2q", 0), ("L2kv", 0), ("L3", 2), ("L3", 8)]
KV = [("L0_xcond_kv_w", "L0_xcond_kv_b"), ("L1_xcond_w_kv", "L1_xcond_b_kv"), ("L2_xcond_Wkv", "L2_xcond_bkv"),
      ("L3_xcond_W_kvc", "L3_xcond_b_kvc")]
KV_CTX = (0, 0, 1, 2)
V_BIAS = [("L0_xcond_qkv_b", 512), ("L0_xcond_kv_b", 256), ("L1_xcond_b_qkv", 512), ("L1_xcond_b_kv", 256),
          ("L2_xcond_bkv", 256), ("L3_xcond_b_qkv", 512), ("L3_xcond_b_kvc", 256)]


def bias_column(name, tile=0):
    at = 0
    for n, tiles in BIASES:
        if n == name:
            return at + tile
        at += tiles
    raise KeyError(name)


TOKEN_STAGES = [
    dict(proj=None, ln=(1e-6, ("L0", 2), ("L0", 0)), mlp=None, ln2=None, out=("qkv", "L0_xcond_qkv_w", "L0_xcond_qkv_b")),
    dict(proj=("L0_xcond_sa_proj_w", "L0_xcond_sa_proj_b", ("L0", 4)), ln=(1e-6, None, None), mlp=None, ln2=None,
         out=("q", "L0_xcond_q_w", "L0_xcond_q_b")),
    dict(proj=("L0_xcond_ca_proj_w", "L0_xcond_ca_proj_b", None), ln=(1e-6, ("L0", 8), ("L0", 6)),
         mlp=("L0_xcond_fc1_w", "L0_xcond_fc1_b", "gelu", "L0_xcond_fc2_w", "L0_xcond_fc2_b", ("L0", 10)),
         ln2=(1e-6, ("L1", 2), ("L1", 0)), out=("qkv", "L1_xcond_w_qkv", "L1_xcond_b_qkv")),
    dict(proj=("L1_xcond_w_so", "L1_xcond_b_so", ("L1", 4)), ln=(1e-6, ("L1", 8), ("L1", 6)), mlp=None, ln2=None,
         out=("q", "L1_xcond_w_q", "L1_xcond_b_q")),
    dict(proj=("L1_xcond_w_co", "L1_xcond_b_co", ("L1", 10)), ln=(1e-6, ("L1", 14), ("L1", 12)),
         mlp=("L1_xcond_w_m1", "L1_xcond_b_m1", "swiglu", "L1_xcond_w_m2", "L1_xcond_b_m2", ("L1", 16)),
         ln2=(1e-5, ("L2q", 0), ("L2q", 2)), out=("q", "L2_xcond_Wq", "L2_xcond_bq")),
    dict(proj=("L2_xcond_Wp", "L2_xcond_bp", None), ln=(1e-6, ("L3", 2), ("L3", 0)), mlp=None, ln2=None,
         out=("qkv", "L3_xcond_W_qkv", "L3_xcond_b_qkv")),
    dict(proj=("L3_xcond_W_proj", "L3_xcond_b_proj", ("L3", 4)), ln=(1e-6, None, None), mlp=None, ln2=None,
         out=("q", "L3_xcond_W_qc", "L3_xcond_b_qc")),
    dict(proj=("L3_xcond_W_cproj", "L3_xcond_b_cproj", None), ln=(1e-6, ("L3", 8), ("L3", 6)),
         mlp=("L3_xcond_W_mlp1", "L3_xcond_b_mlp1", "gelu_tanh", "L3_xcond_W_mlp2", "L3_xcond_b_mlp2", ("L3", 10)),
         ln2=None, out=None),
]
ATTENTION = [("self", None, 0), ("cross", 0, 1), ("window", None, 2), ("topk", 1, 3), ("cross", 2, 4),
             ("self", None, 5), ("cross", 3, 6)]
HALVES = 16
MAX_TILES = {"self": 32, "cross": 8, "window": 4}
EXP_STEPS = {"self": 16, "cross": 3, "window": 2}
LEAD = {"self": (8, 8), "cross": (4, 4), "window": (2, 2)}
PE_RAW = {"self": 3, "cross": 2, "window": 1}
PE_NORM = {"self": 6, "cross": 2, "window": 1}
PE_TURN_MAX = {"self": 12, "cross": 2, "window": 1}
ACT_RAW = {"self": 2, "cross": 0, "window": 0}
ACT_FINAL = {"self": 7, "cross": 2, "window": 1}
ACT_ROWS = {"self": 12, "cross": 2, "window": 1}
PV_LAG = 1


def half_after(i, q, n=1):
    return (i + (q + n) // 4, (q + n) % 4) if q + n >= 4 else (i, q + n)


def half_before(i, q):
    return (i, q - 1) if q else (i - 1, 3)


def max_tiles_by_step(kind, q, last):
    tiles = []
    if kind != "self":
        steps = EXP_STEPS[kind] - 1
        near = [] if last and q == 3 else [(1, k) for k in range(LEAD[kind][(q + 1) % 2], MAX_TILES[kind])]
        far = [] if last and q >= 2 else [(2, k) for k in range(LEAD[kind][q % 2])]
        return [near[len(near) * e // steps:len(near) * (e + 1) // steps] for e in range(steps)] + [far]
    if not (last and q == 3):
        tiles += [(1, k) for k in range(LEAD[kind][(q + 1) % 2], MAX_TILES[kind])]
    if not (last and q >= 2):
        tiles += [(2, k) for k in range(LEAD[kind][q % 2])]
    full = MAX_TILES[kind] - LEAD[kind][(q + 1) % 2] + LEAD[kind][q % 2]
    steps = EXP_STEPS[kind]
    return [tiles[full * e // steps:full * (e + 1) // steps] for e in range(steps)]


def head_last(w):
    return w.rearrange("p (g j d) -> p g d j", j=HG, d=HD)


class TokenOrder:

    def __init__(self, stages):
        n = dict(lin=0, pair=0, lnt=0, y=0, xt=0, h=0, split=0, ab=0, ln=0, res=0, store=0)
        self.stages = []
        self.xt_last_product = []
        self.h_last_product = []
        for st in stages:
            phases = []
            if st["proj"]:
                phases += [("proj", *st["proj"]), ("residual", st["ln"])]
            else:
                phases += [("norm", st["ln"])]
            phases.append(("spread", st["ln"]))
            if st["mlp"]:
                up_w, up_b, kind, dn_w, dn_b, gate = st["mlp"]
                phases += [("up", up_w, up_b, kind), ("down", dn_w, dn_b, gate), ("residual", st["ln2"])]
                if st["ln2"]:
                    phases.append(("spread", st["ln2"]))
            if st["out"]:
                phases.append(st["out"])
            items = []
            xt = [None] * CH
            hb = [None] * CH
            yb = [None] * CH
            for t in range(len(phases) + CH - 1):
                for c in range(CH):
                    if not 0 <= t - c < len(phases):
                        continue
                    ph = phases[t - c]
                    it = dict(kind=ph[0], spec=ph, c=c, first=(t - c, c))
                    if ph[0] in ("proj", "down"):
                        it["lin"] = n["lin"]
                        n["lin"] += KT
                        it["y"] = yb[c] = n["y"]
                        n["y"] += 1
                        if ph[0] == "down":
                            it["h"] = hb[c]
                            self.h_last_product.append(n["lin"])
                    if ph[0] in ("residual", "norm"):
                        if ph[0] == "residual":
                            it["pair"] = n["pair"]
                            n["pair"] += 1
                            it["y"] = yb[c]
                            it["res"] = n["res"]
                            n["res"] += 1
                        if ph[1]:
                            it["ln"] = n["ln"]
                            n["ln"] += 1
                        else:
                            it["store"] = n["store"]
                            n["store"] += 1
                    if ph[0] == "spread":
                        it["lnt"] = n["lnt"]
                        n["lnt"] += 1
                        it["xt"] = xt[c] = n["xt"]
                        n["xt"] += 1
                    if ph[0] == "up":
                        it["lin"] = n["lin"]
                        n["lin"] += FT * (2 if ph[3] == "swiglu" else 1)
                        it["xt"] = xt[c]
                        self.xt_last_product.append(("lin", n["lin"]))
                        it["h"] = hb[c] = n["h"]
                        n["h"] += 1
                        if ph[3] == "swiglu":
                            it["ab"] = n["ab"]
                            n["ab"] += FT
                    if ph[0] in ("qkv", "q"):
                        it["lin"] = n["lin"]
                        it["split"] = n["split"]
                        tiles = KT * (2 if ph[0] == "qkv" else 1)
                        n["lin"] += tiles
                        n["split"] += tiles
                        it["xt"] = xt[c]
                        if ph[0] == "qkv":
                            it["pair"] = n["pair"]
                            n["pair"] += 1
                            it["v"] = n["pair"]
                            self.xt_last_product.append(("pair", n["pair"]))
                        else:
                            self.xt_last_product.append(("lin", n["lin"]))
                    items.append(it)
            self.stages.append(items)
        self.n = n


def build_program(nc, ins, out, stages):
    order = TokenOrder(TOKEN_STAGES[:stages])
    ctx = ExitStack()
    with ctx:
        def sb(name, shape, dt=F32):
            return ctx.enter_context(nc.sbuf_tensor(name, shape, dt))

        def sem(name):
            return ctx.enter_context(nc.semaphore(name))

        def sems(name, n):
            return [sem(f"{name}{i}") for i in range(n)]

        q_parts = nc.dram_tensor("q_parts", (2 * B, 2, PARTS, P, CW), BF16, kind="Internal").ap()
        k_parts = nc.dram_tensor("k_parts", (2 * B, PARTS, P, N), BF16, kind="Internal").ap()
        kc_parts = nc.dram_tensor("kc_parts", (len(KV) * 2 * B, PARTS, P, SP), BF16, kind="Internal").ap()

        x = sb("x", [P, TOK // P, D])
        v_all = sb("v_all", [P, 2 * B, N // P, P])
        o_t = sb("o_t", [P, 2 * B, N])
        ident = sb("ident", [P, P])
        ident_bf = sb("ident_bf", [P, P], BF16)
        bias_cols = sb("bias_cols", [P, 2 * P])
        bias_cols_hl = sb("bias_cols_hl", [P, 2 * P])
        mod = sb("mod", [P, MT, B])
        v_bias = sb("v_bias", [P, len(V_BIAS), 2 * B, 2])
        v_ctx = sb("v_ctx", [P, len(KV), B, D])
        v_ctx_rest = sb("v_ctx_rest", [P, len(KV), B, D])
        reorder = sb("reorder", [P, 2 * D])
        v_topk_rest = sb("v_topk_rest", [32, B, D])
        mask_row = sb("mask_row", [1, B, SP], BF16)
        minus_half = sb("minus_half", [P, 4])

        WBYTES = (28 * 1024, 24 * 1024)
        weights = [sb(f"weights{i}", [P, WBYTES[i] // 4]) for i in range(2)]
        WORK = 80 * 1024
        work = sb("work", [P, WORK // 4])

        class Carve:
            def __init__(self):
                self.at = 0

            def take(self, words, dt=F32):
                ap = work[:, self.at:self.at + words]
                self.at += words
                assert self.at * 4 <= WORK, self.at * 4
                return ap if dt is F32 else ap.bitcast(dt)

        cw = Carve()
        ada_w = cw.take(KT * MT * P).rearrange("p (k n) -> p k n", k=KT)
        bias_rows = cw.take(2 * P).rearrange("p (r n) -> p r n", r=2)
        bias_rows_hl = cw.take(2 * P).rearrange("p (r n) -> p r n", r=2)
        cond_t = cw.take(KT * B).rearrange("p (k b) -> p k b", k=KT)
        cond_silu = cw.take(KT * 32).rearrange("p (k r b) -> p k r b", k=KT, b=B)
        ctx_tok = cw.take(2 * B * D).rearrange("p (t d) -> p t d", t=2 * B)
        ctx_norm = weights[0][:, 4096:4096 + 2 * 2 * B * D].rearrange("p (e t d) -> p e t d", e=2, t=2 * B)
        mod_rest = MT - 48
        mod_raw = weights[0][:, 2048:4096].rearrange("p (r n) -> p r n", r=4)
        ctx_t = cw.take(3 * KT * B * SP).rearrange("p (e k s) -> p e k s", e=3, k=KT)
        ctx_stats = cw.take(6 * 2 * B).rearrange("p (t s) -> p t s", s=6)
        ctx_mv = cw.take(2 * 2 * B).rearrange("p (t s) -> p t s", s=2)
        ctx_eps = cw.take(2 * 2 * B).rearrange("p (e t) -> p e t", e=2)
        ctx_rstd = cw.take(2 * 2 * B).rearrange("p (e t) -> p e t", e=2)
        kc32 = [cw.take(B * SP) for _ in range(2)]
        kc_rest = [cw.take(B * SP) for _ in range(2)]
        kc_split = [cw.take(PARTS * B * SP // 2, BF16).rearrange("p (a s) -> p a s", a=PARTS) for _ in range(4)]
        v_rest = weights[1][0:32, 4096:4096 + len(KV) * B * D].rearrange("p (l b d) -> p l b d", l=len(KV), b=B)
        mask_u8 = cw.take(B * SP, U8)[0:1, 0:B * SP].rearrange("p (b s) -> p b s", b=B)
        mask_f = cw.take(B * SP)[0:1, :].rearrange("p (b s) -> p b s", b=B)

        ct = Carve()
        h = [ct.take(FT * CW).rearrange("p (m t) -> p m t", m=FT) for _ in range(2)]
        xt = [ct.take(KT * CW).rearrange("p (k t) -> p k t", k=KT) for _ in range(2)]
        xn = [ct.take(4 * D).rearrange("p (t d) -> p t d", t=4) for _ in range(2)]
        y = [ct.take(KT * CW).rearrange("p (k t) -> p k t", k=KT) for _ in range(2)]
        gate_half = [ct.take(CW) for _ in range(2)]
        x32 = [ct.take(CW) for _ in range(2)]
        xrest = [ct.take(CW) for _ in range(2)]
        split = [ct.take(PARTS * CW // 2, BF16).rearrange("p (a t) -> p a t", a=PARTS) for _ in range(3)]
        stats = [ct.take(4 * 6).rearrange("p (t s) -> p t s", s=6) for _ in range(2)]
        mv = [ct.take(4 * 2).rearrange("p (t s) -> p t s", s=2) for _ in range(2)]
        var_eps = [ct.take(4) for _ in range(2)]
        rstd = [ct.take(4) for _ in range(2)]

        ca = Carve()
        q_stack = [ca.take(HG * N // 2, BF16).rearrange("p (a j t) -> p a j t", a=2, j=HG) for _ in range(2)]
        k_stack = [ca.take(HG * N // 2, BF16).rearrange("p (j t) -> p j t", j=HG) for _ in range(2)]
        v_ones = [ca.take(N // P * HG * 2 * HD).rearrange("p (t j e) -> p t j e", t=N // P, j=HG) for _ in range(2)]
        v_ones_rest = [ca.take(HG * 2 * HD).rearrange("p (j e) -> p j e", j=HG) for _ in range(2)]
        NPR = 4
        probs = [ca.take(2 * CW) for _ in range(NPR)]
        o_raw = ca.take(CW)
        o_norm = ca.take(4 * HG * HD).rearrange("p (t d) -> p t d", t=4)
        o_rsum = ca.take(4 * HG)
        row_max = ca.take(HG * 4 * 2)
        neg_max = ca.take(HG * 4)
        max_parts = ca.take(HG * 4, BF16)
        max_rows = ca.take(P // 2, BF16)[0:2 * HG * 4, :]
        top1 = [ca.take(2 * 8).rearrange("p (a e) -> p a e", a=2) for _ in range(2)]
        top2 = [ca.take(2 * 8).rearrange("p (a e) -> p a e", a=2) for _ in range(2)]
        neg_top = [ca.take(2) for _ in range(2)]

        ps = ctx.enter_context(nc.psum_tensor("ps", [P, 8, 512], F32))
        LIN = (0, 1, 2, 3)
        PS_SPREAD, PS_PAIR = 4, 6
        PS_EXP, PS_MAX, PS_OUT, PS_MISC = 0, 4, 6, 7

        stage_end = {e: sem(f"{e}_stage_end") for e in ("pe", "act", "dve", "pool", "sp")}
        bias_loaded, ada_loaded, cond_loaded, ctx_loaded, mask_loaded, x_loaded = (
            sem(n) for n in ("bias_loaded", "ada_loaded", "cond_loaded", "ctx_loaded", "mask_loaded", "x_loaded"))
        w_loaded, kv_loaded = sem("w_loaded"), sem("kv_loaded")
        kc_stored = sems("kc_stored", 4)
        act_link, dve_link, pool_link = sem("act_link"), sem("dve_link"), sem("pool_link")
        pre_pe, pre_act, pre_dve, pre_pool, pre_dma = (sem(f"pre_{n}") for n in ("pe", "act", "dve", "pool", "dma"))
        lin_full = sem("lin_full")
        lin_free = sems("lin_free", len(LIN))
        pair_full, pair_free = sem("pair_full"), sem("pair_free")
        spread_full = sem("spread_full")
        y_ready, xn_ready, xt_ready, h_ready, h_done = (sem(n) for n in ("y_ready", "xn_ready", "xt_ready", "h_ready", "h_done"))
        a_ready, var_ready, rstd_ready = sem("a_ready"), sem("var_ready"), sem("rstd_ready")
        hi_ready, mid_ready, lo_ready = sem("hi_ready"), sem("mid_ready"), sem("lo_ready")
        parts_stored = sems("parts_stored", 3)
        x_final, out_stored = sem("x_final"), sem("out_stored")
        mod_rows_full, mod_rows_ready = sem("mod_rows_full"), sem("mod_rows_ready")
        reordered, bias_reordered, kv_reordered = sem("reordered"), sem("bias_reordered"), sem("kv_reordered")
        q_loaded = sems("q_loaded", 4)
        k_loaded = sems("k_loaded", 2)
        v_ready = sem("v_ready")
        init_done, q_ones_ready = sem("init_done"), sem("q_ones_ready")
        max_full, max_done, max_parts_ready = sem("max_full"), sem("max_done"), sem("max_parts_ready")
        rows_full, rows_ready, rows_loaded = sem("rows_full"), sem("rows_ready"), sem("rows_loaded")
        exp_full, exp_done, pv_done = sem("exp_full"), sem("exp_done"), sem("pv_done")
        raw_ready, raw_t_full, norm_ready, norm_t_full, o_ready = (
            sem(n) for n in ("raw_ready", "raw_t_full", "norm_ready", "norm_t_full", "o_ready"))
        rsum_ready = sem("rsum_ready")
        top_ready, weight_ready, prob_ready, turn_full, turned = (
            sem(n) for n in ("top_ready", "weight_ready", "prob_ready", "turn_full", "turned"))
        turned_rest, all_exp_ready = sem("turned_rest"), sem("all_exp_ready")
        neg_top_ready = sem("neg_top_ready")
        masked_ready = sem("masked_ready")
        topk_link, topk_hold = sem("topk_link"), sem("topk_hold")

        NSTAGE = 1 + stages + min(stages, len(ATTENTION))
        ENGINES = ("pe", "act", "dve", "pool", "sp")

        def leave_stage(eng, name):
            eng.drain().then_inc(stage_end[name], 1)

        def enter_stage(eng, name, number):
            for other in ENGINES:
                if other != name:
                    eng.wait_ge(stage_end[other], number)

        def stage_sequence():
            number = 1
            for s in range(stages):
                yield "token", s, number
                number += 1
                if s + 1 < stages:
                    yield "attention", s, number
                    number += 1

        def weight_list(s):
            st = TOKEN_STAGES[s]
            names = []
            if st["proj"]:
                names.append(st["proj"][0])
            if st["mlp"]:
                names += [st["mlp"][0], st["mlp"][3]]
            if st["out"]:
                names.append(st["out"][1])
            return names

        weight_at, weight_count = {}, [0]
        for s in range(stages):
            at, buf = 0, weights[s % 2]
            for name in weight_list(s):
                rows, cols = ins[name].shape
                words = rows // P * cols
                weight_at[name] = buf[:, at:at + words].rearrange("p (k n) -> p k n", k=rows // P)
                at += words
            assert at * 4 <= WBYTES[s % 2], (s, at * 4)
            weight_count.append(weight_count[-1] + len(weight_list(s)))

        def load_weights(sp, s):
            for name in weight_list(s):
                sp.dma_start(weight_at[name], ins[name].rearrange("(k p) n -> p k n", p=P)).then_inc(w_loaded, 16)

        def x_rows(dram, b):
            half = P - SHIFT
            yield dram[b, SHIFT:SHIFT + (N // P - 1) * P, :].rearrange("(t p) d -> p t d", p=P), slice(0, P), slice(0, N // P - 1)
            yield dram[b, N - half:N, :], slice(0, half), slice(N // P - 1, N // P)
            yield dram[b, 0:SHIFT, :], slice(half, P), slice(N // P - 1, N // P)

        def mod_col(which, k, b):
            layer, tile = which
            return mod[:, MOD0[layer] + tile + k, b:b + 1]

        def bias_col(name, tile):
            c = bias_column(name, tile)
            return bias_cols[:, c:c + 1]

        def bias_col_head_last(name, tile):
            c = bias_column(name, tile)
            return bias_cols_hl[:, c:c + 1]


        def sp_token(sp, s):
            for it in order.stages[s]:
                c = it["c"]
                if it["kind"] in ("q", "qkv"):
                    tiles = KT * (2 if it["kind"] == "qkv" else 1)
                    for m in range(tiles):
                        n = it["split"] + m
                        turn = c // 2 * 2 + m % KT
                        if m < KT:
                            dst = q_parts[turn, c % 2, :, :, :]
                        else:
                            dst = k_parts[turn, :, :, c % 2 * CW:(c % 2 + 1) * CW]
                        sp.wait_ge(lo_ready, n + 1)
                        sp.dma_start(dst.rearrange("a p t -> p a t"), split[n % 3]).then_inc(parts_stored[n % 3], 16)
                if "store" in it:
                    sp.wait_ge(x_final, it["store"] + 1)
                    store_chunk(sp, c)
            for r in range(3):
                uses = sum(1 for n in range(split_uses(s)) if n % 3 == r)
                if uses:
                    sp.wait_ge(parts_stored[r], 16 * uses)
            if s + 1 == len(TOKEN_STAGES):
                sp.wait_ge(out_stored, 16 * stored[0])

        stored = [0]

        def store_chunk(sp, c):
            b, first = c // 2, c % 2 * 4
            if first == 0:
                sp.dma_start(out[b, SHIFT:SHIFT + CW, :].rearrange("(t p) d -> p t d", p=P), x[:, c * 4:c * 4 + 4, :]).then_inc(out_stored, 16)
                stored[0] += 1
            else:
                half = P - SHIFT
                sp.dma_start(out[b, SHIFT + CW:SHIFT + CW + 3 * P, :].rearrange("(t p) d -> p t d", p=P),
                             x[:, c * 4:c * 4 + 3, :]).then_inc(out_stored, 16)
                sp.dma_start(out[b, N - half:N, :], x[0:half, c * 4 + 3, :]).then_inc(out_stored, 16)
                sp.dma_start(out[b, 0:SHIFT, :], x[half:P, c * 4 + 3, :]).then_inc(out_stored, 16)
                stored[0] += 3

        def split_uses(s):
            n = 0
            for st in order.stages[:s + 1]:
                for it in st:
                    if it["kind"] in ("q", "qkv"):
                        n = max(n, it["split"] + KT * (2 if it["kind"] == "qkv" else 1))
            return n

        def before(s, per_kind):
            return sum(per_kind(ATTENTION[a]) for a in range(s))

        def usual(count):
            return lambda a: HALVES * (count[a[0]] if a[0] in count else 0)

        def base(s, what):
            if what == "max":
                return before(s, usual({**MAX_TILES, "topk": 8}))
            if what == "exp":
                return before(s, usual(EXP_STEPS))
            if what == "pv":
                return before(s, usual({**EXP_STEPS, "topk": 4}))
            if what == "half":
                return before(s, usual({k: 1 for k in ("self", "cross", "window", "topk")}))
            if what == "maxrow":
                return before(s, usual({k: 1 for k in ("self", "cross", "window")}))
            if what == "unit":
                return before(s, lambda a: HALVES // 2)
            if what == "load":
                return before(s, lambda a: HALVES // 4 * 16 * loads(a))
            if what == "topk":
                return before(s, usual({"topk": 1}))
            raise KeyError(what)

        def has_mask(a):
            return a[0] == "cross" and a[1] == 0

        def loads(a):
            return len(K_RUNS) + has_mask(a)

        def wait_stacks(pe, s, i, q):
            par = q // 2
            pe.wait_ge(q_loaded[q], 16 * len(Q_RUNS) * (HALVES // 4 * s + i + 1))
            if q % 2 == 0:
                pe.wait_ge(k_loaded[par], base(s, "load") + (i + 1) * 16 * loads(ATTENTION[s]))

        def k_view(kind, par):
            if kind in ("self", "window"):
                return k_stack[par]
            return k_stack[par].rearrange("p j t -> p (j t)")[:, 0:HG * SP].rearrange("p (j s) -> p j s", j=HG)

        def on_halves(eng, body):
            turns = HALVES // 4
            body(0, True, False)
            with eng.Fori(1, turns - 1) as i:
                body(i, False, False)
            body(turns - 1, False, True)

        def sp_attention(sp, s):
            kind, layer, _ = ATTENTION[s]
            lb, rb = base(s, "load"), base(s, "maxrow")
            def stacks_read(i, q):
                if kind == "topk":
                    sp.wait_ge(max_full, base(s, "max") + (i * 4 + q + 1) * 8)
                else:
                    sp.wait_ge(exp_full, base(s, "exp") + (i * 4 + q + 1) * EXP_STEPS[kind])

            def load_queries(i, q, first):
                par, a = q // 2, q % 2
                if not first:
                    stacks_read(i - 1, q)
                for at, part, n in Q_RUNS:
                    src = q_parts[i, a, part:part + 1, par * 64:par * 64 + 64, :].rearrange("x (d j) t -> x d (j t)", j=HG)
                    sp.dma_start(q_stack[par][at * HD:(at + n) * HD, a, :, :], src.to_broadcast([n, HD, HG * CW]))\
                        .then_inc(q_loaded[q], 16)

            def load_keys(i, par, first):
                if not first:
                    stacks_read(i - 1, 2 * par + 1)
                for at, n in K_RUNS:
                    rows = slice(par * 64, par * 64 + 64)
                    src = k_parts[i, 0:n, rows, :] if kind in ("self", "window") else kc_parts[i + layer * 4, 0:n, rows, :]
                    sp.dma_start(k_view(kind, par)[at * HD:(at + n) * HD, :, :], src.rearrange("x (d j) t -> x d (j t)", j=HG))\
                        .then_inc(k_loaded[par], 16)
                if has_mask(ATTENTION[s]):
                    if first:
                        sp.wait_ge(init_done, s + 1)
                    at = slice(i, i + 1) if isinstance(i, int) else bass.ds(i, 1)
                    sp.dma_start(k_view(kind, par)[R_MASK:R_MASK + 1, :, :], mask_by_turn[:, at, :].to_broadcast([1, HG, SP]))\
                        .then_inc(k_loaded[par], 16)

            def max_row(i, q):
                p = i * 4 + q
                par, hq = q // 2, q % 2
                sp.wait_ge(rows_ready, rb + p + 1)
                sp.dma_start(q_stack[par][R_MAX:R_MAX + 2, hq, :, :].rearrange("p j t -> p (j t)"), max_rows[:, :]).then_inc(rows_loaded, 16)

            def body(i, first, last):
                for q in range(4):
                    if q == 0:
                        load_keys(i, 1, first)
                        load_queries(i, 3, first)
                    if q == 1 and not last:
                        load_queries(i + 1, 0, False)
                    if q == 2 and not last:
                        load_keys(i + 1, 0, False)
                        load_queries(i + 1, 1, False)
                    if q == 3 and not last:
                        load_queries(i + 1, 2, False)
                    if kind != "topk" and not (last and q == 3):
                        max_row(*half_after(i, q))

            load_queries(0, 0, True)
            load_keys(0, 0, True)
            load_queries(0, 1, True)
            load_queries(0, 2, True)
            if kind != "topk":
                max_row(0, 0)
            if s + 1 < stages:
                load_weights(sp, s + 1)
            on_halves(sp, body)
            for q in range(4):
                sp.wait_ge(q_loaded[q], 16 * len(Q_RUNS) * HALVES // 4 * (s + 1))
            for par in range(2):
                sp.wait_ge(k_loaded[par], base(s + 1, "load"))
            if kind != "topk":
                sp.wait_ge(rows_loaded, 16 * (rb + HALVES))

        mask_by_turn = sb("mask_by_turn", [1, 2 * B, SP], BF16)

        MIDS0 = KT * len(KV)

        def columns_head_last(pool, w):
            n = w.shape[1]
            tmp = reorder[:, 0:n]
            nc.gpsimd.tensor_copy(tmp.rearrange("p (g d j) -> p g d j", j=HG, d=HD), head_last(w)).then_inc(reordered, 1)
            reorders[0] += 1
            pool.wait_ge(reordered, reorders[0])
            nc.gpsimd.tensor_copy(w, tmp).then_inc(reordered, 1)
            reorders[0] += 1
            pool.wait_ge(reordered, reorders[0])

        reorders = [0]

        def reorder_weights(pool, s):
            st = TOKEN_STAGES[s]
            if st["out"]:
                pool.wait_ge(w_loaded, 16 * weight_count[s + 1])
                w = weight_at[st["out"][1]]
                for k in range(KT):
                    columns_head_last(pool, w[:, k, 0:D * (2 if st["out"][0] == "qkv" else 1)])

        def pool_token(pool, s):
            for it in order.stages[s]:
                if "ln" in it:
                    n = it["ln"]
                    pool.wait_ge(var_ready, n + 1)
                    nc.gpsimd.tensor_tensor(rstd[n % 2], var_eps[n % 2], minus_half[:, :], ALU.pow).then_inc(rstd_ready, 1)
                if it["kind"] in ("q", "qkv"):
                    for m in range(KT * (2 if it["kind"] == "qkv" else 1)):
                        n = it["split"] + m
                        pool.wait_ge(mid_ready, MIDS0 + n + 1)
                        nc.gpsimd.tensor_tensor(split[n % 3][:, 2, :], xrest[n % 2], split[n % 3][:, 1, :], ALU.subtract)\
                            .then_inc(lo_ready, 1)

        def pool_attention(pool, s):
            kind, layer, _ = ATTENTION[s]
            links = [pool_links(s)]

            def link(ins_):
                links[0] += 1
                ins_.then_inc(pool_link, 1)
                pool.wait_ge(pool_link, links[0])

            if kind != "topk":
                for par in range(2):
                    kv = k_view(kind, par).bitcast(F32)
                    link(nc.gpsimd.memset(kv[R_MASK:R_ALL, :, :], ONE_BF16_TWICE))
                    link(nc.gpsimd.memset(kv[R_MASK:R_MASK + 1, :, :], 0.0))
            pool.drain().then_inc(init_done, 1)

            def value_ones(par):
                tiles = N // P if kind in ("self", "window") else 1
                link(nc.gpsimd.memset(v_ones[par][:, 0:tiles, :, HD:2 * HD], 1.0))
                if kind == "cross":
                    link(nc.gpsimd.memset(v_ones_rest[par], 0.0))
                    for j in range(HG):
                        link(nc.gpsimd.memset(v_ones_rest[par][32 * j:32 * j + SR, j, HD:2 * HD], 1.0))
                if kind == "topk":
                    link(nc.gpsimd.memset(v_ones_rest[par], 1.0))

            def copy_values(i, par, first):
                u = i * 2 + par
                if not first:
                    steps = 4 if kind == "topk" else EXP_STEPS[kind]
                    pool.wait_ge(pv_done, base(s, "pv") + (u - 1) * 2 * steps)
                if kind in ("self", "window"):
                    src = v_all[:, bass.ds(i, 1), :, par * 64:par * 64 + 64] if not isinstance(i, int) else v_all[:, i:i + 1, :, par * 64:par * 64 + 64]
                    nc.gpsimd.tensor_copy(v_ones[par][:, :, :, 0:HD], src.rearrange("p a t (j e) -> p (a t) j e", j=HG)).then_inc(v_ready, 1)
                    return
                flat = v_ctx[:, layer, :, :].rearrange("p b (k f) -> p (b k) f", k=KT)
                flat_rest = v_ctx_rest[:, layer, :, :].rearrange("p b (k f) -> p (b k) f", k=KT)
                at = bass.ds(i, 1) if not isinstance(i, int) else slice(i, i + 1)
                src = flat[:, at, par * 64:par * 64 + 64].rearrange("p a (j e) -> p (a j) e", j=HG)
                nc.gpsimd.tensor_copy(v_ones[par][:, 0, :, 0:HD], src).then_inc(v_ready, 1)
                pool.wait_ge(v_ready, v_base(s) + u * v_copies(kind) + 1)
                if kind == "cross":
                    src = flat_rest[:, at, par * 64:par * 64 + 64].rearrange("p a (j e) -> p (a j) e", j=HG)
                    nc.gpsimd.tensor_copy(v_ones_rest[par][:, :, 0:HD], src).then_inc(v_ready, 1)
                else:
                    plain = v_topk_rest[:, :, :].rearrange("p b (k f) -> p (b k) f", k=KT)
                    src = plain[:, at, par * 64:par * 64 + 64].rearrange("p a (j e) -> p (a j) e", j=HG)
                    nc.gpsimd.tensor_copy(v_ones_rest[par][0:32, :, 0:HD], src).then_inc(v_ready, 1)

            def subtract(i, q, k):
                n = (i * 4 + q) * 8 + k
                a = k % 2
                if not (isinstance(n, int) and n < 2):
                    pool.wait_ge(turn_full, base(s, "topk") * 8 + n - 1)
                pool.wait_ge(weight_ready, base(s, "topk") * 8 + n + 1)
                nc.gpsimd.tensor_tensor(tk_prob(a), tk_exp(a), tk_rest_exp(a), ALU.subtract).then_inc(prob_ready, 1)

            def body(i, first, last):
                for q in range(4):
                    for k in range(3 if kind == "topk" else 0):
                        subtract(i, q, k)
                    if q == 0:
                        copy_values(i, 1, first)
                    if q == 2 and not last:
                        copy_values(i + 1, 0, False)
                    for k in range(3, 8 if kind == "topk" else 0):
                        subtract(i, q, k)

            value_ones(0)
            copy_values(0, 0, True)
            value_ones(1)
            assert links[0] == pool_links(s + 1)
            on_halves(pool, body)
            if s + 1 < stages:
                reorder_weights(pool, s + 1)

        def pool_links(s):
            return 4 + sum(2 * {"cross": 4 + HG, "topk": 2}.get(ATTENTION[a][0], 3) for a in range(s))

        def v_copies(kind):
            return {"self": 1, "window": 1, "cross": 2, "topk": 2}[kind]

        def v_base(s):
            return before(s, lambda a: HALVES // 2 * v_copies(a[0]))

        def tk(a, n):
            at = probs[a][:, :]
            return at[:, n * 2 * S:(n + 1) * 2 * S].rearrange("p (h s) -> p h s", h=2)

        def tk_left(a):
            return tk(a, 0)

        def tk_exp(a):
            return tk(a, 1)

        def tk_prob(a):
            return tk(a, 2)

        tk_rest_store = [v_ones[a][:, 1:8, :, :].rearrange("p t j e -> p (t j e)") for a in range(2)]

        def tk_rest_exp(a):
            return tk_rest_store[a][:, 0:2 * S].rearrange("p (h s) -> p h s", h=2)

        def turned_main(a):
            return probs[2 + a][:, 0:512].rearrange("p (j t) -> p j t", j=HG)

        def turned_last(a):
            return probs[2 + a][0:SR, 512:1024].rearrange("p (j t) -> p j t", j=HG)

        bias_rows_total = sum(n for _, n in BIASES)
        bias_dmas = len(BIASES) + sum(1 for n, t in BIASES if bias_column(n) < P < bias_column(n) + t)

        def lin_wait(pe, n):
            if n >= len(LIN):
                pe.wait_ge(lin_free[n % len(LIN)], n // len(LIN))

        def pe_token(pe, s):
            st = TOKEN_STAGES[s]
            pe.wait_ge(w_loaded, 16 * weight_count[s + 1])
            for it in order.stages[s]:
                c, kind = it["c"], it["kind"]
                if kind in ("proj", "down"):
                    w = weight_at[it["spec"][1]]
                    if kind == "down":
                        pe.wait_ge(h_ready, FT * (it["h"] + 1))
                    for m in range(KT):
                        n = it["lin"] + m
                        lin_wait(pe, n)
                        ks = KT if kind == "proj" else FT
                        for k in range(ks):
                            if kind == "proj":
                                src = o_t[:, c // 2 * 2 + k, c % 2 * CW:(c % 2 + 1) * CW]
                            else:
                                src = h[it["h"] % 2][:, k, :]
                            last = nc.tensor.matmul(ps[:, n % 4, :], w[:, k, m * P:(m + 1) * P], src,
                                                    start=(k == 0), stop=(k == ks - 1))
                        last.then_inc(lin_full, 1)
                if kind == "residual":
                    pe.wait_ge(y_ready, KT * (it["y"] + 1))
                    if it["pair"]:
                        pe.wait_ge(pair_free, it["pair"])
                    for t in range(4):
                        for k in range(KT):
                            last = nc.tensor.transpose(ps[:, PS_PAIR + t // 2, (t % 2 * KT + k) * P:(t % 2 * KT + k + 1) * P],
                                                       y[it["y"] % 2][:, k, t * P:(t + 1) * P], ident[:, :])
                    last.then_inc(pair_full, 1)
                if kind == "spread":
                    n = it["lnt"]
                    pe.wait_ge(xn_ready, n + 1)
                    if n:
                        pe.wait_ge(xt_ready, KT * n)
                    for k in range(KT):
                        for t in range(4):
                            last = nc.tensor.transpose(ps[:, PS_SPREAD + k, t * P:(t + 1) * P],
                                                       xn[n % 2][:, t, k * P:(k + 1) * P], ident[:, :])
                    last.then_inc(spread_full, 1)
                if kind in ("up", "q", "qkv"):
                    w = weight_at[it["spec"][1]]
                    tiles = {"q": KT, "qkv": 2 * KT}.get(kind) or (FT * (2 if it["spec"][3] == "swiglu" else 1))
                    swiglu = kind == "up" and it["spec"][3] == "swiglu"
                    pe.wait_ge(xt_ready, KT * (it["xt"] + 1))
                    for m in range(tiles):
                        n = it["lin"] + m
                        lin_wait(pe, n)
                        mm = m // 2 + m % 2 * FT if swiglu else m
                        for k in range(KT):
                            last = nc.tensor.matmul(ps[:, n % 4, :], w[:, k, mm * P:(mm + 1) * P], xt[it["xt"] % 2][:, k, :],
                                                    start=(k == 0), stop=(k == KT - 1))
                        last.then_inc(lin_full, 1)
                    if kind == "qkv":
                        if it["pair"]:
                            pe.wait_ge(pair_free, it["pair"])
                        for t in range(4):
                            for k in range(KT):
                                last = nc.tensor.matmul(ps[:, PS_PAIR + t // 2, t % 2 * D:(t % 2 + 1) * D],
                                                        xt[it["xt"] % 2][:, k, t * P:(t + 1) * P], w[:, k, 2 * D:3 * D],
                                                        start=(k == 0), stop=(k == KT - 1))
                        last.then_inc(pair_full, 1)

        def pe_attention(pe, s):
            kind, layer, _ = ATTENTION[s]
            if kind == "topk":
                return pe_topk(pe, s)
            M, E = MAX_TILES[kind], EXP_STEPS[kind]
            mb, eb, pb, hb, rb, ub = (base(s, n) for n in ("max", "exp", "pv", "half", "maxrow", "unit"))
            out_bank = ps[:, PS_OUT, :]
            misc = ps[:, PS_MISC, :]
            misc_bf = misc.bitcast(BF16)

            def wait_last_rows():
                pe.wait_ge(init_done, s + 1)
                pe.wait_ge(q_ones_ready, 2 * before(s + 1, lambda a: a[0] != "topk"))

            def max_tile(i, q, k):
                p = i * 4 + q
                par = q // 2
                if k == 0:
                    wait_stacks(pe, s, i, q)
                n = p * M + k
                pe_wait_reuse(pe, max_done, mb, n, 2, i, q, k)
                dst = ps[:, PS_MAX + k % 2, :]
                if kind == "self":
                    t, j, kh = k // (2 * HG), k // 2 % HG, k % 2
                    qs = q_stack[par][0:R_MASK, q % 2, j, t * P:(t + 1) * P]
                    last = nc.tensor.matmul(dst, qs, k_view(kind, par)[0:R_MASK, j, kh * CW:(kh + 1) * CW], start=True, stop=True)
                elif kind == "cross":
                    t, jp = k // 2, k % 2
                    for a in range(2):
                        j = jp * 2 + a
                        qs = q_stack[par][0:R_MAX, q % 2, j, t * P:(t + 1) * P]
                        last = nc.tensor.matmul(dst[:, a * S:(a + 1) * S], qs, k_view(kind, par)[0:R_MAX, j, 0:S], start=True, stop=True)
                else:
                    at = q % 2 * CW + k * P
                    for j in range(HG):
                        last = nc.tensor.matmul(dst[:, j * P:(j + 1) * P], q_stack[par][0:R_MASK, q % 2, j, k * P:(k + 1) * P],
                                                k_view(kind, par)[0:R_MASK, j, at:at + P], start=True, stop=True)
                last.then_inc(max_full, 1)

            def turn_max(i, q):
                p = i * 4 + q
                pe.wait_ge(max_parts_ready, rb + p + 1)
                if kind == "self":
                    if not (isinstance(i, int) and i == 0 and q < 2):
                        pe.wait_ge(o_ready, hb + p - 1)
                elif not (isinstance(i, int) and i == 0 and q < 3):
                    pe.wait_ge(o_ready, hb + p - 2)
                nc.tensor.transpose(misc_bf[0:32, 0:P], max_parts[:, 0:32], ident_bf[:, :]).then_inc(rows_full, 1)

            def exp_step(i, q, e):
                p = i * 4 + q
                par = q // 2
                n = p * E + e
                slot = (q * E + e) % 2
                if e == 0:
                    pe.wait_ge(rows_loaded, 16 * (rb + p + 1))
                pe_wait_reuse(pe, exp_done, eb, n, 2, i, q, e, E)
                for a in range(2):
                    dst = ps[:, PS_EXP + slot * 2 + a, :]
                    if kind == "self":
                        kt, j = e // 2, e % 2 * 2 + a
                        last = nc.tensor.matmul(dst, k_view(kind, par)[0:R_ALL, j, kt * P:(kt + 1) * P],
                                                q_stack[par][0:R_ALL, q % 2, j, :], start=True, stop=True)
                    elif kind == "window":
                        at = q % 2 * CW + (e * 2 + a) * P
                        for j in range(HG):
                            last = nc.tensor.matmul(dst[:, j * P:(j + 1) * P], k_view(kind, par)[0:R_ALL, j, at:at + P],
                                                    q_stack[par][0:R_ALL, q % 2, j, at - q % 2 * CW:at - q % 2 * CW + P], start=True, stop=True)
                    elif e < 2:
                        j = e * 2 + a
                        last = nc.tensor.matmul(dst, k_view(kind, par)[0:R_ALL, j, 0:P],
                                                q_stack[par][0:R_ALL, q % 2, j, :], start=True, stop=True)
                    elif a == 0:
                        for j in range(HG):
                            last = nc.tensor.matmul(dst[32 * j:32 * j + 32, :], k_view(kind, par)[0:R_ALL, j, P:SP],
                                                    q_stack[par][0:R_ALL, q % 2, j, :], start=True, stop=True)
                last.then_inc(exp_full, 1)

            def pv_wait(i, q, e):
                p = i * 4 + q
                pe.wait_ge(exp_done, eb + p * E + e + 1)

            def pv_first(i, q):
                p = i * 4 + q
                if not (isinstance(i, int) and i == 0 and q == 0):
                    pe.wait_ge(raw_ready, hb + p)
                if q % 2 == 0:
                    pe.wait_ge(v_ready, v_base(s) + (i * 2 + q // 2 + 1) * v_copies(kind))

            def pv_step(i, q, e):
                par = q // 2
                if kind == "self":
                    kt, late = (e // 2, 0) if e % 2 else (e // 2 - 1, 1)
                    if not late:
                        pv_wait(i, q, e)
                    cols = slice(late * CW // 2, (late + 1) * CW // 2)
                    if kt == 0:
                        if not late:
                            return
                        pv_first(i, q)
                        cols = slice(0, CW)
                    for j in range(HG):
                        pr = probs[(q * E + 2 * kt + j // 2) % NPR]
                        last = nc.tensor.matmul(out_bank[32 * j:32 * j + 32, cols], v_ones[par][:, kt, j, :],
                                                pr[:, j % 2 * CW + cols.start:j % 2 * CW + cols.stop], start=(kt == 0), stop=(late == 1 and kt == N // P - 1))
                    if late:
                        last.then_inc(pv_done, 2)
                elif kind == "window":
                    pv_wait(i, q, e)
                    if e == 0:
                        pv_first(i, q)
                    pr = probs[(q * E + e) % NPR]
                    for a in range(2):
                        w = e * 2 + a
                        for j in range(HG):
                            last = nc.tensor.matmul(out_bank[32 * j:32 * j + 32, w * P:(w + 1) * P],
                                                    v_ones[par][:, q % 2 * 4 + w, j, :], pr[:, a * CW + j * P:a * CW + (j + 1) * P],
                                                    start=True, stop=True)
                    last.then_inc(pv_done, 1)
                else:
                    if e == 0:
                        return
                    pv_wait(i, q, e)
                    if e == 1:
                        pv_first(i, q)
                    for j in range(HG):
                        if e == 1:
                            pr = probs[(q * E + j // 2) % NPR][:, j % 2 * CW:(j % 2 + 1) * CW]
                            w = v_ones[par][:, 0, j, :]
                        else:
                            pr = probs[(q * E + 2) % NPR][:, 0:CW]
                            w = v_ones_rest[par][:, j, :]
                        last = nc.tensor.matmul(out_bank[32 * j:32 * j + 32, :], w, pr, start=(e == 1), stop=(e == 2))
                    last.then_inc(pv_done, 2 if e == 1 else 1)

            def values_due(i, q, first, e):
                if kind == "self":
                    at = e - 2
                    if at >= 1:
                        pv_step(i, q, at)
                    elif not (first and q == 0):
                        pv_step(*half_before(i, q), E + at)
                elif e >= PV_LAG:
                    pv_step(i, q, e - PV_LAG)
                elif not (first and q == 0):
                    pv_step(*half_before(i, q), E + e - PV_LAG)

            def half(i, q, first, last):
                for e, tiles in enumerate(max_tiles_by_step(kind, q, last)):
                    at = [(*half_after(i, q, ahead), k) for ahead, k in tiles]
                    if kind == "self":
                        exp_step(i, q, e)
                        for tile in at[:1]:
                            max_tile(*tile)
                        values_due(i, q, first, e)
                        for tile in at[1:]:
                            max_tile(*tile)
                    elif e == 0:
                        values_due(i, q, first, e)
                        for tile in at:
                            max_tile(*tile)
                        exp_step(i, q, e)
                    else:
                        exp_step(i, q, e)
                        if e == PE_TURN_MAX[kind] and not (last and q == 3):
                            turn_max(*half_after(i, q))
                        for tile in at[:2]:
                            max_tile(*tile)
                        if e == PE_RAW[kind] and not (first and q == 0):
                            turn_raw(pe, s, *half_before(i, q), 2 if last and q == 3 else 3)
                        for tile in at[2:]:
                            max_tile(*tile)
                        values_due(i, q, first, e)
                        if e == PE_NORM[kind] and not (first and q == 0):
                            turn_norm(pe, s, *half_before(i, q))
                    if kind == "self":
                        if not (first and q == 0):
                            if e == PE_RAW[kind]:
                                turn_raw(pe, s, *half_before(i, q), 2)
                            if e == PE_NORM[kind]:
                                turn_norm(pe, s, *half_before(i, q))
                        if e == PE_TURN_MAX[kind] and not (last and q == 3):
                            turn_max(*half_after(i, q))

            def body(i, first, last):
                for q in range(4):
                    half(i, q, first, last)

            if kind == "cross":
                wait_last_rows()
            for k in range(M):
                max_tile(0, 0, k)
            turn_max(0, 0)
            for k in range(LEAD[kind][1]):
                max_tile(0, 1, k)
            if kind != "cross":
                wait_last_rows()
            on_halves(pe, body)
            for e in ((E - 2, E - 1, E) if kind == "self" else (E - 1,)):
                pv_step(HALVES // 4 - 1, 3, e)
            turn_raw(pe, s, HALVES // 4 - 1, 3, 0)
            turn_norm(pe, s, HALVES // 4 - 1, 3)

        def pe_wait_reuse(pe, done, base_count, n, ring, i, q, k, per=None):
            if isinstance(n, int) and n < ring:
                return
            pe.wait_ge(done, base_count + n - ring + 1)

        def turn_raw(pe, s, i, q, rows):
            hb, rb = base(s, "half"), base(s, "maxrow")
            p = i * 4 + q
            pe.wait_ge(raw_ready, hb + p + 1)
            if rows:
                pe.wait_ge(rows_ready, rb + p + rows)
            if not (isinstance(p, int) and p == 0):
                pe.wait_ge(o_ready, hb + p)
            for t in range(4):
                last_i = nc.tensor.transpose(ps[:, PS_MISC, t * P:(t + 1) * P], o_raw[:, t * P:(t + 1) * P], ident[:, :])
            last_i.then_inc(raw_t_full, 1)

        def turn_norm(pe, s, i, q):
            hb = base(s, "half")
            p = i * 4 + q
            pe.wait_ge(norm_ready, hb + p + 1)
            for a in range(2):
                last_i = nc.tensor.transpose(ps[:, PS_MISC, a * P:(a + 1) * P], o_norm[:, 2 * a:2 * a + 2, :], ident[:, :])
            last_i.then_inc(norm_t_full, 1)

        def pe_topk(pe, s):
            mb, hb, tb, pb = base(s, "max"), base(s, "half"), base(s, "topk"), base(s, "pv")

            def scores(i, q, k):
                p = i * 4 + q
                par = q // 2
                n = p * 8 + k
                if k == 0:
                    wait_stacks(pe, s, i, q)
                if not (isinstance(n, int) and n < 2):
                    pe.wait_ge(max_done, mb + n - 1)
                    pe.wait_ge(all_exp_ready, tb * 8 + n - 1)
                t, jp = k // 2, k % 2
                for a in range(2):
                    j = jp * 2 + a
                    qs = q_stack[par][0:R_MASK, q % 2, j, t * P:(t + 1) * P]
                    last = nc.tensor.matmul(ps[:, PS_MAX + k % 2, a * S:(a + 1) * S], qs, k_view("topk", par)[0:R_MASK, j, 0:S],
                                            start=True, stop=True)
                last.then_inc(max_full, 1)

            def turn(i, q, k):
                p = i * 4 + q
                n = p * 8 + k
                t, jp = k // 2, k % 2
                pe.wait_ge(prob_ready, tb * 8 + n + 1)
                if jp == 0:
                    m = p * 4 + t
                    if not (isinstance(m, int) and m < 2):
                        pe.wait_ge(turned, tb * 4 + m - 1)
                        pe.wait_ge(turned_rest, tb * 4 + m - 1)
                for a in range(2):
                    j = jp * 2 + a
                    pr = tk_prob(k % 2)[:, a, :]
                    nc.tensor.transpose(ps[:, PS_EXP + t % 2, j * P:(j + 1) * P], pr[:, 0:P], ident[:, :])
                    last = nc.tensor.transpose(ps[0:SR, PS_EXP + 2 + t % 2, j * P:(j + 1) * P], pr[:, P:S], ident[:, :])
                last.then_inc(turn_full, 1)

            def pv(i, q, t):
                p = i * 4 + q
                par = q // 2
                m = p * 4 + t
                pe.wait_ge(turned, tb * 4 + m + 1)
                pe.wait_ge(turned_rest, tb * 4 + m + 1)
                if t == 0:
                    if not (isinstance(i, int) and i == 0 and q == 0):
                        pe.wait_ge(raw_ready, hb + p)
                    if q % 2 == 0:
                        pe.wait_ge(v_ready, v_base(s) + (i * 2 + q // 2 + 1) * v_copies("topk"))
                for j in range(HG):
                    dst = ps[32 * j:32 * j + 32, PS_OUT, t * P:(t + 1) * P]
                    nc.tensor.matmul(dst, v_ones[par][:, 0, j, :], turned_main(t % 2)[:, j, :], start=True, stop=False)
                    last = nc.tensor.matmul(dst, v_ones_rest[par][0:SR, j, :], turned_last(t % 2)[:, j, :], start=False, stop=True)
                last.then_inc(pv_done, 1)

            def body(i, first, last):
                for q in range(4):
                    for k in range(8):
                        if k + 2 < 8:
                            scores(i, q, k + 2)
                        elif not (last and q == 3):
                            scores(*half_after(i, q), k + 2 - 8)
                        before = half_before(i, q)
                        started = not (first and q == 0)
                        if k:
                            turn(i, q, k - 1)
                        elif started:
                            turn(*before, 7)
                        if k == 4 and started:
                            turn_raw(pe, s, *before, 0)
                        if k % 2 == 0 and k >= 4:
                            pv(i, q, k // 2 - 2)
                        elif k % 2 == 0 and started:
                            pv(*before, k // 2 + 2)
                        if k == 6 and started:
                            turn_norm(pe, s, *before)

            scores(0, 0, 0)
            scores(0, 0, 1)
            on_halves(pe, body)
            turn(HALVES // 4 - 1, 3, 7)
            pv(HALVES // 4 - 1, 3, 2)
            pv(HALVES // 4 - 1, 3, 3)
            turn_raw(pe, s, HALVES // 4 - 1, 3, 0)
            turn_norm(pe, s, HALVES // 4 - 1, 3)

        def act_token(act, s):
            for it in order.stages[s]:
                c, kind = it["c"], it["kind"]
                b = c // 2
                if kind == "spread":
                    n = it["xt"]
                    act.wait_ge(spread_full, it["lnt"] + 1)
                    if n >= 2:
                        what, count = order.xt_last_product[n - 2]
                        act.wait_ge(lin_full if what == "lin" else pair_full, count)
                    _, scale, shift = it["spec"][1]
                    for k in range(KT):
                        src = ps[:, PS_SPREAD + k, :]
                        if scale:
                            nc.scalar.activation(xt[n % 2][:, k, :], src, ACT.Identity, bias=mod_col(shift, k, b),
                                                 scale=mod_col(scale, k, b)).then_inc(xt_ready, 1)
                        else:
                            nc.scalar.activation(xt[n % 2][:, k, :], src, ACT.Copy).then_inc(xt_ready, 1)
                if kind == "up":
                    _, _, bname, how = it["spec"]
                    hn = it["h"]
                    if hn >= 2 and how != "swiglu":
                        act.wait_ge(lin_full, order.h_last_product[hn - 2])
                    for m in range(FT):
                        if how == "swiglu":
                            n = it["lin"] + 2 * m
                            ab = it["ab"] + m
                            act.wait_ge(lin_full, n + 1)
                            if ab >= 2:
                                act.wait_ge(h_done, ab - 1)
                            nc.scalar.activation(gate_half[ab % 2], ps[:, n % 4, :], ACT.Silu, bias=bias_col(bname, m))\
                                .then_inc(lin_free[n % 4], 1)
                        else:
                            n = it["lin"] + m
                            act.wait_ge(lin_full, n + 1)
                            func = ACT.Gelu if how == "gelu" else ACT.Gelu_apprx_tanh
                            last = nc.scalar.activation(h[hn % 2][:, m, :], ps[:, n % 4, :], func, bias=bias_col(bname, m))
                            last.then_inc(lin_free[n % 4], 1)
                    if how != "swiglu":
                        act.drain().then_inc(h_ready, FT)
                if kind in ("q", "qkv"):
                    bname = it["spec"][2]
                    for m in range(KT * (2 if kind == "qkv" else 1)):
                        n, sn = it["lin"] + m, it["split"] + m
                        act.wait_ge(lin_full, n + 1)
                        if sn >= 2:
                            act.wait_ge(mid_ready, MIDS0 + sn - 1)
                        if sn >= 3:
                            act.wait_ge(parts_stored[sn % 3], 16 * (sn // 3))
                        nc.scalar.activation(x32[sn % 2], ps[:, n % 4, :], ACT.Identity, bias=bias_col_head_last(bname, m)).then_inc(hi_ready, 1)
                        nc.scalar.activation(split[sn % 3][:, 0, :], ps[:, n % 4, :], ACT.Identity, bias=bias_col_head_last(bname, m))\
                            .then_inc(lin_free[n % 4], 1)
                    if kind == "qkv":
                        act.wait_ge(pair_full, it["v"])
                        for k in range(KT):
                            src = ps[:, PS_PAIR:PS_PAIR + 2, :].rearrange("p a (t d) -> p (a t) d", t=2)[:, :, k * P:(k + 1) * P]
                            last = nc.scalar.activation(v_all[:, b * 2 + k, c % 2 * 4:c % 2 * 4 + 4, :], src, ACT.Copy)
                        last.then_inc(pair_free, 1)

        def act_o_copies(act, s):
            hb = base(s, "half")
            pv_per = {**EXP_STEPS, "topk": 4}[ATTENTION[s][0]]
            vb = ATTENTION[s][2]

            def raw(i, q):
                p = i * 4 + q
                act.wait_ge(pv_done, base(s, "pv") + (p + 1) * pv_per)
                if not (isinstance(p, int) and p == 0):
                    act.wait_ge(raw_t_full, hb + p)
                nc.scalar.activation(o_raw, ps[:, PS_OUT, :], ACT.Copy).then_inc(raw_ready, 1)

            def final(i, q):
                p = i * 4 + q
                par = q // 2
                act.wait_ge(norm_t_full, hb + p + 1)
                dyn = not isinstance(i, int)
                at = bass.ds(i, 1) if dyn else slice(i, i + 1)
                for r in range(2):
                    rows = slice(64 * r, 64 * r + 64)
                    bias = v_bias[rows, vb, at, par:par + 1].rearrange("p a c -> p (a c)")
                    dst = o_t[par * 64:par * 64 + 64, at, q % 2 * CW:(q % 2 + 1) * CW]
                    dst = dst.rearrange("p x (a r t) -> p (x a) r t", a=2, r=2)[:, :, r, :]
                    src = ps[rows, PS_MISC, 0:2 * P].rearrange("p (a t) -> p a t", a=2)
                    last = nc.scalar.activation(dst, src, ACT.Identity, bias=bias)
                last.then_inc(o_ready, 1)

            return raw, final

        def act_attention(act, s):
            kind = ATTENTION[s][0]
            raw, final = act_o_copies(act, s)
            if kind == "topk":
                return act_topk(act, s, raw, final)
            E = EXP_STEPS[kind]
            eb, pb, rb = base(s, "exp"), base(s, "pv"), base(s, "maxrow")

            def rows(i, q):
                p = i * 4 + q
                act.wait_ge(rows_full, rb + p + 1)
                act.wait_ge(rows_loaded, 16 * (rb + p))
                nc.scalar.activation(max_rows[:, :], ps[:, PS_MISC, :].bitcast(BF16)[0:32, 0:P], ACT.Copy).then_inc(rows_ready, 1)

            def exp_step(i, q, e):
                n = (i * 4 + q) * E + e
                slot, ring = (q * E + e) % 2, (q * E + e) % NPR
                act.wait_ge(exp_full, eb + n + 1)
                if not (isinstance(n, int) and n < NPR):
                    act.wait_ge(pv_done, pb + n - NPR + 1)
                if kind == "cross" and e == 2:
                    dst, src = probs[ring][:, 0:CW], ps[:, PS_EXP + slot * 2, :]
                else:
                    dst = probs[ring].rearrange("p (a t) -> p a t", a=2)
                    src = ps[:, PS_EXP + slot * 2:PS_EXP + slot * 2 + 2, :]
                nc.scalar.activation(dst, src, ACT.Exp, scale=SCALE).then_inc(exp_done, 1)

            def body(i, first, last):
                for q in range(4):
                    for e in range(E):
                        if e == ACT_RAW[kind] and not (first and q == 0):
                            raw(*half_before(i, q))
                        exp_step(i, q, e)
                        if e == ACT_ROWS[kind] and not (last and q == 3):
                            rows(*half_after(i, q))
                        if e == ACT_FINAL[kind] and not (first and q == 0):
                            final(*half_before(i, q))

            rows(0, 0)
            on_halves(act, body)
            raw(HALVES // 4 - 1, 3)
            final(HALVES // 4 - 1, 3)

        def act_topk(act, s, raw, final):
            tb = base(s, "topk")

            def all_exponentials(i, q, k):
                n = (i * 4 + q) * 8 + k
                a = k % 2
                act.wait_ge(neg_top_ready, tb * 8 + n + 1)
                if not (isinstance(n, int) and n < 2):
                    act.wait_ge(prob_ready, tb * 8 + n - 1)
                act.wait_ge(max_done, base(s, "max") + n + 1)
                for b in range(2):
                    last = nc.scalar.activation(tk_exp(a)[:, b, :], ps[:, PS_MAX + a, b * S:(b + 1) * S], ACT.Exp,
                                                bias=neg_top[a][:, b:b + 1], scale=SCALE)
                last.then_inc(all_exp_ready, 1)

            def rest_exponentials(i, q, k):
                n = (i * 4 + q) * 8 + k
                a = k % 2
                act.wait_ge(top_ready, tb * 16 + 2 * n + 2)
                for b in range(2):
                    last = nc.scalar.activation(tk_rest_exp(a)[:, b, :], tk_left(a)[:, b, :], ACT.Exp,
                                                bias=neg_top[a][:, b:b + 1], scale=SCALE)
                last.then_inc(weight_ready, 1)

            def turned_copy(i, q, t):
                p = i * 4 + q
                m = p * 4 + t
                act.wait_ge(turn_full, tb * 8 + 2 * (m + 1))
                if not (isinstance(m, int) and m < 2):
                    act.wait_ge(pv_done, base(s, "pv") + m - 1)
                nc.scalar.activation(turned_main(t % 2), ps[:, PS_EXP + t % 2, :].rearrange("p (j t) -> p j t", j=HG), ACT.Copy)\
                    .then_inc(turned, 1)

            def rest_copy(i, q, t):
                m = (i * 4 + q) * 4 + t
                act.wait_ge(turn_full, tb * 8 + 2 * (m + 1))
                if not (isinstance(m, int) and m < 2):
                    act.wait_ge(pv_done, base(s, "pv") + m - 1)
                nc.scalar.activation(turned_last(t % 2), ps[0:SR, PS_EXP + 2 + t % 2, :].rearrange("p (j t) -> p j t", j=HG), ACT.Copy)\
                    .then_inc(turned_rest, 1)

            def body(i, first, last):
                for q in range(4):
                    for k in range(8):
                        before = half_before(i, q)
                        started = not (first and q == 0)
                        if k % 2 == 0 and k >= 4:
                            rest_copy(i, q, k // 2 - 2)
                        elif k % 2 == 0 and started:
                            rest_copy(*before, k // 2 + 2)
                        if k:
                            rest_exponentials(i, q, k - 1)
                        elif started:
                            rest_exponentials(*before, 7)
                        all_exponentials(i, q, k)
                        if k % 2 == 1 and k >= 3:
                            turned_copy(i, q, k // 2 - 1)
                        if k == 1 and started:
                            turned_copy(*before, 3)
                        if k == 3 and started:
                            raw(*before)
                        if k == 7 and started:
                            final(*before)

            on_halves(act, body)
            last_half = (HALVES // 4 - 1, 3)
            rest_exponentials(*last_half, 7)
            rest_copy(*last_half, 2)
            turned_copy(*last_half, 3)
            rest_copy(*last_half, 3)
            raw(*last_half)
            final(*last_half)

        def dve_token(dve, s, link):
            if s == 0:
                dve.wait_ge(x_loaded, 16 * 3 * B)
            for it in order.stages[s]:
                c, kind = it["c"], it["kind"]
                b = c // 2
                if kind in ("proj", "down"):
                    _, _, bname, gate = it["spec"]
                    yn = it["y"]
                    if yn >= 2:
                        dve.wait_ge(pair_full, y_turned[yn - 2])
                    for m in range(KT):
                        n = it["lin"] + m
                        dve.wait_ge(lin_full, n + 1)
                        if gate:
                            ins_ = nc.vector.tensor_scalar(y[yn % 2][:, m, :], ps[:, n % 4, :], bias_col(bname, m),
                                                           mod_col(gate, m, b), ALU.add, ALU.mult)
                        else:
                            ins_ = nc.vector.tensor_scalar(y[yn % 2][:, m, :], ps[:, n % 4, :], bias_col(bname, m), None, ALU.add)
                        ins_.then_inc(lin_free[n % 4], 1)
                    dve.drain().then_inc(y_ready, KT)
                if kind == "up" and it["spec"][3] == "swiglu":
                    bname = it["spec"][2]
                    hn = it["h"]
                    if hn >= 2:
                        dve.wait_ge(lin_full, order.h_last_product[hn - 2])
                    for m in range(FT):
                        n, ab = it["lin"] + 2 * m + 1, it["ab"] + m
                        dve.wait_ge(lin_full, n + 1)
                        dve.wait_ge(lin_free[(n - 1) % 4], (n - 1) // 4 + 1)
                        ins_ = nc.vector.scalar_tensor_tensor(out=h[hn % 2][:, m, :], in0=ps[:, n % 4, :], scalar=bias_col(bname, FT + m),
                                                              in1=gate_half[ab % 2], op0=ALU.add, op1=ALU.mult)
                        ins_.then_inc(lin_free[n % 4], 1)
                        dve.wait_ge(lin_free[n % 4], n // 4 + 1)
                        dve.sem_inc(h_done, 1)
                    dve.drain().then_inc(h_ready, FT)
                if kind in ("residual", "norm"):
                    rows = x[:, c * 4:c * 4 + 4, :]
                    if kind == "residual":
                        dve.wait_ge(pair_full, it["pair"] + 1)
                        ins_ = nc.vector.tensor_tensor(rows, rows, ps[:, PS_PAIR:PS_PAIR + 2, :].rearrange("p a (t d) -> p (a t) d", t=2), ALU.add)
                        ins_.then_inc(pair_free, 1)
                        dve.wait_ge(pair_free, it["pair"] + 1)
                    if "store" in it:
                        dve.drain().then_inc(x_final, 1)
                    else:
                        n = it["ln"]
                        eps = it["spec"][1][0]
                        for t in range(4):
                            last = nc.vector.bn_stats(stats[n % 2][:, t, :], rows[:, t, :])
                        link(last)
                        for t in range(4):
                            last = nc.vector.bn_aggr(mv[n % 2][:, t, :], stats[n % 2][:, t, :])
                        link(last)
                        nc.vector.tensor_scalar_add(var_eps[n % 2], mv[n % 2][:, :, 1], eps).then_inc(var_ready, 1)
                        dve.wait_ge(rstd_ready, n + 1)
                        if n >= 2:
                            dve.wait_ge(spread_full, n - 1)
                        for t in range(4):
                            last = nc.vector.tensor_scalar(xn[n % 2][:, t, :], rows[:, t, :], mv[n % 2][:, t, 0:1], rstd[n % 2][:, t:t + 1],
                                                           ALU.subtract, ALU.mult)
                        last.then_inc(xn_ready, 1)
                if kind in ("q", "qkv"):
                    for m in range(KT * (2 if kind == "qkv" else 1)):
                        n, sn = it["lin"] + m, it["split"] + m
                        dve.wait_ge(lin_free[n % 4], n // 4 + 1)
                        if sn >= 2:
                            dve.wait_ge(lo_ready, sn - 1)
                        link(nc.vector.tensor_tensor(xrest[sn % 2], x32[sn % 2], split[sn % 3][:, 0, :], ALU.subtract))
                        nc.vector.tensor_copy(split[sn % 3][:, 1, :], xrest[sn % 2]).then_inc(mid_ready, 1)

        y_turned = {}
        for st_items in order.stages:
            for it in st_items:
                if it["kind"] == "residual":
                    y_turned[it["y"]] = it["pair"] + 1

        def dve_normalise(dve, s):
            hb = base(s, "half")

            def normalise(i, q):
                p = i * 4 + q
                dve.wait_ge(raw_t_full, hb + p + 1)
                if not (isinstance(p, int) and p == 0):
                    dve.wait_ge(norm_t_full, hb + p)
                both = ps[:, PS_MISC, :].rearrange("p (c e) -> p c e", e=2 * HD)
                nc.vector.reciprocal(o_rsum, both[:, :, HD]).then_inc(rsum_ready, 1)
                dve.wait_ge(rsum_ready, hb + p + 1)
                nc.vector.tensor_tensor(o_norm.rearrange("p t (j e) -> p (t j) e", j=HG), both[:, :, 0:HD],
                                        o_rsum.unsqueeze(2).to_broadcast([P, 4 * HG, HD]), ALU.mult).then_inc(norm_ready, 1)

            return normalise

        def dve_attention(dve, s):
            kind = ATTENTION[s][0]
            normalise = dve_normalise(dve, s)
            if kind == "topk":
                return dve_topk(dve, s, normalise)
            M, E = MAX_TILES[kind], EXP_STEPS[kind]
            mb, rb = base(s, "max"), base(s, "maxrow")

            def reduce_tile(i, q, k):
                n = (i * 4 + q) * M + k
                if kind != "self" and k == 0 and not (isinstance(i, int) and i == 0 and q == 0):
                    dve.wait_ge(max_parts_ready, rb + i * 4 + q)
                dve.wait_ge(max_full, mb + n + 1)
                src = ps[:, PS_MAX + k % 2, :]
                if kind == "self":
                    t, j, kh = k // (2 * HG), k // 2 % HG, k % 2
                    dst = row_max.rearrange("p (j t h) -> p j t h", j=HG, t=4)[:, j, t, kh:kh + 1]
                    ins_ = nc.vector.tensor_reduce(dst, src, AX.X, ALU.max)
                elif kind == "cross":
                    t, jp = k // 2, k % 2
                    dst = neg_max.rearrange("p (j t) -> p j t", j=HG)[:, jp * 2:jp * 2 + 2, t]
                    ins_ = nc.vector.tensor_reduce(dst, src[:, 0:2 * S].rearrange("p (a s) -> p a s", a=2), AX.X, ALU.max, negate=True)
                else:
                    dst = neg_max.rearrange("p (j t) -> p j t", j=HG)[:, :, k]
                    ins_ = nc.vector.tensor_reduce(dst, src.rearrange("p (j s) -> p j s", j=HG), AX.X, ALU.max, negate=True)
                ins_.then_inc(max_done, 1)

            def parts(i, q):
                p = i * 4 + q
                ln_ = links_before(s) + p * links_per(kind)
                dve.wait_ge(max_done, mb + (p + 1) * M)
                step = 0
                if kind == "self":
                    nc.vector.tensor_reduce(neg_max, row_max.rearrange("p (c h) -> p c h", h=2), AX.X, ALU.max, negate=True)\
                        .then_inc(masked_ready, 1)
                    step += 1
                    dve.wait_ge(masked_ready, ln_ + step)
                if not (isinstance(p, int) and p == 0):
                    dve.wait_ge(rows_full, rb + p)
                nc.vector.tensor_copy(max_parts[:, 0:16], neg_max).then_inc(masked_ready, 1)
                step += 1
                dve.wait_ge(masked_ready, ln_ + step)
                nc.vector.tensor_tensor(max_parts[:, 16:32], neg_max, max_parts[:, 0:16], ALU.subtract).then_inc(max_parts_ready, 1)

            def body(i, first, last):
                for q in range(4):
                    for e, tiles in enumerate(max_tiles_by_step(kind, q, last)):
                        for n, (ahead, k) in enumerate(tiles):
                            if n == 2 and e == PE_RAW[kind] and kind != "self" and not (first and q == 0):
                                normalise(*half_before(i, q))
                            reduce_tile(*half_after(i, q, ahead), k)
                            if (ahead, k) == (1, M - 1):
                                parts(*half_after(i, q))
                        if e == PE_RAW[kind] and (kind == "self" or len(tiles) <= 2) and not (first and q == 0):
                            normalise(*half_before(i, q))

            for par in range(2):
                row = q_stack[par].rearrange("p a j t -> p (a j t)").bitcast(F32)[R_MASK:R_MASK + 1, :]
                nc.vector.memset(row, ONE_BF16_TWICE).then_inc(q_ones_ready, 1)
            for k in range(M):
                reduce_tile(0, 0, k)
            parts(0, 0)
            for k in range(LEAD[kind][1]):
                reduce_tile(0, 1, k)
            on_halves(dve, body)
            normalise(HALVES // 4 - 1, 3)

        def links_per(kind):
            return {"self": 2, "cross": 1, "window": 1, "topk": 0}[kind]

        def links_before(s):
            return before(s, lambda a: HALVES * links_per(a[0]))

        def dve_topk(dve, s, normalise):
            mb, tb = base(s, "max"), base(s, "topk")

            def strike(i, q, k):
                n = (i * 4 + q) * 8 + k
                a = k % 2
                first_use = isinstance(n, int) and n < 2
                at = tb * 48 + n * 6
                scores = [ps[:, PS_MAX + a, b * S:(b + 1) * S] for b in range(2)]
                left = [tk_left(a)[:, b, :] for b in range(2)]

                def hold(sem_, value):
                    dve.wait_ge(sem_, value)
                    dve.sem_inc(topk_hold, 1)

                if not first_use:
                    hold(weight_ready, tb * 8 + n - 1)
                hold(max_full, mb + n + 1)
                nc.vector.max(top1[a][:, 0, :], scores[0]).then_inc(topk_link, 1)
                nc.vector.max(top1[a][:, 1, :], scores[1]).then_inc(top_ready, 1)
                hold(topk_link, at + 1)
                nc.vector.match_replace(left[0], top1[a][:, 0, :], scores[0], BIG).then_inc(topk_link, 1)
                hold(top_ready, tb * 16 + 2 * n + 1)
                nc.vector.tensor_scalar(neg_top[a], top1[a][:, :, 0], -SCALE, None, ALU.mult).then_inc(neg_top_ready, 1)
                nc.vector.match_replace(left[1], top1[a][:, 1, :], scores[1], BIG).then_inc(max_done, 1)
                hold(topk_link, at + 2)
                nc.vector.max(top2[a][:, 0, :], left[0]).then_inc(topk_link, 1)
                hold(max_done, mb + n + 1)
                nc.vector.max(top2[a][:, 1, :], left[1]).then_inc(topk_link, 1)
                hold(topk_link, at + 3)
                nc.vector.match_replace(left[0], top2[a][:, 0, :], left[0], BIG).then_inc(topk_link, 1)
                hold(topk_link, at + 4)
                nc.vector.match_replace(left[1], top2[a][:, 1, :], left[1], BIG).then_inc(topk_link, 1)
                dve.wait_ge(topk_link, at + 6)
                dve.sem_inc(top_ready, 1)

            def body(i, first, last):
                for q in range(4):
                    before = (i, q - 1) if q else (i - 1, 3)
                    for k in range(8):
                        strike(i, q, k)
                        if k == 5 and not (first and q == 0):
                            normalise(*before)

            on_halves(dve, body)
            normalise(HALVES // 4 - 1, 3)


        block = ctx.enter_context(nc.Block())

        @block.sync
        def _(sp):
            for b in range(B):
                for k in range(KT):
                    sp.dma_start(cond_t[:, k, b:b + 1], ins["cond_1024"][b, k * P:(k + 1) * P].rearrange("(p a) -> p a", a=1))\
                        .then_inc(cond_loaded, 16)
            at = 0
            for name, tiles in ADA:
                sp.dma_start(ada_w[:, :, at:at + tiles * P], ins[name].rearrange("(k p) n -> p k n", p=P)).then_inc(ada_loaded, 16)
                at += tiles * P
            row = 0
            for name, tiles in BIASES:
                src = ins[name].rearrange("(m p) -> m p", p=P)
                done = 0
                while done < tiles:
                    n = min(tiles - done, P - row % P)
                    sp.dma_start(bias_rows[row % P:row % P + n, row // P, :], src[done:done + n, :]).then_inc(bias_loaded, 16)
                    row += n
                    done += n
            for b in range(B):
                sp.dma_start(ctx_tok[:, 2 * b, :], ins["ctx_1024"][b, 0:P, :]).then_inc(ctx_loaded, 16)
                sp.dma_start(ctx_tok[0:SR, 2 * b + 1, :], ins["ctx_1024"][b, P:S, :]).then_inc(ctx_loaded, 16)
                sp.dma_start(ctx_tok[SR:32, 2 * b + 1, :], ins["ctx_1024"][b, S - (SP - S):S, :]).then_inc(ctx_loaded, 16)
                sp.dma_start(mask_u8[:, b, 0:S], ins["mask_BxS2_bf0"][b:b + 1, :]).then_inc(mask_loaded, 16)
                sp.dma_start(mask_u8[:, b, S:SP], ins["mask_BxS2_bf0"][b:b + 1, S - (SP - S):S]).then_inc(mask_loaded, 16)
            for l, (w, _) in enumerate(KV):
                sp.dma_start(weights[1][:, l * KT * 2 * D:(l + 1) * KT * 2 * D].rearrange("p (k n) -> p k n", k=KT),
                             ins[w].rearrange("(k p) n -> p k n", p=P)).then_inc(kv_loaded, 16)
            for b in range(B):
                for src, parts, tiles in x_rows(ins["x"], b):
                    dst = x[parts, b * (N // P) + tiles.start:b * (N // P) + tiles.stop, :]
                    sp.dma_start(dst, src if tiles.stop - tiles.start > 1 else src.unsqueeze(1)).then_inc(x_loaded, 16)
            load_weights(sp, 0)
            for l in range(len(KV)):
                for m in range(KT):
                    n = l * KT + m
                    sp.wait_ge(pre_pool, 3 + n + 1)
                    for b in range(B):
                        sp.dma_start(kc_parts[l * 4 + b * 2 + m, :, :, :].rearrange("a p s -> p a s"),
                                     kc_split[n % 4][:, :, b * SP:(b + 1) * SP]).then_inc(kc_stored[n % 4], 16)
            sp.wait_ge(pre_act, 2 * len(KV) * B)
            for j in range(HG):
                def heads(ap):
                    return ap.rearrange("p l b (g j e) -> p (l b g) j e", g=H // HG, j=HG)[:, :, j, :]
                sp.dma_start(heads(v_ctx_rest[32 * j:32 * j + SR, :, :, :]), heads(v_rest[0:SR, :, :, :])).then_inc(pre_dma, 16)
            sp.dma_start(v_topk_rest[:, :, :], v_rest[:, 1, :, :]).then_inc(pre_dma, 16)
            for r in range(4):
                sp.wait_ge(kc_stored[r], 16 * B * (KT * len(KV) // 4))
            sp.wait_ge(pre_dma, 16 * (HG + 1))
            leave_stage(sp, "sp")

            for kind, s, number in stage_sequence():
                enter_stage(sp, "sp", number)
                if kind == "token":
                    sp_token(sp, s)
                else:
                    sp_attention(sp, s)
                leave_stage(sp, "sp")
            if stages < len(TOKEN_STAGES):
                enter_stage(sp, "sp", number + 1)
                for c in range(CH):
                    store_chunk(sp, c)
                sp.wait_ge(out_stored, 16 * stored[0])

        @block.gpsimd
        def _(pool):
            nc.gpsimd.memset(ident[:, :], 0.0).then_inc(pool_link, 1)
            nc.gpsimd.memset(minus_half[:, :], -0.5).then_inc(pool_link, 1)
            nc.gpsimd.memset(v_ctx_rest[:, :, :, :], 0.0).then_inc(pool_link, 1)
            pool.wait_ge(pool_link, 3)
            nc.gpsimd.affine_select(out=ident[:, :], in_=ident[:, :], compare_op=ALU.not_equal, fill=1.0, base=0,
                                    pattern=[[-1, P]], channel_multiplier=1).then_inc(pool_link, 1)
            pool.wait_ge(pool_link, 4)
            nc.gpsimd.tensor_copy(ident_bf[:, :], ident[:, :]).then_inc(pre_pool, 1)
            pool.wait_ge(pre_dve, 1)
            for e in range(2):
                nc.gpsimd.tensor_tensor(ctx_rstd[:, e, :], ctx_eps[:, e, :], minus_half[:, :], ALU.pow).then_inc(pre_pool, 1)
            pool.wait_ge(kv_loaded, 16 * len(KV))
            for l in range(len(KV)):
                for k in range(KT):
                    at = (l * KT + k) * 2 * D
                    columns_head_last(pool, weights[1][:, at:at + D])
            pool.sem_inc(kv_reordered, 1)
            for n in range(KT * len(KV)):
                pool.wait_ge(mid_ready, n + 1)
                if n >= 4:
                    pool.wait_ge(kc_stored[n % 4], 16 * B * (n // 4))
                nc.gpsimd.tensor_tensor(kc_split[n % 4][:, 2, :], kc_rest[n % 2], kc_split[n % 4][:, 1, :], ALU.subtract)\
                    .then_inc(pre_pool, 1)
            reorder_weights(pool, 0)
            leave_stage(pool, "pool")
            for kind, s, number in stage_sequence():
                enter_stage(pool, "pool", number)
                (pool_token if kind == "token" else pool_attention)(pool, s)
                leave_stage(pool, "pool")

        @block.tensor
        def _(pe):
            pe.wait_ge(pre_pool, 1)
            pe.wait_ge(bias_loaded, 16 * bias_dmas)
            pe.wait_ge(bias_reordered, 2)
            last = None
            for r in range(2):
                rows = P if r == 0 else bias_rows_total - P
                nc.tensor.transpose(ps[:, 0, r * P:r * P + rows], bias_rows[0:rows, r, :], ident[0:rows, 0:rows])
                last = nc.tensor.transpose(ps[:, 0, (2 + r) * P:(2 + r) * P + rows], bias_rows_hl[0:rows, r, :], ident[0:rows, 0:rows])
            last.then_inc(pre_pe, 1)
            pe.wait_ge(ada_loaded, 16 * len(ADA))
            pe.wait_ge(act_link, 1)
            for r in range(4):
                groups, cols = (4, CW) if r < 3 else (1, mod_rest * P)
                for k in range(KT):
                    for g in range(groups):
                        at = (r * 4 + g) * CW
                        last = nc.tensor.matmul(ps[32 * g:32 * g + 32, 1 + r, 0:cols], cond_silu[:, k, :, :].rearrange("p r b -> p (r b)"),
                                                ada_w[:, k, at:at + cols], start=(k == 0), stop=(k == KT - 1))
                last.then_inc(mod_rows_full, 1)
            for r in range(4):
                pe.wait_ge(mod_rows_ready, r + 1)
                for j in range(4 if r < 3 else mod_rest):
                    if r < 3:
                        last = nc.tensor.transpose(ps[:, 5 + r, j * P:(j + 1) * P], mod_raw[:, r, j * P:(j + 1) * P], ident[:, :])
                    else:
                        last = nc.tensor.transpose(ps[:, 1, j * 32:(j + 1) * 32], mod_raw[0:32, 3, j * P:(j + 1) * P], ident[0:32, 0:32])
            last.then_inc(pre_pe, 1)
            pe.wait_ge(pre_dve, 1 + 4 * B + 2)
            for e in range(3):
                if e == 0:
                    pe.wait_ge(ctx_loaded, 16 * 3 * B)
                else:
                    pe.wait_ge(pre_dve, 1 + e * 2 * B)
                for k in range(KT):
                    for t in range(2 * B):
                        n = P if t % 2 == 0 else 32
                        at = t // 2 * SP + t % 2 * P
                        src = ctx_tok[0:n, t, k * P:(k + 1) * P] if e == 0 else ctx_norm[0:n, e - 1, t, k * P:(k + 1) * P]
                        last = nc.tensor.transpose(ps[:, 2 + (e * KT + k) % 6, at:at + n], src, ident[0:n, 0:n])
                    last.then_inc(pre_pe, 1)
            pe.wait_ge(kv_loaded, 16 * len(KV))
            pe.wait_ge(kv_reordered, 1)
            for l in range(len(KV)):
                w = weights[1][:, l * KT * 2 * D:(l + 1) * KT * 2 * D].rearrange("p (k n) -> p k n", k=KT)
                for m in range(KT):
                    n = l * KT + m
                    if n == 0:
                        pe.wait_ge(act_link, 1 + 3 * KT)
                        pe.wait_ge(pre_dve, 1 + 4 * B + 2 + 1)
                    if n >= 2:
                        pe.wait_ge(hi_ready, n - 1)
                    for k in range(KT):
                        last = nc.tensor.matmul(ps[:, n % 2, 0:B * SP], w[:, k, m * P:(m + 1) * P], ctx_t[:, KV_CTX[l], k, :],
                                                start=(k == 0), stop=(k == KT - 1))
                    last.then_inc(pre_pe, 1)
                for b in range(B):
                    for t in range(2):
                        n = (l * B + b) * 2 + t
                        if n >= 2:
                            pe.wait_ge(pre_act, n - 1)
                        rows = P if t == 0 else 32
                        for k in range(KT):
                            last = nc.tensor.matmul(ps[0:rows, 2 + n % 2, 0:D], ctx_t[:, KV_CTX[l], k, b * SP + t * P:b * SP + t * P + rows],
                                                    w[:, k, D:2 * D], start=(k == 0), stop=(k == KT - 1))
                        last.then_inc(pre_pe, 1)
            leave_stage(pe, "pe")
            for kind, s, number in stage_sequence():
                enter_stage(pe, "pe", number)
                (pe_token if kind == "token" else pe_attention)(pe, s)
                leave_stage(pe, "pe")

        @block.scalar
        def _(act):
            act.wait_ge(cond_loaded, 16 * KT * B)
            nc.scalar.activation(cond_silu, cond_t.unsqueeze(2).to_broadcast([P, KT, 32 // B, B]), ACT.Silu).then_inc(act_link, 1)
            for r in range(4):
                act.wait_ge(mod_rows_full, r + 1)
                rows, cols = (P, CW) if r < 3 else (32, mod_rest * P)
                nc.scalar.activation(mod_raw[0:rows, r, 0:cols], ps[0:rows, 1 + r, 0:cols], ACT.Copy).then_inc(mod_rows_ready, 1)
            for e in range(3):
                for k in range(KT):
                    act.wait_ge(pre_pe, 2 + e * KT + k + 1)
                    if e == 1 and k == 0:
                        act.wait_ge(pre_dve, 1 + 4 * B + 2 + 1)
                    src = ps[:, 2 + (e * KT + k) % 6, 0:B * SP]
                    if e == 1:
                        for b in range(B):
                            last = nc.scalar.activation(ctx_t[:, e, k, b * SP:(b + 1) * SP], src[:, b * SP:(b + 1) * SP], ACT.Identity,
                                                        bias=mod_col(("L2kv", 2), k, b), scale=mod_col(("L2kv", 0), k, b))
                        last.then_inc(act_link, 1)
                    else:
                        nc.scalar.activation(ctx_t[:, e, k, :], src, ACT.Copy).then_inc(act_link, 1)
            for l, (_, bname) in enumerate(KV):
                for m in range(KT):
                    n = l * KT + m
                    act.wait_ge(pre_pe, 2 + 3 * KT + l * (KT + 2 * B) + m + 1)
                    if n >= 2:
                        act.wait_ge(mid_ready, n - 1)
                    if n >= 4:
                        act.wait_ge(kc_stored[n % 4], 16 * B * (n // 4))
                    src = ps[:, n % 2, 0:B * SP]
                    nc.scalar.activation(kc32[n % 2], src, ACT.Identity, bias=bias_col_head_last(bname, m))
                    nc.scalar.activation(kc_split[n % 4][:, 0, :], src, ACT.Identity, bias=bias_col_head_last(bname, m)).then_inc(hi_ready, 1)
                for b in range(B):
                    for t in range(2):
                        n = (l * B + b) * 2 + t
                        act.wait_ge(pre_pe, 2 + 3 * KT + l * (KT + 2 * B) + KT + b * 2 + t + 1)
                        if t == 0:
                            nc.scalar.activation(v_ctx[:, l, b, :], ps[:, 2 + n % 2, 0:D], ACT.Copy).then_inc(pre_act, 1)
                        else:
                            nc.scalar.activation(v_rest[:, l, b, :], ps[0:32, 2 + n % 2, 0:D], ACT.Copy).then_inc(pre_act, 1)
            leave_stage(act, "act")
            for kind, s, number in stage_sequence():
                enter_stage(act, "act", number)
                (act_token if kind == "token" else act_attention)(act, s)
                leave_stage(act, "act")

        @block.vector
        def _(dve):
            links = [0]

            def link(ins_):
                links[0] += 1
                ins_.then_inc(dve_link, 1)
                dve.wait_ge(dve_link, links[0])

            dve.wait_ge(bias_loaded, 16 * bias_dmas)
            for r in range(2):
                rows = P if r == 0 else bias_rows_total - P
                dst = bias_rows_hl[0:rows, r, :].rearrange("p (g d j) -> p g d j", j=HG, d=HD)
                nc.vector.tensor_copy(dst, head_last(bias_rows[0:rows, r, :])).then_inc(bias_reordered, 1)
            link(nc.vector.memset(ctx_mv, 1.0))
            dve.wait_ge(ctx_loaded, 16 * 3 * B)
            for t in range(2 * B):
                n = P if t % 2 == 0 else 32
                last = nc.vector.bn_stats(ctx_stats[0:n, t, :], ctx_tok[0:n, t, :])
            link(last)
            for t in range(2 * B):
                n = P if t % 2 == 0 else 32
                last = nc.vector.bn_aggr(ctx_mv[0:n, t, :], ctx_stats[0:n, t, :])
            link(last)
            for e, eps in enumerate((1e-5, 1e-6)):
                last = nc.vector.tensor_scalar_add(ctx_eps[:, e, :], ctx_mv[:, :, 1], eps)
            last.then_inc(pre_dve, 1)
            dve.wait_ge(pre_pool, 3)
            for e in range(2):
                for t in range(2 * B):
                    n = P if t % 2 == 0 else 32
                    nc.vector.tensor_scalar(ctx_norm[0:n, e, t, :], ctx_tok[0:n, t, :], ctx_mv[0:n, t, 0:1], ctx_rstd[0:n, e, t:t + 1],
                                            ALU.subtract, ALU.mult).then_inc(pre_dve, 1)
            dve.wait_ge(pre_pe, 1)
            nc.vector.tensor_copy(bias_cols_hl[:, 0:bias_rows_total], ps[:, 0, 2 * P:2 * P + bias_rows_total])
            link(nc.vector.tensor_copy(bias_cols[:, 0:bias_rows_total], ps[:, 0, 0:bias_rows_total]))
            for n, (name, at) in enumerate(V_BIAS):
                c = bias_column(name, at // P)
                for r in range(2):
                    for g in range(2):
                        nc.vector.tensor_copy(v_bias[64 * r:64 * r + 64, n, :, g].rearrange("p (b k) -> p b k", b=B),
                                              bias_cols[64 * g:64 * g + 64, c:c + KT].unsqueeze(1).to_broadcast([64, B, KT]))
            dve.wait_ge(pre_pe, 2)
            for b in range(B):
                full = MT - mod_rest
                for r in range(3):
                    tiles = slice(16 * r, 16 * r + 16)
                    nc.vector.tensor_tensor(mod[:, tiles, b].rearrange("p (g j) -> p g j", g=4),
                                            ps[:, 5 + r, :].rearrange("p (j g x) -> p g j x", j=4, g=4)[:, :, :, b],
                                            bias_cols[:, tiles].rearrange("p (g j) -> p g j", g=4), ALU.add)
                last = nc.vector.tensor_tensor(mod[:, full:MT, b], ps[:, 1, 0:mod_rest * 32].rearrange("p (j x) -> p j x", x=32)[:, :, b],
                                               bias_cols[:, full:MT], ALU.add)
                last.then_inc(pre_dve, 1)
            dve.wait_ge(pre_dve, 1 + 4 * B + 2)
            for which, tile in SCALE_TILES:
                at = MOD0[which] + tile
                last = nc.vector.tensor_scalar_add(mod[:, at:at + KT, :], mod[:, at:at + KT, :], 1.0)
            last.then_inc(pre_dve, 1)
            dve.wait_ge(mask_loaded, 16 * 2 * B)
            link(nc.vector.tensor_copy(mask_f, mask_u8))
            link(nc.vector.tensor_scalar(mask_f, mask_f, 0.0, None, ALU.not_equal))
            link(nc.vector.tensor_scalar(mask_row[:, :, :], mask_f, BIG, 10.0, ALU.mult, ALU.mult))
            for i in range(2 * B):
                last = nc.vector.tensor_copy(mask_by_turn[:, i, :], mask_row[:, i // 2, :])
            link(last)
            for n in range(KT * len(KV)):
                dve.wait_ge(hi_ready, n + 1)
                if n >= 2:
                    dve.wait_ge(pre_pool, 3 + n - 1)
                link(nc.vector.tensor_tensor(kc_rest[n % 2], kc32[n % 2], kc_split[n % 4][:, 0, :], ALU.subtract))
                nc.vector.tensor_copy(kc_split[n % 4][:, 1, :], kc_rest[n % 2]).then_inc(mid_ready, 1)
            leave_stage(dve, "dve")
            for kind, s, number in stage_sequence():
                enter_stage(dve, "dve", number)
                if kind == "token":
                    dve_token(dve, s, link)
                else:
                    dve_attention(dve, s)
                leave_stage(dve, "dve")


INPUTS = (["x", "cond_1024", "ctx_1024", "mask_BxS2_bf0"] + [n for n, _ in BIASES] + [n for n, _ in ADA] + [w for w, _ in KV]
          + [n for st in TOKEN_STAGES for n in ([st["proj"][0]] if st["proj"] else [])
             + ([st["mlp"][0], st["mlp"][3]] if st["mlp"] else []) + ([st["out"][1]] if st["out"] else [])])


def kernel(**inputs):
    import concourse.bacc as bacc
    from concourse.bass_utils import run_bass_kernel_spmd

    nc = bacc.Bacc("TRN2", target_bir_lowering=False, num_devices=1)
    arrays, ins = {}, {}
    for name in INPUTS:
        a = np.ascontiguousarray(inputs[name])
        arrays["in_" + name] = a
        ins[name] = nc.dram_tensor("in_" + name, a.shape, mybir.dt.from_np(a.dtype), kind="ExternalInput").ap()
    out = nc.dram_tensor("out", (B, N, D), F32, kind="ExternalOutput").ap()
    build_program(nc, ins, out, len(TOKEN_STAGES))
    return run_bass_kernel_spmd(nc, [arrays], core_ids=[0]).results[0]["out"]
```
